# Optimizing a Trainium2 kernel written in Bass

```python
import numpy as np
import jax
import jax.numpy as jnp

def _softmax(x, axis=-1):
    return jax.nn.softmax(x, axis=axis)

def _gelu(x):
    return jax.nn.gelu(x, approximate=True)

def _silu(x):
    return jax.nn.silu(x)

def _sigmoid(x):
    return jax.nn.sigmoid(x)

def _layernorm(x, axis=-1, eps=1e-05):
    m = jnp.mean(x, axis=axis, keepdims=True)
    v = jnp.var(x, axis=axis, keepdims=True)
    return (x - m) / jnp.sqrt(v + eps)

def _scatter_add(tgt, idx, src, axis=0):
    return tgt.at[idx].add(src)

def _segment_sum(src, seg, n):
    return jax.ops.segment_sum(src, seg, n)
kernel_name = 'mk_decoder_postln_d2_seqx_r4_52950f'

def setup_inputs(seed: int=0):
    np.random.seed(seed)
    _w = jnp.asarray

    def _rec_inputs():
        import jax
        import jax.numpy as jnp
        _rk = jax.random.key(seed)
        x = -0.0002928 + 1 * jax.random.normal(jax.random.fold_in(_rk, 1), (32, 256, 256), jnp.float32)
        _lenS = 256 - jax.random.randint(jax.random.fold_in(_rk, 7), (32,), 0, max(1, 256 // 4) + 1, jnp.int32)
        _lenS2 = 120 - jax.random.randint(jax.random.fold_in(_rk, 8), (32,), 0, max(1, 120 // 4) + 1, jnp.int32)
        _ctx_1024P = jax.random.normal(jax.random.fold_in(_rk, 11), (32, 16, 256), jnp.float32)
        _ctx_1024c = jax.random.dirichlet(jax.random.fold_in(_rk, 511), 0.3 * jnp.ones((16,), jnp.float32), (32, 120))
        _ctx_1024t = jnp.einsum('bsk,bkd->bsd', _ctx_1024c, _ctx_1024P)
        _ctx_1024t = _ctx_1024t * jax.lax.rsqrt(jnp.mean(jnp.square(_ctx_1024t)) + 1e-12) * 0.953939
        ctx_1024 = -1.39393e-06 + 0.999914 * (_ctx_1024t + 0.3 * jax.random.normal(jax.random.fold_in(_rk, 611), (32, 120, 256), jnp.float32))
        return (x, ctx_1024)
    x, ctx_1024 = _rec_inputs()

    def _L0_attn_setup():
        import jax, jax.numpy as jnp
        import numpy as np
        import math
        NUM_RFS = 256
        DIM = 256
        OUT_DIM = 256
        B, S = (4, 512)

        def _rfs(xw, ab, AB, gs):
            dot_products = jnp.einsum('...d,rd->...r', xw, ab[:, None] * gs)
            correction = (0.5 * jnp.sum(xw * xw, axis=-1))[..., None] * (ab * ab)
            return 1.0 / math.sqrt(NUM_RFS) * AB * jnp.exp(dot_products - correction)
        key = jax.random.key(seed)
        k1, k2, k3, k4 = jax.random.split(key, 4)
        x = jax.random.normal(k1, (B, S, DIM), dtype=jnp.float32) * 0.03
        input_weights = jax.random.normal(k2, (OUT_DIM, DIM), dtype=jnp.float32) * 0.03
        xis = jax.random.uniform(k3, (NUM_RFS,), dtype=jnp.float32) * 0.5
        proj_matrix = jax.random.normal(k4, (NUM_RFS, DIM), dtype=jnp.float32)
        return {'x': x, 'input_weights': input_weights, 'xis': xis, 'proj_matrix': proj_matrix}
    _L0_attn_all = _L0_attn_setup()
    _L0_attn_in = {k: v for k, v in _L0_attn_all.items() if k in ('input_weights', 'xis', 'proj_matrix')}
    del _L0_attn_all

    def _L0_xattn_setup():
        import jax, jax.numpy as jnp
        import numpy as np
        HEADS = 16
        D_MODEL = 256
        D_K = D_MODEL // HEADS
        key = jax.random.key(seed)
        ks = jax.random.split(key, 11)
        B, S = (2, 512)
        scale = 1.0 / np.sqrt(D_MODEL)
        inp = {'q': jax.random.normal(ks[0], (B, S, D_MODEL), dtype=jnp.float32), 'k': jax.random.normal(ks[1], (B, S, D_MODEL), dtype=jnp.float32), 'v': jax.random.normal(ks[2], (B, S, D_MODEL), dtype=jnp.float32), 'Wq': jax.random.normal(ks[3], (D_MODEL, D_MODEL), dtype=jnp.float32) * scale, 'bq': jnp.zeros((D_MODEL,), dtype=jnp.float32), 'Wk': jax.random.normal(ks[4], (D_MODEL, D_MODEL), dtype=jnp.float32) * scale, 'bk': jnp.zeros((D_MODEL,), dtype=jnp.float32), 'Wv': jax.random.normal(ks[5], (D_MODEL, D_MODEL), dtype=jnp.float32) * scale, 'bv': jnp.zeros((D_MODEL,), dtype=jnp.float32), 'Wo': jax.random.normal(ks[6], (D_MODEL, D_MODEL), dtype=jnp.float32) * scale, 'bo': jnp.zeros((D_MODEL,), dtype=jnp.float32)}
        return inp
    _L0_xattn_all = _L0_xattn_setup()
    _L0_xattn_in = {k: v for k, v in _L0_xattn_all.items() if k in ('Wq', 'bq', 'Wk', 'bk', 'Wv', 'bv', 'Wo', 'bo')}
    del _L0_xattn_all

    def _L0_ffn_setup():
        import jax, jax.numpy as jnp
        import numpy as np
        B, S, DIM = (4, 1024, 256)
        BASE_COUPLING = 0.1
        NUM_CYCLES = 3

        def _gelu(x):
            return jax.nn.gelu(x, approximate=False)

        def _coupling_net(h, w1, b1, w2, b2, w3, b3, w4, b4):
            h = _gelu(h @ w1 + b1)
            h = _gelu(h @ w2 + b2)
            h = _gelu(h @ w3 + b3)
            return jax.nn.sigmoid(h @ w4 + b4)

        def _global_net(h, w1, b1, w2, b2, w3, b3):
            h = _gelu(h @ w1 + b1)
            h = _gelu(h @ w2 + b2)
            return jax.nn.sigmoid(h @ w3 + b3)

        def _twist(x):
            o_r, o_i, p_r, p_i = jnp.split(x, 4, axis=-1)
            return jnp.concatenate([p_r, -p_i, -o_r, o_i], axis=-1)
        key = jax.random.key(seed)
        ks = jax.random.split(key, 9)
        d = DIM

        def w(k, fan_in, fan_out):
            return jax.random.normal(k, (fan_in, fan_out), dtype=jnp.float32) / np.sqrt(fan_in).astype(np.float32)
        inp = {'x': jax.random.normal(ks[0], (B, S, d), dtype=jnp.float32)}
        cn_dims = [(d, d), (d, d // 2), (d // 2, d // 4), (d // 4, 1)]
        for i, (a, b) in enumerate(cn_dims):
            inp[f'cn_w{i + 1}'] = w(ks[1 + i], a, b)
            inp[f'cn_b{i + 1}'] = jnp.zeros((b,), dtype=jnp.float32)
        gc_dims = [(d, d // 2), (d // 2, d // 4), (d // 4, 1)]
        for i, (a, b) in enumerate(gc_dims):
            inp[f'gc_w{i + 1}'] = w(ks[5 + i], a, b)
            inp[f'gc_b{i + 1}'] = jnp.zeros((b,), dtype=jnp.float32)
        inp['adaptive_range'] = jnp.full((1,), 0.2, dtype=jnp.float32)
        return inp
    _L0_ffn_all = _L0_ffn_setup()
    _L0_ffn_in = {k: v for k, v in _L0_ffn_all.items() if k in ('cn_w1', 'cn_b1', 'cn_w2', 'cn_b2', 'cn_w3', 'cn_b3', 'cn_w4', 'cn_b4', 'gc_w1', 'gc_b1', 'gc_w2', 'gc_b2', 'gc_w3', 'gc_b3', 'adaptive_range')}
    del _L0_ffn_all

    def _L1_attn_setup():
        import jax, jax.numpy as jnp
        from jax import lax
        import numpy as np
        INPUT_DIM, STATE_DIM, CONV_K, EXPAND = (256, 16, 4, 2)
        INNER = INPUT_DIM * EXPAND
        BATCH, SEQ = (2, 512)
        key = jax.random.key(seed)
        ks = jax.random.split(key, 6)
        x = jax.random.normal(ks[0], (BATCH, SEQ, INPUT_DIM), jnp.float32)
        W_in = jax.random.normal(ks[1], (2 * INNER, INPUT_DIM), jnp.float32) * 0.02
        conv_w = jax.random.normal(ks[2], (INNER, 1, CONV_K), jnp.float32) * 0.1
        conv_b = jnp.zeros((INNER,), jnp.float32)
        A_log = jax.random.normal(ks[3], (INNER, STATE_DIM), jnp.float32)
        D = jnp.ones((INNER,), jnp.float32)
        W_out = jax.random.normal(ks[4], (INPUT_DIM, INNER), jnp.float32) * 0.02
        return {'x': x, 'W_in': W_in, 'conv_w': conv_w, 'conv_b': conv_b, 'A_log': A_log, 'D': D, 'W_out': W_out}
    _L1_attn_all = _L1_attn_setup()
    _L1_attn_in = {k: v for k, v in _L1_attn_all.items() if k in ('W_in', 'conv_w', 'conv_b', 'A_log', 'D', 'W_out')}
    del _L1_attn_all

    def _L1_xattn_setup():
        import jax, jax.numpy as jnp
        import numpy as np
        E, T, H, F = (16, 512, 256, 1024)
        key = jax.random.key(seed)
        kx, k1, k2, k3 = jax.random.split(key, 4)
        s = 1.0 / np.sqrt(H)
        return {'x': jax.random.normal(kx, (E, T, H), dtype=jnp.float32), 'w1': jax.random.normal(k1, (E, F, H), dtype=jnp.float32) * s, 'v1': jax.random.normal(k2, (E, F, H), dtype=jnp.float32) * s, 'w2': jax.random.normal(k3, (E, F, H), dtype=jnp.float32) * s}
    _L1_xattn_all = _L1_xattn_setup()
    _L1_xattn_in = {k: v for k, v in _L1_xattn_all.items() if k in ()}
    del _L1_xattn_all

    def _L1_ffn_setup():
        import jax, jax.numpy as jnp
        import numpy as np
        B, S, H, E = (4, 512, 256, 8)
        key = jax.random.key(seed)
        k1, k2, k3 = jax.random.split(key, 3)
        scale_w = 1.0 / np.sqrt(H)
        return {'x': jax.random.normal(k1, (B, S, H), dtype=jnp.float32), 'router_w': jax.random.normal(k2, (H, E), dtype=jnp.float32) * scale_w, 'router_b': jnp.zeros((E,), dtype=jnp.float32), 'expert_w': jax.random.normal(k3, (E, H, H), dtype=jnp.float32) * scale_w, 'expert_b': jnp.zeros((E, H), dtype=jnp.float32)}
    _L1_ffn_all = _L1_ffn_setup()
    _L1_ffn_in = {k: v for k, v in _L1_ffn_all.items() if k in ('router_w', 'router_b', 'expert_w', 'expert_b')}
    del _L1_ffn_all
    return {'x': x, 'ctx_1024': ctx_1024, 'L0_attn_input_weights': _L0_attn_in['input_weights'], 'L0_attn_xis': _L0_attn_in['xis'], 'L0_attn_proj_matrix': _L0_attn_in['proj_matrix'], 'L0_xattn_Wq': _L0_xattn_in['Wq'], 'L0_xattn_bq': _L0_xattn_in['bq'], 'L0_xattn_Wk': _L0_xattn_in['Wk'], 'L0_xattn_bk': _L0_xattn_in['bk'], 'L0_xattn_Wv': _L0_xattn_in['Wv'], 'L0_xattn_bv': _L0_xattn_in['bv'], 'L0_xattn_Wo': _L0_xattn_in['Wo'], 'L0_xattn_bo': _L0_xattn_in['bo'], 'L0_ffn_cn_w1': _L0_ffn_in['cn_w1'], 'L0_ffn_cn_b1': _L0_ffn_in['cn_b1'], 'L0_ffn_cn_w2': _L0_ffn_in['cn_w2'], 'L0_ffn_cn_b2': _L0_ffn_in['cn_b2'], 'L0_ffn_cn_w3': _L0_ffn_in['cn_w3'], 'L0_ffn_cn_b3': _L0_ffn_in['cn_b3'], 'L0_ffn_cn_w4': _L0_ffn_in['cn_w4'], 'L0_ffn_cn_b4': _L0_ffn_in['cn_b4'], 'L0_ffn_gc_w1': _L0_ffn_in['gc_w1'], 'L0_ffn_gc_b1': _L0_ffn_in['gc_b1'], 'L0_ffn_gc_w2': _L0_ffn_in['gc_w2'], 'L0_ffn_gc_b2': _L0_ffn_in['gc_b2'], 'L0_ffn_gc_w3': _L0_ffn_in['gc_w3'], 'L0_ffn_gc_b3': _L0_ffn_in['gc_b3'], 'L0_ffn_adaptive_range': _L0_ffn_in['adaptive_range'], 'L1_attn_W_in': _L1_attn_in['W_in'], 'L1_attn_conv_w': _L1_attn_in['conv_w'], 'L1_attn_conv_b': _L1_attn_in['conv_b'], 'L1_attn_A_log': _L1_attn_in['A_log'], 'L1_attn_D': _L1_attn_in['D'], 'L1_attn_W_out': _L1_attn_in['W_out'], 'L1_ffn_router_w': _L1_ffn_in['router_w'], 'L1_ffn_router_b': _L1_ffn_in['router_b'], 'L1_ffn_expert_w': _L1_ffn_in['expert_w'], 'L1_ffn_expert_b': _L1_ffn_in['expert_b']}

def reference(x, ctx_1024, L0_attn_input_weights, L0_attn_xis, L0_attn_proj_matrix, L0_xattn_Wq, L0_xattn_bq, L0_xattn_Wk, L0_xattn_bk, L0_xattn_Wv, L0_xattn_bv, L0_xattn_Wo, L0_xattn_bo, L0_ffn_cn_w1, L0_ffn_cn_b1, L0_ffn_cn_w2, L0_ffn_cn_b2, L0_ffn_cn_w3, L0_ffn_cn_b3, L0_ffn_cn_w4, L0_ffn_cn_b4, L0_ffn_gc_w1, L0_ffn_gc_b1, L0_ffn_gc_w2, L0_ffn_gc_b2, L0_ffn_gc_w3, L0_ffn_gc_b3, L0_ffn_adaptive_range, L1_attn_W_in, L1_attn_conv_w, L1_attn_conv_b, L1_attn_A_log, L1_attn_D, L1_attn_W_out, L1_ffn_router_w, L1_ffn_router_b, L1_ffn_expert_w, L1_ffn_expert_b):
    import jax
    import jax.numpy as jnp

    def _L0_attn_ref(x, input_weights, xis, proj_matrix):
        import jax, jax.numpy as jnp
        import numpy as np
        import math
        NUM_RFS = 256
        DIM = 256
        OUT_DIM = 256
        B, S = (4, 512)

        def _rfs(xw, ab, AB, gs):
            dot_products = jnp.einsum('...d,rd->...r', xw, ab[:, None] * gs)
            correction = (0.5 * jnp.sum(xw * xw, axis=-1))[..., None] * (ab * ab)
            return 1.0 / math.sqrt(NUM_RFS) * AB * jnp.exp(dot_products - correction)
        ab = xis
        AB = jnp.exp(xis)
        weights = _rfs(input_weights, ab, AB, proj_matrix)
        feats = _rfs(x, ab, AB, proj_matrix)
        return jnp.einsum('bsr,or->bso', feats, weights)

    def _L0_xattn_ref(q, k, v, Wq, bq, Wk, bk, Wv, bv, Wo, bo):
        import jax, jax.numpy as jnp
        import numpy as np
        HEADS = 16
        D_MODEL = 256
        D_K = D_MODEL // HEADS
        B, S, _ = q.shape

        def proj(x, W, b):
            y = jnp.einsum('bsd,de->bse', x, W) + b
            return y.reshape(B, -1, HEADS, D_K).transpose(0, 2, 1, 3)
        qh = proj(q, Wq, bq)
        kh = proj(k, Wk, bk)
        vh = proj(v, Wv, bv)
        scores = jnp.einsum('bhqd,bhkd->bhqk', qh, kh) / np.sqrt(D_K)
        weights = jax.nn.softmax(scores, axis=-1)
        context = jnp.einsum('bhqk,bhkd->bhqd', weights, vh)
        context = context.transpose(0, 2, 1, 3).reshape(B, S, HEADS * D_K)
        return jnp.einsum('bsd,de->bse', context, Wo) + bo

    def _L0_ffn_ref(x, cn_w1, cn_b1, cn_w2, cn_b2, cn_w3, cn_b3, cn_w4, cn_b4, gc_w1, gc_b1, gc_w2, gc_b2, gc_w3, gc_b3, adaptive_range):
        import jax, jax.numpy as jnp
        import numpy as np
        B, S, DIM = (4, 1024, 256)
        BASE_COUPLING = 0.1
        NUM_CYCLES = 3

        def _gelu(x):
            return jax.nn.gelu(x, approximate=False)

        def _coupling_net(h, w1, b1, w2, b2, w3, b3, w4, b4):
            h = _gelu(h @ w1 + b1)
            h = _gelu(h @ w2 + b2)
            h = _gelu(h @ w3 + b3)
            return jax.nn.sigmoid(h @ w4 + b4)

        def _global_net(h, w1, b1, w2, b2, w3, b3):
            h = _gelu(h @ w1 + b1)
            h = _gelu(h @ w2 + b2)
            return jax.nn.sigmoid(h @ w3 + b3)

        def _twist(x):
            o_r, o_i, p_r, p_i = jnp.split(x, 4, axis=-1)
            return jnp.concatenate([p_r, -p_i, -o_r, o_i], axis=-1)
        global_context = x.mean(axis=1, keepdims=True)
        gf = _global_net(global_context, gc_w1, gc_b1, gc_w2, gc_b2, gc_w3, gc_b3)
        out = x
        for _ in range(NUM_CYCLES):
            tf = _coupling_net(out, cn_w1, cn_b1, cn_w2, cn_b2, cn_w3, cn_b3, cn_w4, cn_b4)
            combined = 0.7 * gf + 0.3 * tf
            coupling = BASE_COUPLING + adaptive_range * (combined - 0.5) * 2.0
            out = out + coupling * _twist(out)
        return out

    def _L1_attn_ref(x, W_in, conv_w, conv_b, A_log, D, W_out):
        import jax, jax.numpy as jnp
        from jax import lax
        import numpy as np
        INPUT_DIM, STATE_DIM, CONV_K, EXPAND = (256, 16, 4, 2)
        INNER = INPUT_DIM * EXPAND
        BATCH, SEQ = (2, 512)
        b, s, _ = x.shape
        inner = W_in.shape[0] // 2
        K = conv_w.shape[-1]
        state = A_log.shape[1]
        xr = x @ W_in.T
        x_ssm, res = (xr[..., :inner], xr[..., inner:])
        xc = jnp.transpose(x_ssm, (0, 2, 1))
        xc = jnp.pad(xc, ((0, 0), (0, 0), (K - 1, 0)))
        xc = lax.conv_general_dilated(xc, conv_w, (1,), 'VALID', feature_group_count=inner, dimension_numbers=('NCH', 'OIH', 'NCH'))
        x_conv = jax.nn.silu(jnp.transpose(xc, (0, 2, 1)) + conv_b)
        delta = jax.nn.softplus(x_conv)
        A = -jnp.exp(A_log)
        A_d = jnp.exp(delta[..., None] * A)
        Bx = x_conv * x_conv

        def step(h, inp):
            a_t, bx_t, c_t = inp
            h = a_t * h + bx_t[..., None]
            y = c_t * jnp.sum(h, axis=-1)
            return (h, y)
        h0 = jnp.zeros((b, inner, state), x.dtype)
        _, ys = lax.scan(step, h0, (jnp.moveaxis(A_d, 1, 0), jnp.moveaxis(Bx, 1, 0), jnp.moveaxis(x_conv, 1, 0)))
        y_ssm = jnp.moveaxis(ys, 0, 1)
        y = y_ssm * jax.nn.silu(res) + D * x_conv
        return y @ W_out.T

    def _L1_xattn_ref(x, w1, v1, w2):
        import jax, jax.numpy as jnp
        import numpy as np
        E, T, H, F = (16, 512, 256, 1024)
        x1 = jnp.einsum('eth,efh->etf', x, w1)
        x2 = jnp.einsum('eth,efh->etf', x, v1)
        h = jax.nn.gelu(x1, approximate=True) * x2
        return jnp.einsum('etf,efh->eth', h, w2)

    def _L1_ffn_ref(x, router_w, router_b, expert_w, expert_b):
        import jax, jax.numpy as jnp
        import numpy as np
        B, S, H, E = (4, 512, 256, 8)
        b, s, h = x.shape
        xt = x.reshape(b * s, h)
        logits = xt @ router_w + router_b
        probs = jax.nn.softmax(logits, axis=-1)
        gate = jnp.max(probs, axis=-1)
        idx = jnp.argmax(probs, axis=-1)
        out_all = jnp.einsum('th,ehd->ted', xt, expert_w) + expert_b[None, :, :]
        e_out = jnp.take_along_axis(out_all, idx[:, None, None], axis=1)[:, 0, :]
        y = gate[:, None] * e_out
        return y.reshape(b, s, h)
    x = _layernorm(x + _L0_attn_ref(x, L0_attn_input_weights, L0_attn_xis, L0_attn_proj_matrix), axis=-1)
    x = _layernorm(x + _L0_xattn_ref(x, ctx_1024, ctx_1024, L0_xattn_Wq, L0_xattn_bq, L0_xattn_Wk, L0_xattn_bk, L0_xattn_Wv, L0_xattn_bv, L0_xattn_Wo, L0_xattn_bo), axis=-1)
    x = _layernorm(x + _L0_ffn_ref(x, L0_ffn_cn_w1, L0_ffn_cn_b1, L0_ffn_cn_w2, L0_ffn_cn_b2, L0_ffn_cn_w3, L0_ffn_cn_b3, L0_ffn_cn_w4, L0_ffn_cn_b4, L0_ffn_gc_w1, L0_ffn_gc_b1, L0_ffn_gc_w2, L0_ffn_gc_b2, L0_ffn_gc_w3, L0_ffn_gc_b3, L0_ffn_adaptive_range), axis=-1)
    x = _layernorm(x + _L1_attn_ref(x, L1_attn_W_in, L1_attn_conv_w, L1_attn_conv_b, L1_attn_A_log, L1_attn_D, L1_attn_W_out), axis=-1)
    x = _layernorm(x + _L1_xattn_ref(x, ctx_1024, ctx_1024, ctx_1024), axis=-1)
    x = _layernorm(x + _L1_ffn_ref(x, L1_ffn_router_w, L1_ffn_router_b, L1_ffn_expert_w, L1_ffn_expert_b), axis=-1)
    return x

_drawn_inputs = setup_inputs


def setup_inputs(seed=0):
    import zlib

    import numpy as np

    out = dict(_drawn_inputs(seed))
    spreads = {'L0_xattn_bq': (0.0, 0.1),
     'L0_xattn_bk': (0.0, 2.0),
     'L0_xattn_bv': (0.0, 0.1),
     'L0_xattn_bo': (0.0, 0.1),
     'L0_ffn_cn_b1': (0.0, 0.702),
     'L0_ffn_cn_b2': (0.0, 2.0),
     'L0_ffn_cn_b3': (0.0, 0.517),
     'L0_ffn_gc_b1': (0.0, 0.472),
     'L0_ffn_gc_b2': (0.0, 0.487),
     'L1_attn_conv_b': (0.0, 0.1),
     'L1_attn_D': (1.0, 0.6),
     'L1_ffn_router_b': (0.0, 0.1),
     'L1_ffn_expert_b': (0.0, 0.1)}
    factors = {'L0_ffn_cn_w2': 2.798, 'L1_attn_A_log': 8.0}
    for name, (base, spread) in spreads.items():
        noise = np.random.default_rng([zlib.crc32(name.encode()), seed]).standard_normal(out[name].shape)
        drawn = base * np.exp(spread * noise) if base else spread * noise
        out[name] = jnp.asarray(drawn.astype(out[name].dtype))
    for name, factor in factors.items():
        out[name] = (out[name] * factor).astype(out[name].dtype)
    return out
```

```python
from contextlib import ExitStack

import numpy as np

import concourse.bass as bass
from concourse import mybir

F32 = mybir.dt.float32
BF16 = mybir.dt.bfloat16
ALU = mybir.AluOpType
ACT = mybir.ActivationFunctionType
AX = mybir.AxisListType.X

P = 128
B, S, D = 32, 256, 256
KEYS = 120
HEADS, DK = 16, 16
NB = 2
G = B // NB
T = NB * S
NT = T // P
DC = D // P
HC = HEADS // DC
DV = DK + 1
INNER, STATES, TAPS = 512, 16, 4
IC = INNER // P
PAD = TAPS - 1
EXPERTS = 8
RFS = 256
EPS = 1e-5
RING = 4

COLUMNS = {}
for _name, _n in [("xis", DC), ("bq", DC), ("bk", DC), ("cn_b1", 2), ("cn_b2", 1), ("cn_b3", 1), ("cn_b4", 1),
                  ("gc_b1", 1), ("gc_b2", 1), ("gc_b3", 1), ("range", 1), ("sign", 1), ("conv_w", IC * TAPS),
                  ("conv_b", IC), ("D", IC), ("A_log", IC * STATES), ("head_mask", HC)]:
    COLUMNS[_name] = (sum(n for _, n in COLUMNS.values()), _n)
N_COLUMNS = sum(n for _, n in COLUMNS.values())
ROWS = {}
for _name, _n in [("xis", RFS), ("bv", D), ("bo", D), ("router_b", EXPERTS), ("rank", EXPERTS)]:
    ROWS[_name] = (sum(n for _, n in ROWS.values()), _n)
N_ROWS = sum(n for _, n in ROWS.values())

WEIGHTS = {
    "projT": (P, DC * RFS), "rfwT": (P, DC * D),
    "wq": (P, DC * D), "wk": (P, DC * D), "wv": (P, DC * D), "wo": (P, DC * D),
    "cn_w1": (P, DC * 256), "cn_w2": (P, DC * 128), "cn_w3": (P, 64), "cn_w4": (64, P),
    "gc_w1": (P, DC * 128), "gc_w2": (P, 64), "gc_w3": (64, P),
    "winT": (P, DC * 2 * INNER), "woutT": (P, IC * D),
    "router_w": (P, DC * EXPERTS), "expert_w": (P, DC * EXPERTS * D), "expert_b": (EXPERTS, D),
    "columns": (P, N_COLUMNS), "rows": (P, N_ROWS), "ident": (P, P),
}


class Signal:

    def __init__(self, sem, per, head=0):
        self.sem, self.per, self.head = sem, per, head

    def at(self, g, n):
        return g * self.per + n + self.head

    def start_ahead(self, eng):
        eng.sem_inc(self.sem, self.head)


class Chain(Signal):

    def start(self, eng, g):
        self.eng, self.g, self.n = eng, g, 0

    def then(self, ins):
        self.n += 1
        return ins.then_inc(self.sem, 1)

    def settle(self, behind=0):
        self.eng.wait_ge(self.sem, self.at(self.g, self.n - behind))

    def link(self, ins):
        self.then(ins)
        self.settle()

    def end(self):
        assert self.n == self.per, (self.n, self.per)


def program(nc, ins, out):
    with ExitStack() as ctx:
        def sb(name, shape, dt=F32):
            return ctx.enter_context(nc.sbuf_tensor(name, shape, dt))

        def sem(name, per=1, head=0):
            return Signal(ctx.enter_context(nc.semaphore(name)), per, head)

        def chain(name, per):
            return Chain(ctx.enter_context(nc.semaphore(name)), per)

        bank = [ctx.enter_context(nc.psum_tensor(f"bank{i}", [P, 512], F32)) for i in range(8)]

        W = {name: sb("w_" + name, list(shape)) for name, shape in WEIGHTS.items()}

        def col(name, k=0, rows=P):
            at = COLUMNS[name][0] + k
            return W["columns"][0:rows, at:at + 1]

        def row(name):
            at, n = ROWS[name]
            return W["rows"][:, at:at + n]

        def chunks(name, k):
            return W[name][:, :].rearrange("p (k n) -> p k n", k=k)

        projT, rfwT = chunks("projT", DC), chunks("rfwT", DC)
        wq, wk, wv, wo = (chunks(n, DC) for n in ("wq", "wk", "wv", "wo"))
        cn_w1, cn_w2, gc_w1 = (chunks(n, DC) for n in ("cn_w1", "cn_w2", "gc_w1"))
        winT, woutT = chunks("winT", DC), chunks("woutT", IC)
        router_w, expert_w = chunks("router_w", DC), chunks("expert_w", DC)
        ident = W["ident"]

        rf_scaled = projT
        rf_norm = sb("rf_norm", [P, RFS])
        rf_bias = sb("rf_bias", [P, DC])
        rf_out = rfwT
        decay = sb("decay", [P, IC * STATES])
        half_b4 = sb("half_b4", [P, 1])
        half_gb3 = sb("half_gb3", [P, 1])
        gate_scale = sb("gate_scale", [P, 1])
        glob_scale = sb("glob_scale", [P, 1])
        base_sign = sb("base_sign", [P, 1])
        eps = sb("eps", [P, 1])
        head_rows = sb("head_rows16", [2 * HEADS, HEADS, KEYS], BF16)
        ident16 = sb("ident16", [P, P], BF16)

        x0 = sb("x0", [P, NT, D])
        x0T = sb("x0T", [P, DC, T])
        ctxT = sb("ctxT", [P, DC, NB * KEYS])
        sqsum = sb("sqsum", [P, T])
        feats = sb("feats", [P, DC, T])
        sq = feats
        rf_sq, rf_sqsum = feats[:, :, 0:D], sqsum[:, 0:D]
        kT = sb("kT", [P, DC, NB * KEYS])
        kmask = sb("kmask", [P, NB, DC, HC, KEYS])
        vals = sb("vals", [KEYS, NB, HEADS, DV])
        qT = sb("qT", [P, DC, T])
        smax = sb("smax", [P, NT, HEADS])
        smax_hi = sb("smax_hi", [P, NT, 2, HEADS], BF16)
        smax_rest = sb("smax_rest", [P, NT, HEADS])
        smaxT = sb("smaxT", [2 * HEADS, T], BF16)
        probs = sb("probs", [KEYS, 4, 2, S])
        wsum = sb("wsum", [P, NT, HEADS])
        ctxn = feats[:, :, :].rearrange("p c (t h d) -> p (c t) h d", t=2, h=HEADS)
        ctxnT = qT
        zsum = sb("zsum", [P, DC, NB])
        g1 = sb("g1", [P, NB])
        g2 = sb("g2", [64, NB])
        gt = sb("gt", [P, NB])
        base = sb("base", [P, NB])
        spare = kmask[:, :, :, :, :].rearrange("p b c h k -> p (b c h k)")

        def in_spare(k, n, rows=P):
            return spare[0:rows, k * NB * S:(k + n) * NB * S]

        h1 = in_spare(0, 2).rearrange("p (b r s) -> p b r s", b=NB, r=2)
        h2 = in_spare(2, 1).rearrange("p (b s) -> p b s", b=NB)
        h3 = in_spare(3, 1, 64).rearrange("p (b s) -> p b s", b=NB)
        gate = in_spare(4, 1).rearrange("p (b s) -> p b s", b=NB)
        couple = in_spare(5, 1).rearrange("p (b s) -> p b s", b=NB)
        turn = sq[:, :, :].rearrange("p c (b s) -> p c b s", b=NB)

        xpad = sb("xpad", [P, IC, NB, PAD + S])
        conv = sb("conv", [P, IC, T])
        xc = sb("xc", [P, IC, T])
        res = sb("res", [P, IC, T])
        soft = sb("soft", [P, IC, T])
        delta = soft
        xc2 = sb("xc2", [P, IC, T])
        a_ring = sb("a_ring", [P, RING, NB, S])
        h_ring = sb("h_ring", [P, RING, T])
        yT = conv

        ctxTb = sb("ctxTb", [P, DC, NB * KEYS])
        ctxb = sb("ctxb", [KEYS, NB, D])
        ug = sb("ug", [KEYS, T])
        uu = sb("uu", [KEYS, T])
        logit = sb("logit", [P, NT, EXPERTS])
        lmax = sb("lmax", [P, NT])
        prob = sb("prob", [P, NT, EXPERTS])
        pmax = sb("pmax", [P, NT])
        psm = sb("psm", [P, NT])
        pinv = sb("pinv", [P, NT])
        pgate = sb("pgate", [P, NT])
        pick = sb("pick", [P, NT, EXPERTS])
        prank = sb("prank", [P, NT, EXPERTS])
        rmax = sb("rmax", [P, NT])
        weight = sb("weight", [P, NT, EXPERTS])
        weightT = ug[0:EXPERTS, :]

        class Norm:
            def __init__(self, name, x, xT):
                self.stats = sb(f"{name}_stats", [P, NT, 6])
                self.mv = sb(f"{name}_mv", [P, NT, 2])
                self.logv = sb(f"{name}_logv", [P, NT])
                self.rstd = sb(f"{name}_rstd", [P, NT])
                self.x = self.sum = x
                self.xT = xT
                self.sub_ready = sem(f"{name}_sub_ready", 2)
                self.sum_ready = sem(f"{name}_sum_ready", 2)
                self.var_ready = sem(f"{name}_var_ready", 1)
                self.log_ready = sem(f"{name}_log_ready", 1)
                self.rstd_ready = sem(f"{name}_rstd_ready", 1)
                self.x_ready = sem(f"{name}_x_ready", NT)
                if xT is not None:
                    self.turned = sem(f"{name}_turned", DC)
                    self.xT_ready = sem(f"{name}_xT_ready", DC)
                self.chain = chain(f"{name}_chain", NT)

        x12, x3, x45, x6 = (sb(n, [P, NT, D]) for n in ("x12", "x3", "x45", "x6"))
        x12T, x3T, x45T = (sb(n, [P, DC, T]) for n in ("x12T", "x3T", "x45T"))
        n1, n2, n3 = Norm("ln1", x12, x12T), Norm("ln2", x12, x12T), Norm("ln3", x3, x3T)
        n4, n5, n6 = Norm("ln4", x45, x45T), Norm("ln5", x45, x45T), Norm("ln6", x6, None)
        x1b, acc = x12, x6

        loaded_w = sem("loaded_w")
        loaded_x = sem("loaded_x", 3 * 16)
        loaded_ctx = sem("loaded_ctx", 2 * 16)
        stored = sem("stored", 16, 1)
        const_v = chain("const_v", 14)
        const_v2 = sem("const_v2")
        const_a = sem("const_a")
        const_p = sem("const_p")
        const_t = sem("const_t")

        held = sem("held")
        sq_chain = chain("sq_chain", 2)
        sqsum_ready = sem("sqsum_ready", 1)
        dots_ready = sem("dots_ready", DC, 1)
        feats_ready = sem("feats_ready", DC)

        kT_psum = sem("kT_psum", 1)
        v_psum = sem("v_psum", 1)
        q_psum = sem("q_psum", DC)
        kT_ready = sem("kT_ready", DC)
        qT_ready = sem("qT_ready", DC)
        vals_ready = sem("vals_ready", NB)
        kmask_ready = sem("kmask_ready", NB * DC)
        scores_ready = sem("scores_ready", NT * DC)
        smax_ready = sem("smax_ready", NT * DC)
        hi_chain = chain("hi_chain", 2)
        hi_ready = sem("hi_ready", 1)
        smaxT_psum = sem("smaxT_psum", 1)
        smaxT_ready = sem("smaxT_ready", 1)
        logits_ready = sem("logits_ready", NB * HEADS // 2)
        probs_ready = sem("probs_ready", NB * HEADS // 2)
        pv_ready = sem("pv_ready", NB * HEADS // 2)
        att_chain = chain("att_chain", NT)
        ctxn_ready = sem("ctxn_ready", NT)
        ctxn_turned = sem("ctxn_turned", DC)
        ctxnT_ready = sem("ctxnT_ready", DC)
        x1b_ready = sem("x1b_ready", 1)

        zsum_ready = sem("zsum_ready", DC)
        glob_psum = sem("glob_psum", 3)
        glob_ready = sem("glob_ready", 3)
        base_ready = sem("base_ready", 1)
        CYC = 3 * NB
        l1_psum = sem("l1_psum", CYC)
        l1_ready = sem("l1_ready", 2 * CYC)
        l2_psum = sem("l2_psum", CYC)
        l2_ready = sem("l2_ready", CYC)
        l3_psum = sem("l3_psum", CYC)
        l3_ready = sem("l3_ready", CYC)
        l4_psum = sem("l4_psum", CYC)
        gate_ready = sem("gate_ready", CYC)
        cyc_chain = chain("cyc_chain", 3 * CYC)
        z_ready = sem("z_ready", 2 * CYC)

        in_psum = sem("in_psum", 2 * IC)
        in_read = sem("in_read", 2 * IC)
        conv_chain = chain("conv_chain", IC * (TAPS - 1))
        conv_ready = sem("conv_ready", IC)
        xc_ready = sem("xc_ready", IC)
        exp_ready = sem("exp_ready", 1)
        soft_ready = sem("soft_ready", 1)
        xc2_ready = sem("xc2_ready", 1)
        delta_ready = sem("delta_ready", IC)
        STEPS = IC * STATES
        decay_ready = sem("decay_ready", STEPS)
        state_ready = sem("state_ready", STEPS)
        state_summed = sem("state_summed", STEPS)
        y_chain = chain("y_chain", 2 * IC)
        ysum_read = sem("ysum_read", IC)
        y_ready = sem("y_ready", IC)

        u_psum = sem("u_psum", 1)
        ug_ready = sem("ug_ready", 1)
        uu_ready = sem("uu_ready", 1)
        router_psum = sem("router_psum", 1)
        logit_chain = chain("logit_chain", 2)
        logit_ready = sem("logit_ready", 1)
        prob_ready = sem("prob_ready", 1)
        pick_chain = chain("pick_chain", 8)
        weight_ready = sem("weight_ready", 1)
        weight_turned = sem("weight_turned", 1)
        weightT_ready = sem("weightT_ready", 1)
        bias_ready = sem("bias_ready", 2)
        MOE = NT * EXPERTS // 2
        expert_ready = sem("expert_ready", MOE)
        acc_start = sem("acc_start", 2)
        expert_added = sem("expert_added", 2 * MOE, 1)

        def norm_add(v, n, g, parts):
            for half, (sub, resid) in enumerate(parts):
                v.wait_ge(n.sub_ready.sem, n.sub_ready.at(g, half + 1))
                v.tensor_tensor(out=n.sum[:, 2 * half:2 * half + 2, :], in0=sub, in1=resid,
                                op=ALU.add).then_inc(n.sum_ready.sem, 1)

        def norm_stats(v, n, g):
            n.chain.start(v, g)
            for t in range(NT):
                v.wait_ge(n.sum_ready.sem, n.sum_ready.at(g, t // 2 + 1))
                n.chain.then(v.bn_stats(n.stats[:, t, :], n.sum[:, t, :]))
            n.chain.settle()
            v.sem_inc(held.sem, 1)
            for t in range(NT):
                last = v.bn_aggr(n.mv[:, t, :], n.stats[:, t, :])
            last.then_inc(n.var_ready.sem, 1)
            n.chain.end()

        def norm_rstd(a, n, g):
            a.wait_ge(n.var_ready.sem, n.var_ready.at(g, 1))
            a.activation(n.logv[:, :], n.mv[:, :, 1], ACT.Ln, bias=eps[:, :]).then_inc(n.log_ready.sem, 1)
            a.wait_ge(n.log_ready.sem, n.log_ready.at(g, 1))
            a.activation(n.rstd[:, :], n.logv[:, :], ACT.Exp, scale=-0.5).then_inc(n.rstd_ready.sem, 1)

        def norm_apply(v, n, g):
            v.wait_ge(n.rstd_ready.sem, n.rstd_ready.at(g, 1))
            for t in range(NT):
                v.tensor_scalar(n.x[:, t, :], n.sum[:, t, :], n.mv[:, t, 0:1], n.rstd[:, t:t + 1],
                                ALU.subtract, ALU.mult).then_inc(n.x_ready.sem, 1)

        def norm_turn(pe, n, g, banks):
            for c in range(DC):
                for t in range(NT):
                    pe.wait_ge(n.x_ready.sem, n.x_ready.at(g, t + 1))
                    last = pe.transpose(banks[c][:, t * P:(t + 1) * P], n.x[:, t, c * P:(c + 1) * P], ident[:, :])
                last.then_inc(n.turned.sem, 1)

        def norm_copy(a, n, g, banks):
            for c in range(DC):
                a.wait_ge(n.turned.sem, n.turned.at(g, c + 1))
                a.copy(n.xT[:, c, :], banks[c][:, :]).then_inc(n.xT_ready.sem, 1)

        def tiles(bank_, half=None):
            return bank_[:, :].rearrange("p (t d) -> p t d", t=2)

        OUT = [bank[2], bank[3]]
        TURN = [bank[4], bank[5]]
        MB = [bank[6], bank[7]]

        block = ctx.enter_context(nc.Block())

        @block.sync
        def _(sp):
            for name in W:
                sp.dma_start(W[name][:, :], ins[name]).then_inc(loaded_w.sem, 16)
            sp.dma_start(head_rows[:, :, :], ins["head_rows"]).then_inc(loaded_w.sem, 16)

            def load_front(g):
                sp.dma_start(x0T[:, :, :], ins["xT"][g]).then_inc(loaded_x.sem, 16)
                sp.dma_start(x0[:, :, :], ins["x"][g]).then_inc(loaded_x.sem, 16)
                sp.dma_start(ctxT[:, :, :], ins["ctxT"][g]).then_inc(loaded_x.sem, 16)

            def load_back(g):
                sp.dma_start(ctxTb[:, :, :], ins["ctxT"][g]).then_inc(loaded_ctx.sem, 16)
                sp.dma_start(ctxb[:, :, :], ins["ctx"][g]).then_inc(loaded_ctx.sem, 16)

            def front_free(g):
                sp.wait_ge(n1.sum_ready.sem, n1.sum_ready.at(g, 2))
                sp.sem_inc(held.sem, 1)
                sp.wait_ge(v_psum.sem, v_psum.at(g, 1))
                sp.sem_inc(held.sem, 1)
                sp.wait_ge(kT_psum.sem, kT_psum.at(g, 1))
                sp.sem_inc(held.sem, 1)

            def store(g):
                sp.wait_ge(n6.x_ready.sem, n6.x_ready.at(g, NT))
                sp.sem_inc(held.sem, 1)
                sp.dma_start(out[g], n6.x[:, :, :]).then_inc(stored.sem, 16)

            stored.start_ahead(sp)
            load_front(0)
            load_back(0)
            with sp.Fori(0, G - 1) as i:
                front_free(i)
                load_front(i + 1)
                sp.wait_ge(n5.sub_ready.sem, n5.sub_ready.at(i, 2))
                sp.sem_inc(held.sem, 1)
                load_back(i + 1)
                store(i)
            store(G - 1)
            sp.wait_ge(stored.sem, stored.at(G, 0))

        @block.tensor
        def _(pe):
            def mm(o, l, r, start, stop):
                return pe.matmul(o, l, r, start=start, stop=stop)

            def setup():
                pe.wait_ge(loaded_w.sem, 16 * (len(W) + 1))
                pe.wait_ge(const_v.sem, const_v.per)
                pe.wait_ge(const_p.sem, 3)
                for r in range(DC):
                    for c in range(DC):
                        mm(bank[r][:, 0:D], rf_scaled[:, c, r * P:(r + 1) * P], rfwT[:, c, :], c == 0, False)
                    mm(bank[r][:, 0:D], rf_norm[:, r * P:(r + 1) * P], rf_sqsum[:, :], False, True)\
                        .then_inc(const_t.sem, 1)

            def rfs(g):
                pe.wait_ge(loaded_x.sem, loaded_x.at(g, 48))
                pe.wait_ge(sqsum_ready.sem, sqsum_ready.at(g, 1))
                for r in range(DC):
                    for c in range(DC):
                        mm(bank[r][:, :], rf_scaled[:, c, r * P:(r + 1) * P], x0T[:, c, :], c == 0, False)
                    mm(bank[r][:, :], rf_norm[:, r * P:(r + 1) * P], sqsum[:, :], False, True)\
                        .then_inc(dots_ready.sem, 1)

            def project(g, n, ready, lhsT, rhs, k, banks, wait_each=None):
                if wait_each is None:
                    pe.wait_ge(ready.sem, ready.at(g, ready.per))
                for t in range(NT):
                    for c in range(k):
                        last = mm(banks[t // 2][:, t % 2 * D:t % 2 * D + D], lhsT[:, c, t * P:(t + 1) * P],
                                  rhs[:, c, :], c == 0, c == k - 1)
                    if t % 2:
                        last.then_inc(n.sub_ready.sem, 1)

            def qkv(g):
                for e in range(DC):
                    for c in range(DC):
                        last = mm(bank[0][:, e * 240:(e + 1) * 240], wk[:, c, e * P:(e + 1) * P], ctxT[:, c, :],
                                  c == 0, c == DC - 1)
                last.then_inc(kT_psum.sem, 1)
                for b in range(NB):
                    for c in range(DC):
                        last = mm(bank[1][0:KEYS, b * D:(b + 1) * D], ctxT[:, c, b * KEYS:(b + 1) * KEYS],
                                  wv[:, c, :], c == 0, c == DC - 1)
                last.then_inc(v_psum.sem, 1)

            def queries(g):
                pe.wait_ge(n1.xT_ready.sem, n1.xT_ready.at(g, DC))
                pe.wait_ge(n1.sum_ready.sem, n1.sum_ready.at(g, 2))
                for e in range(DC):
                    for c in range(DC):
                        last = mm(bank[2 + e][:, :], wq[:, c, e * P:(e + 1) * P], n1.xT[:, c, :], c == 0, c == DC - 1)
                    last.then_inc(q_psum.sem, 1)

            def scores(g):
                pe.wait_ge(vals_ready.sem, vals_ready.at(g, NB))
                for s in range(NT * DC):
                    t, e = divmod(s, DC)
                    pair = s % 2
                    pe.wait_ge(qT_ready.sem, qT_ready.at(g, DC))
                    pe.wait_ge(kmask_ready.sem, kmask_ready.at(g, (t // 2 + 1) * DC))
                    if s >= 2:
                        pe.wait_ge(smax_ready.sem, smax_ready.at(g, s - 1))
                    for half in range(2):
                        last = mm(bank[2 * pair + half][:, 0:480], qT[:, e, t * P:(t + 1) * P],
                                  kmask[:, t // 2, e, 4 * half:4 * half + 4, :], True, True)
                    last.then_inc(scores_ready.sem, 1)
                pe.wait_ge(hi_ready.sem, hi_ready.at(g, 1))
                pe.wait_ge(n1.xT_ready.sem, n1.xT_ready.at(g, DC))
                smaxT_bank = bank[4][0:2 * HEADS, 0:T // 2].bitcast(BF16)
                for t in range(NT):
                    last = pe.transpose(smaxT_bank[:, t * P:(t + 1) * P],
                                        smax_hi[:, t, :, :].rearrange("p a h -> p (a h)"), ident16[:, :])
                last.then_inc(smaxT_psum.sem, 1)

            def weigh(g, s):
                b, pair = divmod(s, HEADS // 2)
                if s == 0:
                    pe.wait_ge(smaxT_ready.sem, smaxT_ready.at(g, 1))
                if s >= 4:
                    pe.wait_ge(probs_ready.sem, probs_ready.at(g, s - 3))
                for k in range(2):
                    h = 2 * pair + k
                    dst = bank[s % 4][0:KEYS, k * S:(k + 1) * S]
                    mm(dst, kmask[:, b, h // HC, h % HC, :], qT[:, h // HC, b * S:(b + 1) * S], True, False)
                    last = mm(dst, head_rows[:, h, :], smaxT[:, b * S:(b + 1) * S], False, True)
                last.then_inc(logits_ready.sem, 1)

            def mix(g, s):
                b, pair = divmod(s, HEADS // 2)
                pe.wait_ge(probs_ready.sem, probs_ready.at(g, s + 1))
                if pair == 0 and b:
                    pe.wait_ge(ctxn_ready.sem, ctxn_ready.at(g, 2 * b))
                for q in range(2):
                    for k in range(2):
                        h = 2 * pair + k
                        last = mm(bank[4 + q][:, h * DV:(h + 1) * DV], probs[:, s % 4, k, q * P:(q + 1) * P],
                                  vals[:, b, h, :], True, True)
                last.then_inc(pv_ready.sem, 1)

            def attend(g):
                n = NB * HEADS // 2
                for s in range(n + 2):
                    if s < n:
                        weigh(g, s)
                    if s >= 2:
                        mix(g, s - 2)
                pe.wait_ge(probs_ready.sem, probs_ready.at(g, n))
                for c in range(DC):
                    for t in range(NT):
                        pe.wait_ge(ctxn_ready.sem, ctxn_ready.at(g, t + 1))
                        last = pe.transpose(bank[c][:, t * P:(t + 1) * P],
                                            ctxn[:, t, c * HC:(c + 1) * HC, :].rearrange("p h d -> p (h d)"),
                                            ident[:, :])
                    last.then_inc(ctxn_turned.sem, 1)
                project(g, n2, ctxnT_ready, ctxnT, wo, DC, OUT)
                norm_turn(pe, n2, g, TURN)

            def glob(g):
                z = bank[0]
                pe.wait_ge(zsum_ready.sem, zsum_ready.at(g, DC))
                for c in range(DC):
                    last = mm(z[:, 0:NB], gc_w1[:, c, :], zsum[:, c, :], c == 0, c == DC - 1)
                last.then_inc(glob_psum.sem, 1)
                pe.wait_ge(glob_ready.sem, glob_ready.at(g, 1))
                mm(z[0:64, NB:2 * NB], W["gc_w2"][:, :], g1[:, :], True, True).then_inc(glob_psum.sem, 1)
                pe.wait_ge(glob_ready.sem, glob_ready.at(g, 2))
                mm(z[:, 2 * NB:3 * NB], W["gc_w3"][:, :], g2[:, :], True, True).then_inc(glob_psum.sem, 1)

            def cycle(g, k):
                for b in range(NB):
                    s = k * NB + b
                    if k:
                        pe.wait_ge(z_ready.sem, z_ready.at(g, 2 * (s - NB) + 2))
                    elif b == 0:
                        pe.wait_ge(glob_ready.sem, glob_ready.at(g, 3))
                        pe.wait_ge(n2.xT_ready.sem, n2.xT_ready.at(g, DC))
                    for r in range(2):
                        for c in range(DC):
                            last = mm(bank[b][:, r * S:(r + 1) * S], cn_w1[:, c, r * P:(r + 1) * P],
                                      n2.xT[:, c, b * S:(b + 1) * S], c == 0, c == DC - 1)
                    last.then_inc(l1_psum.sem, 1)
                for b in range(NB):
                    s = k * NB + b
                    pe.wait_ge(l1_ready.sem, l1_ready.at(g, 2 * s + 2))
                    if k == 0:
                        pe.wait_ge(n2.sum_ready.sem, n2.sum_ready.at(g, 2))
                    for c in range(2):
                        last = mm(bank[2 + b][:, 0:S], cn_w2[:, c, :], h1[:, b, c, :], c == 0, c == 1)
                    last.then_inc(l2_psum.sem, 1)
                for b in range(NB):
                    s = k * NB + b
                    pe.wait_ge(l2_ready.sem, l2_ready.at(g, s + 1))
                    mm(bank[2 + b][0:64, S:2 * S], W["cn_w3"][:, :], h2[:, b, :], True, True)\
                        .then_inc(l3_psum.sem, 1)
                for b in range(NB):
                    s = k * NB + b
                    pe.wait_ge(l3_ready.sem, l3_ready.at(g, s + 1))
                    mm(bank[4 + b][:, 0:S], W["cn_w4"][:, :], h3[:, b, :], True, True).then_inc(l4_psum.sem, 1)

            def rotate_back(g):
                for t in range(NT):
                    pe.wait_ge(z_ready.sem, z_ready.at(g, 2 * (CYC - NB) + 2 * (t // 2) + 2))
                    for c in range(DC):
                        last = pe.transpose(OUT[t // 2][:, t % 2 * D + c * P:t % 2 * D + (c + 1) * P],
                                            n2.xT[:, c, t * P:(t + 1) * P], ident[:, :])
                    if t % 2:
                        last.then_inc(n3.sub_ready.sem, 1)
                norm_turn(pe, n3, g, TURN)

            def mamba_in(g):
                pe.wait_ge(n3.xT_ready.sem, n3.xT_ready.at(g, DC))
                for j in range(2 * IC):
                    if j >= 2:
                        pe.wait_ge(in_read.sem, in_read.at(g, j - 1))
                    for c in range(DC):
                        last = mm(MB[j % 2][:, :], winT[:, c, j * P:(j + 1) * P], n3.xT[:, c, :], c == 0, c == DC - 1)
                    last.then_inc(in_psum.sem, 1)

            def mamba_sum(g, c):
                if c < 2:
                    pe.wait_ge(in_read.sem, in_read.at(g, 2 * IC))
                else:
                    pe.wait_ge(ysum_read.sem, ysum_read.at(g, c - 1))
                for n in range(STATES):
                    k = c * STATES + n
                    pe.wait_ge(state_ready.sem, state_ready.at(g, k + 1))
                    mm(MB[c % 2][:, :], ident[:, :], h_ring[:, k % RING, :], n == 0, n == STATES - 1)\
                        .then_inc(state_summed.sem, 1)

            def mamba_out(g):
                project(g, n4, y_ready, yT, woutT, IC, MB)
                pe.wait_ge(n4.sum_ready.sem, n4.sum_ready.at(g, 2))
                norm_turn(pe, n4, g, MB)

            def gated(g):
                pe.wait_ge(n4.xT_ready.sem, n4.xT_ready.at(g, DC))
                pe.wait_ge(loaded_ctx.sem, loaded_ctx.at(g, 32))
                for b in range(NB):
                    for c in range(DC):
                        last = mm(bank[0][0:KEYS, b * S:(b + 1) * S], ctxTb[:, c, b * KEYS:(b + 1) * KEYS],
                                  n4.xT[:, c, b * S:(b + 1) * S], c == 0, c == DC - 1)
                last.then_inc(u_psum.sem, 1)
                pe.wait_ge(uu_ready.sem, uu_ready.at(g, 1))
                for t in range(NT):
                    last = mm(OUT[t // 2][:, t % 2 * D:t % 2 * D + D], uu[:, t * P:(t + 1) * P],
                              ctxb[:, t // 2, :], True, True)
                    if t % 2:
                        last.then_inc(n5.sub_ready.sem, 1)
                norm_turn(pe, n5, g, TURN)

            def experts(g):
                pe.wait_ge(n5.xT_ready.sem, n5.xT_ready.at(g, DC))
                for t in range(NT):
                    for c in range(DC):
                        last = mm(bank[0][:, t * EXPERTS:(t + 1) * EXPERTS], n5.xT[:, c, t * P:(t + 1) * P],
                                  router_w[:, c, :], c == 0, c == DC - 1)
                last.then_inc(router_psum.sem, 1)
                pe.wait_ge(weight_ready.sem, weight_ready.at(g, 1))
                for t in range(NT):
                    last = pe.transpose(bank[1][0:EXPERTS, t * P:(t + 1) * P], weight[:, t, :], ident[:, :])
                last.then_inc(weight_turned.sem, 1)
                pe.wait_ge(weightT_ready.sem, weightT_ready.at(g, 1))
                pe.wait_ge(n5.sum_ready.sem, n5.sum_ready.at(g, 2))
                for t in range(NT):
                    last = mm(OUT[t // 2][:, t % 2 * D:t % 2 * D + D], weightT[:, t * P:(t + 1) * P],
                              W["expert_b"][:, :], True, True)
                    if t % 2:
                        last.then_inc(bias_ready.sem, 1)
                ring = [bank[0], bank[1], bank[4], bank[5]]
                for s in range(MOE):
                    pair, t = s // NT, s % NT
                    if s >= 4:
                        pe.wait_ge(expert_added.sem, expert_added.at(g, 4 * (s // 2 - 1)))
                    for c in range(DC):
                        last = mm(ring[s % 4][:, :], n5.xT[:, c, t * P:(t + 1) * P],
                                  expert_w[:, c, pair * 2 * D:(pair + 1) * 2 * D], c == 0, c == DC - 1)
                    last.then_inc(expert_ready.sem, 1)

            def front(g, after_back):
                if after_back is not None:
                    pe.wait_ge(expert_added.sem, expert_added.at(after_back, 0))
                rfs(g)
                project(g, n1, feats_ready, feats, rf_out, DC, OUT)
                pe.wait_ge(feats_ready.sem, feats_ready.at(g, DC))
                qkv(g)
                norm_turn(pe, n1, g, TURN)
                queries(g)
                scores(g)
                attend(g)
                glob(g)
                for k in range(3):
                    cycle(g, k)
                rotate_back(g)

            def mamba(g):
                mamba_in(g)
                for c in range(IC):
                    mamba_sum(g, c)
                mamba_out(g)

            def back(g):
                gated(g)
                experts(g)

            setup()
            dots_ready.start_ahead(pe)
            pe.wait_ge(const_a.sem, 4)
            with pe.Fori(0, G) as i:
                front(i, i)
                mamba(i)
                back(i)

        @block.vector
        def _(v):
            def setup():
                const_v.start(v, 0)
                for k in range(RING):
                    const_v.then(v.memset(a_ring[:, k, :, 0:1], 0.0))
                const_v.then(v.memset(xpad[:, :, :, 0:PAD], 0.0))
                const_v.then(v.memset(vals[:, :, :, DK:DV], 1.0))
                const_v.then(v.memset(eps[:, :], EPS))
                v.wait_ge(loaded_w.sem, 16 * (len(W) + 1))
                for c in range(DC):
                    const_v.then(v.tensor_tensor(out=rf_scaled[:, c, :], in0=rf_scaled[:, c, :], in1=row("xis"),
                                                 op=ALU.mult))
                const_v.link(v.tensor_tensor(out=rf_norm[:, :], in0=row("xis"), in1=row("xis"), op=ALU.mult))
                const_v.then(v.tensor_scalar(rf_norm[:, :], rf_norm[:, :], -0.5, None, ALU.mult))
                at = COLUMNS["xis"][0]
                const_v.then(v.tensor_scalar(rf_bias[:, :], W["columns"][:, at:at + DC], -0.5 * float(np.log(RFS)),
                                             None, ALU.add))
                const_v.then(v.tensor_copy(ident16[:, :], ident[:, :]))
                const_v.then(v.tensor_scalar(half_b4[:, :], col("cn_b4"), 0.5, None, ALU.mult))
                const_v.end()
                v.tensor_scalar(half_gb3[:, :], col("gc_b3"), 0.5, None, ALU.mult).then_inc(const_v2.sem, 1)
                v.tensor_scalar(gate_scale[:, :], col("range"), 0.3, col("sign"), ALU.mult, ALU.mult)\
                    .then_inc(const_v2.sem, 1)
                v.tensor_scalar(glob_scale[:, :], col("range"), 0.7, col("sign"), ALU.mult, ALU.mult)\
                    .then_inc(const_v2.sem, 1)
                v.tensor_scalar(base_sign[:, :], col("sign"), 0.1, None, ALU.mult).then_inc(const_v2.sem, 1)
                v.wait_ge(const_a.sem, 1)
                v.tensor_scalar(decay[:, :], decay[:, :], -1.0, None, ALU.mult).then_inc(const_v2.sem, 1)
                v.wait_ge(const_v2.sem, 5)

            def ln1(g):
                v.wait_ge(loaded_x.sem, loaded_x.at(g, 48))
                norm_add(v, n1, g, [(tiles(OUT[h]), x0[:, 2 * h:2 * h + 2, :]) for h in range(2)])
                norm_stats(v, n1, g)
                v.wait_ge(v_psum.sem, v_psum.at(g, 1))
                for b in range(NB):
                    v.tensor_tensor(out=vals[:, b, :, 0:DK],
                                    in0=bank[1][0:KEYS, b * D:(b + 1) * D].rearrange("p (h d) -> p h d", h=HEADS),
                                    in1=row("bv")[0:KEYS, :].rearrange("p (h d) -> p h d", h=HEADS),
                                    op=ALU.add).then_inc(vals_ready.sem, 1)
                norm_apply(v, n1, g)

            def maxima(g):
                for s in range(NT * DC):
                    t, e = divmod(s, DC)
                    v.wait_ge(scores_ready.sem, scores_ready.at(g, s + 1))
                    for half in range(2):
                        h0 = e * HC + 4 * half
                        last = v.tensor_reduce(smax[:, t, h0:h0 + 4],
                                               bank[2 * (s % 2) + half][:, 0:480].rearrange("p (h k) -> p h k", h=4),
                                               AX, ALU.max)
                    last.then_inc(smax_ready.sem, 1)
                v.wait_ge(smax_ready.sem, smax_ready.at(g, NT * DC))
                hi_chain.start(v, g)
                hi_chain.link(v.tensor_scalar(smax_hi[:, :, 0, :], smax[:, :, :], -1.0, None, ALU.mult))
                hi_chain.link(v.scalar_tensor_tensor(out=smax_rest[:, :, :], in0=smax[:, :, :], scalar=-1.0,
                                                     in1=smax_hi[:, :, 0, :], op0=ALU.mult, op1=ALU.subtract))
                hi_chain.end()
                v.tensor_copy(smax_hi[:, :, 1, :], smax_rest[:, :, :]).then_inc(hi_ready.sem, 1)
                v.wait_ge(smaxT_psum.sem, smaxT_psum.at(g, 1))
                v.tensor_copy(smaxT[:, :], bank[4][0:2 * HEADS, 0:T // 2].bitcast(BF16)).then_inc(smaxT_ready.sem, 1)

            def normalize_context(g, b):
                v.wait_ge(pv_ready.sem, pv_ready.at(g, (b + 1) * HEADS // 2))
                for q in range(2):
                    t = 2 * b + q
                    o = bank[4 + q][:, 0:HEADS * DV].rearrange("p (h d) -> p h d", h=HEADS)
                    att_chain.then(v.reciprocal(wsum[:, t, :], o[:, :, DK]))
                for q in range(2):
                    t = 2 * b + q
                    o = bank[4 + q][:, 0:HEADS * DV].rearrange("p (h d) -> p h d", h=HEADS)
                    v.wait_ge(att_chain.sem, att_chain.at(g, t + 1))
                    v.tensor_tensor(out=ctxn[:, t, :, :], in0=o[:, :, 0:DK],
                                    in1=wsum[:, t, :].unsqueeze(2).to_broadcast([P, HEADS, DK]),
                                    op=ALU.mult).then_inc(ctxn_ready.sem, 1)

            def context(g):
                att_chain.start(v, g)
                for b in range(NB):
                    normalize_context(g, b)
                att_chain.end()

            def ln2(g):
                v.wait_ge(x1b_ready.sem, x1b_ready.at(g, 1))
                norm_add(v, n2, g, [(tiles(OUT[h]), x1b[:, 2 * h:2 * h + 2, :]) for h in range(2)])
                norm_stats(v, n2, g)
                norm_apply(v, n2, g)

            def coupling(g):
                for c in range(DC):
                    v.wait_ge(n2.xT_ready.sem, n2.xT_ready.at(g, c + 1))
                    v.tensor_reduce(zsum[:, c, :], n2.xT[:, c, :].rearrange("p (b s) -> p b s", b=NB), AX, ALU.add)\
                        .then_inc(zsum_ready.sem, 1)
                v.wait_ge(glob_ready.sem, glob_ready.at(g, 3))
                v.tensor_scalar(base[:, :], gt[:, :], glob_scale[:, :], base_sign[:, :], ALU.mult, ALU.add)\
                    .then_inc(base_ready.sem, 1)
                v.wait_ge(base_ready.sem, base_ready.at(g, 1))
                cyc_chain.start(v, g)
                for s in range(CYC):
                    b = s % NB
                    z0 = n2.xT[:, 0, b * S:(b + 1) * S]
                    z1 = n2.xT[:, 1, b * S:(b + 1) * S]
                    v.wait_ge(gate_ready.sem, gate_ready.at(g, s + 1))
                    cyc_chain.link(v.tensor_scalar(couple[:, b, :], gate[:, b, :], gate_scale[:, :], base[:, b:b + 1],
                                                   ALU.mult, ALU.add))
                    cyc_chain.then(v.tensor_tensor(out=turn[:, 0, b, :], in0=couple[:, b, :], in1=z1, op=ALU.mult))
                    cyc_chain.link(v.tensor_tensor(out=turn[:, 1, b, :], in0=couple[:, b, :], in1=z0, op=ALU.mult))
                    v.tensor_tensor(out=z0, in0=z0, in1=turn[:, 0, b, :], op=ALU.add).then_inc(z_ready.sem, 1)
                    v.tensor_tensor(out=z1, in0=z1, in1=turn[:, 1, b, :], op=ALU.subtract).then_inc(z_ready.sem, 1)
                cyc_chain.end()

            def ln3(g):
                norm_add(v, n3, g, [(tiles(OUT[h]), n2.x[:, 2 * h:2 * h + 2, :]) for h in range(2)])
                norm_stats(v, n3, g)
                norm_apply(v, n3, g)

            def convolve(g):
                conv_chain.start(v, g)
                for c0 in range(0, IC, 2):
                    v.wait_ge(in_read.sem, in_read.at(g, c0 + 2))
                    for k in range(TAPS):
                        for c in range(c0, c0 + 2):
                            o = conv[:, c, :].rearrange("p (b s) -> p b s", b=NB)
                            x = xpad[:, c, :, k:k + S]
                            w = col("conv_w", c * TAPS + k)
                            if k:
                                conv_chain.settle(1)
                            if k == 0:
                                step = v.tensor_scalar(o, x, w, None, ALU.mult)
                            else:
                                step = v.scalar_tensor_tensor(out=o, in0=x, scalar=w, in1=o, op0=ALU.mult,
                                                              op1=ALU.add)
                            if k < TAPS - 1:
                                conv_chain.then(step)
                            else:
                                step.then_inc(conv_ready.sem, 1)
                                if c == c0:
                                    conv_chain.settle()
                conv_chain.end()

            def scan(g, c, n0, n1_):
                for n in range(n0, n1_):
                    k = c * STATES + n
                    if k == 0:
                        v.wait_ge(xc2_ready.sem, xc2_ready.at(g, 1))
                    v.wait_ge(decay_ready.sem, decay_ready.at(g, k + 1))
                    if k >= RING:
                        v.wait_ge(state_summed.sem, state_summed.at(g, k + 1 - RING))
                    v.tensor_tensor_scan(h_ring[:, k % RING, :], a_ring[:, k % RING, :, :].rearrange("p b s -> p (b s)"),
                                         xc2[:, c, :], 0.0, ALU.mult, ALU.add).then_inc(state_ready.sem, 1)

            def gate_y(g, c):
                v.wait_ge(state_summed.sem, state_summed.at(g, (c + 1) * STATES))
                v.tensor_tensor(out=yT[:, c, :], in0=MB[c % 2][:, :], in1=xc[:, c, :], op=ALU.mult)\
                    .then_inc(ysum_read.sem, 1)
                v.wait_ge(ysum_read.sem, ysum_read.at(g, c + 1))
                y_chain.then(v.tensor_tensor(out=yT[:, c, :], in0=yT[:, c, :], in1=res[:, c, :], op=ALU.mult))
                y_chain.link(v.tensor_scalar(xc2[:, c, :], xc[:, c, :], col("D", c), None, ALU.mult))
                v.tensor_tensor(out=yT[:, c, :], in0=yT[:, c, :], in1=xc2[:, c, :], op=ALU.add)\
                    .then_inc(y_ready.sem, 1)

            def selective(g):
                y_chain.start(v, g)
                for c in range(IC):
                    scan(g, c, 0, 4)
                    if c:
                        gate_y(g, c - 1)
                    scan(g, c, 4, STATES)
                gate_y(g, IC - 1)
                y_chain.end()

            def ln4(g):
                norm_add(v, n4, g, [(tiles(MB[h]), n3.x[:, 2 * h:2 * h + 2, :]) for h in range(2)])
                norm_stats(v, n4, g)
                norm_apply(v, n4, g)

            def gated(g):
                v.wait_ge(ug_ready.sem, ug_ready.at(g, 1))
                v.tensor_tensor(out=uu[:, :], in0=bank[0][0:KEYS, :], in1=ug[:, :], op=ALU.mult)\
                    .then_inc(uu_ready.sem, 1)
                norm_add(v, n5, g, [(tiles(OUT[h]), n4.x[:, 2 * h:2 * h + 2, :]) for h in range(2)])
                norm_stats(v, n5, g)
                norm_apply(v, n5, g)

            def over_experts(a):
                return a.unsqueeze(2).to_broadcast([P, NT, EXPERTS])

            def over_tiles(a):
                return a.unsqueeze(1).to_broadcast([P, NT, EXPERTS])

            def route(g):
                v.wait_ge(router_psum.sem, router_psum.at(g, 1))
                logit_chain.start(v, g)
                logit_chain.link(v.tensor_tensor(
                    out=logit[:, :, :], in0=bank[0][:, 0:NT * EXPERTS].rearrange("p (t e) -> p t e", t=NT),
                    in1=over_tiles(row("router_b")), op=ALU.add))
                logit_chain.link(v.tensor_reduce(lmax[:, :], logit[:, :, :], AX, ALU.max))
                logit_chain.end()
                v.tensor_tensor(out=logit[:, :, :], in0=logit[:, :, :], in1=over_experts(lmax[:, :]),
                                op=ALU.subtract).then_inc(logit_ready.sem, 1)
                v.wait_ge(prob_ready.sem, prob_ready.at(g, 1))
                pick_chain.start(v, g)
                pick_chain.then(v.tensor_reduce(pmax[:, :], prob[:, :, :], AX, ALU.max))
                pick_chain.link(v.tensor_reduce(psm[:, :], prob[:, :, :], AX, ALU.add))
                pick_chain.then(v.reciprocal(pinv[:, :], psm[:, :]))
                pick_chain.link(v.tensor_tensor(out=pick[:, :, :], in0=prob[:, :, :], in1=over_experts(pmax[:, :]),
                                                op=ALU.is_equal))
                pick_chain.then(v.tensor_tensor(out=pgate[:, :], in0=pmax[:, :], in1=pinv[:, :], op=ALU.mult))
                pick_chain.link(v.tensor_tensor(out=prank[:, :, :], in0=pick[:, :, :], in1=over_tiles(row("rank")),
                                                op=ALU.mult))
                pick_chain.link(v.tensor_reduce(rmax[:, :], prank[:, :, :], AX, ALU.max))
                pick_chain.link(v.tensor_tensor(out=pick[:, :, :], in0=prank[:, :, :], in1=over_experts(rmax[:, :]),
                                                op=ALU.is_equal))
                pick_chain.end()
                v.tensor_tensor(out=weight[:, :, :], in0=pick[:, :, :], in1=over_experts(pgate[:, :]),
                                op=ALU.mult).then_inc(weight_ready.sem, 1)
                v.wait_ge(weight_ready.sem, weight_ready.at(g, 1))

            def combine(g):
                v.wait_ge(stored.sem, stored.at(g, 0))
                ring = [bank[0], bank[1], bank[4], bank[5]]
                for h in range(2):
                    v.wait_ge(bias_ready.sem, bias_ready.at(g, h + 1))
                    v.tensor_tensor(out=acc[:, 2 * h:2 * h + 2, :], in0=tiles(OUT[h]), in1=n5.x[:, 2 * h:2 * h + 2, :],
                                    op=ALU.add).then_inc(acc_start.sem, 1)
                v.wait_ge(acc_start.sem, acc_start.at(g, 2))
                for s2 in range(MOE // 2):
                    pair, t0 = s2 // 2, s2 % 2 * 2
                    for e in range(2):
                        for t in (t0, t0 + 1):
                            s = pair * NT + t
                            done = 4 * s2 + 2 * e + (t - t0)
                            if e == 0:
                                v.wait_ge(expert_ready.sem, expert_ready.at(g, s + 1))
                            if e:
                                v.wait_ge(expert_added.sem, expert_added.at(g, done - 1))
                            elif pair:
                                v.wait_ge(expert_added.sem, expert_added.at(g, done - 5))
                            x = 2 * pair + e
                            v.scalar_tensor_tensor(out=acc[:, t, :], in0=ring[s % 4][:, e * D:(e + 1) * D],
                                                   scalar=weight[:, t, x:x + 1], in1=acc[:, t, :], op0=ALU.mult,
                                                   op1=ALU.add).then_inc(expert_added.sem, 1)

            def ln6(g):
                n = n6
                n.chain.start(v, g)
                v.wait_ge(expert_added.sem, expert_added.at(g, 2 * MOE))
                for t in range(NT):
                    n.chain.then(v.bn_stats(n.stats[:, t, :], acc[:, t, :]))
                n.chain.settle()
                v.sem_inc(held.sem, 1)
                for t in range(NT):
                    last = v.bn_aggr(n.mv[:, t, :], n.stats[:, t, :])
                last.then_inc(n.var_ready.sem, 1)
                n.chain.end()
                v.wait_ge(n.rstd_ready.sem, n.rstd_ready.at(g, 1))
                for t in range(NT):
                    v.tensor_scalar(n.x[:, t, :], acc[:, t, :], n.mv[:, t, 0:1], n.rstd[:, t:t + 1],
                                    ALU.subtract, ALU.mult).then_inc(n.x_ready.sem, 1)

            def front(g):
                ln1(g)
                maxima(g)
                context(g)
                ln2(g)
                coupling(g)
                ln3(g)

            def mamba(g):
                convolve(g)
                selective(g)
                ln4(g)

            def back(g):
                gated(g)
                route(g)
                combine(g)
                ln6(g)

            setup()
            expert_added.start_ahead(v)
            with v.Fori(0, G) as i:
                front(i)
                mamba(i)
                back(i)

        @block.scalar
        def _(a):
            def nat():
                a.preload_act_table_set("natural_log_exp_and_others")

            def setup():
                nat()
                a.wait_ge(loaded_w.sem, 16 * (len(W) + 1))
                at, n = COLUMNS["A_log"]
                a.activation(decay[:, :], W["columns"][:, at:at + n], ACT.Exp).then_inc(const_a.sem, 1)
                a.wait_ge(const_v.sem, const_v.per)
                a.wait_ge(const_v2.sem, 5)
                for r in range(DC):
                    a.wait_ge(const_t.sem, DC)
                    a.activation(rf_out[:, r, :], bank[r][:, 0:D], ACT.Exp, bias=rf_bias[:, r:r + 1])\
                        .then_inc(const_a.sem, 1)
                a.activation(g1[:, :], eps[:, :].to_broadcast([P, NB]), ACT.Copy).then_inc(const_a.sem, 1)

            def feat(g):
                for r in range(DC):
                    a.wait_ge(dots_ready.sem, dots_ready.at(g, r + 1))
                    a.activation(feats[:, r, :], bank[r][:, :], ACT.Exp, bias=rf_bias[:, r:r + 1])\
                        .then_inc(feats_ready.sem, 1)

            def keys(g):
                a.wait_ge(kT_psum.sem, kT_psum.at(g, 1))
                for e in range(DC):
                    a.activation(kT[:, e, :], bank[0][:, e * 240:(e + 1) * 240], ACT.Identity, bias=col("bk", e))\
                        .then_inc(kT_ready.sem, 1)

            def queries(g):
                for e in range(DC):
                    a.wait_ge(q_psum.sem, q_psum.at(g, e + 1))
                    a.activation(qT[:, e, :], bank[2 + e][:, :], ACT.Identity, bias=col("bq", e))\
                        .then_inc(qT_ready.sem, 1)

            def softmax(g):
                for s in range(NB * HEADS // 2):
                    a.wait_ge(logits_ready.sem, logits_ready.at(g, s + 1))
                    if s >= 4:
                        a.wait_ge(pv_ready.sem, pv_ready.at(g, s - 3))
                    a.activation(probs[:, s % 4, :, :].rearrange("p k s -> p (k s)"), bank[s % 4][0:KEYS, :],
                                 ACT.Exp, scale=1.0 / np.sqrt(DK)).then_inc(probs_ready.sem, 1)
                for c in range(DC):
                    a.wait_ge(ctxn_turned.sem, ctxn_turned.at(g, c + 1))
                    a.copy(ctxnT[:, c, :], bank[c][:, :]).then_inc(ctxnT_ready.sem, 1)

            def network(g):
                a.preload_act_table_set("gelu_and_others")
                z = bank[0]
                a.wait_ge(glob_psum.sem, glob_psum.at(g, 1))
                a.activation(g1[:, :], z[:, 0:NB], ACT.Gelu, bias=col("gc_b1"), scale=1.0 / S)\
                    .then_inc(glob_ready.sem, 1)
                a.wait_ge(glob_psum.sem, glob_psum.at(g, 2))
                a.activation(g2[:, :], z[0:64, NB:2 * NB], ACT.Gelu, bias=col("gc_b2", 0, 64))\
                    .then_inc(glob_ready.sem, 1)
                a.wait_ge(glob_psum.sem, glob_psum.at(g, 3))
                a.activation(gt[:, :], z[:, 2 * NB:3 * NB], ACT.Tanh, bias=half_gb3[:, :], scale=0.5)\
                    .then_inc(glob_ready.sem, 1)
                for k in range(3):
                    for b in range(NB):
                        s = k * NB + b
                        a.wait_ge(l1_psum.sem, l1_psum.at(g, s + 1))
                        for r in range(2):
                            a.activation(h1[:, b, r, :], bank[b][:, r * S:(r + 1) * S], ACT.Gelu,
                                         bias=col("cn_b1", r)).then_inc(l1_ready.sem, 1)
                    for b in range(NB):
                        s = k * NB + b
                        a.wait_ge(l2_psum.sem, l2_psum.at(g, s + 1))
                        a.activation(h2[:, b, :], bank[2 + b][:, 0:S], ACT.Gelu, bias=col("cn_b2"))\
                            .then_inc(l2_ready.sem, 1)
                    for b in range(NB):
                        s = k * NB + b
                        a.wait_ge(l3_psum.sem, l3_psum.at(g, s + 1))
                        a.activation(h3[:, b, :], bank[2 + b][0:64, S:2 * S], ACT.Gelu, bias=col("cn_b3", 0, 64))\
                            .then_inc(l3_ready.sem, 1)
                    for b in range(NB):
                        s = k * NB + b
                        a.wait_ge(l4_psum.sem, l4_psum.at(g, s + 1))
                        if k:
                            a.wait_ge(z_ready.sem, z_ready.at(g, 2 * (s - NB) + 2))
                        a.activation(gate[:, b, :], bank[4 + b][:, 0:S], ACT.Tanh, bias=half_b4[:, :], scale=0.5)\
                            .then_inc(gate_ready.sem, 1)
                nat()

            def mamba_in(g):
                for j in range(2 * IC):
                    if j == IC:
                        a.preload_act_table_set("silu_and_others")
                    a.wait_ge(in_psum.sem, in_psum.at(g, j + 1))
                    src = MB[j % 2][:, :]
                    if j < IC:
                        a.copy(xpad[:, j, :, PAD:PAD + S], src.rearrange("p (b s) -> p b s", b=NB))\
                            .then_inc(in_read.sem, 1)
                    else:
                        a.activation(res[:, j - IC, :], src, ACT.Silu).then_inc(in_read.sem, 1)
                for c in range(IC):
                    a.wait_ge(conv_ready.sem, conv_ready.at(g, c + 1))
                    a.activation(xc[:, c, :], conv[:, c, :], ACT.Silu, bias=col("conv_b", c)).then_inc(xc_ready.sem, 1)
                nat()
                a.wait_ge(xc_ready.sem, xc_ready.at(g, IC))
                a.activation(soft[:, :, :], xc[:, :, :], ACT.Exp, scale=-1.0).then_inc(exp_ready.sem, 1)
                a.wait_ge(exp_ready.sem, exp_ready.at(g, 1))
                a.activation(soft[:, :, :], soft[:, :, :], ACT.Ln, bias=1.0).then_inc(soft_ready.sem, 1)
                a.activation(xc2[:, :, :], xc[:, :, :], ACT.Square).then_inc(xc2_ready.sem, 1)

            def decays(g, c):
                for n in range(STATES):
                    k = c * STATES + n
                    if n == 0:
                        a.wait_ge(delta_ready.sem, delta_ready.at(g, c + 1))
                    if k >= RING:
                        a.wait_ge(state_ready.sem, state_ready.at(g, k + 1 - RING))
                    a.activation(a_ring[:, k % RING, :, 1:S],
                                 delta[:, c, :].rearrange("p (b s) -> p b s", b=NB)[:, :, 1:S],
                                 ACT.Exp, scale=decay[:, k:k + 1]).then_inc(decay_ready.sem, 1)

            def gated(g):
                a.preload_act_table_set("gelu_apprx_tanh_and_others")
                a.wait_ge(u_psum.sem, u_psum.at(g, 1))
                a.activation(ug[:, :], bank[0][0:KEYS, :], ACT.Gelu_apprx_tanh).then_inc(ug_ready.sem, 1)
                nat()

            def experts(g):
                a.wait_ge(logit_ready.sem, logit_ready.at(g, 1))
                a.activation(prob[:, :, :], logit[:, :, :], ACT.Exp).then_inc(prob_ready.sem, 1)
                a.wait_ge(weight_turned.sem, weight_turned.at(g, 1))
                a.copy(weightT[:, :], bank[1][0:EXPERTS, :]).then_inc(weightT_ready.sem, 1)
                norm_rstd(a, n6, g)

            def front(g):
                feat(g)
                keys(g)
                norm_rstd(a, n1, g)
                norm_copy(a, n1, g, TURN)
                queries(g)
                softmax(g)
                norm_rstd(a, n2, g)
                norm_copy(a, n2, g, TURN)
                network(g)
                norm_rstd(a, n3, g)
                norm_copy(a, n3, g, TURN)

            def mamba(g):
                mamba_in(g)
                for c in range(IC):
                    decays(g, c)
                norm_rstd(a, n4, g)
                norm_copy(a, n4, g, MB)

            def back(g):
                gated(g)
                norm_rstd(a, n5, g)
                norm_copy(a, n5, g, TURN)
                experts(g)

            setup()
            with a.Fori(0, G) as i:
                front(i)
                mamba(i)
                back(i)

        @block.gpsimd
        def _(p):
            def setup():
                p.wait_ge(loaded_w.sem, 16 * (len(W) + 1))
                for c in range(DC):
                    p.tensor_tensor(out=rf_sq[:, c, :], in0=rfwT[:, c, :], in1=rfwT[:, c, :], op=ALU.mult)\
                        .then_inc(const_p.sem, 1)
                p.wait_ge(const_p.sem, 2)
                p.tensor_tensor(out=rf_sqsum[:, :], in0=rf_sq[:, 0, :], in1=rf_sq[:, 1, :], op=ALU.add)\
                    .then_inc(const_p.sem, 1)
                p.wait_ge(const_p.sem, 3)
                p.wait_ge(const_t.sem, DC)

            def norms(g):
                p.wait_ge(loaded_x.sem, loaded_x.at(g, 48))
                p.wait_ge(dots_ready.sem, dots_ready.at(g, 0))
                sq_chain.start(p, g)
                for c in range(DC):
                    sq_chain.then(p.tensor_tensor(out=sq[:, c, :], in0=x0T[:, c, :], in1=x0T[:, c, :], op=ALU.mult))
                sq_chain.settle()
                sq_chain.end()
                p.tensor_tensor(out=sqsum[:, :], in0=sq[:, 0, :], in1=sq[:, 1, :], op=ALU.add)\
                    .then_inc(sqsum_ready.sem, 1)

            def mask_keys(g):
                at, n = COLUMNS["head_mask"]
                mask = W["columns"][:, at:at + n].unsqueeze(2).to_broadcast([P, HC, KEYS])
                p.wait_ge(kT_ready.sem, kT_ready.at(g, DC))
                for b in range(NB):
                    for e in range(DC):
                        k = kT[:, e, b * KEYS:(b + 1) * KEYS].unsqueeze(1).to_broadcast([P, HC, KEYS])
                        p.tensor_tensor(out=kmask[:, b, e, :, :], in0=k, in1=mask, op=ALU.mult)\
                            .then_inc(kmask_ready.sem, 1)

            def add_bias(g):
                p.wait_ge(n1.turned.sem, n1.turned.at(g, DC))
                p.tensor_tensor(out=x1b[:, :, :], in0=n1.x[:, :, :], in1=row("bo").unsqueeze(1).to_broadcast([P, NT, D]),
                                op=ALU.add).then_inc(x1b_ready.sem, 1)

            def deltas(g):
                p.wait_ge(soft_ready.sem, soft_ready.at(g, 1))
                for c in range(IC):
                    p.tensor_tensor(out=delta[:, c, :], in0=xc[:, c, :], in1=soft[:, c, :], op=ALU.add)\
                        .then_inc(delta_ready.sem, 1)

            def front(g):
                norms(g)
                mask_keys(g)
                add_bias(g)

            setup()
            with p.Fori(0, G) as i:
                front(i)
                deltas(i)


def host_arrays(x, ctx_1024, **w):
    x, c = np.asarray(x), np.asarray(ctx_1024)
    w = {k: np.asarray(a) for k, a in w.items()}

    def rows_to_chunks(a):
        k = a.shape[0] // P
        return a.reshape(k, P, -1).transpose(1, 0, 2).reshape(P, -1)

    def as_columns(a, n):
        return a.reshape(n, -1).T if a.size > n else np.broadcast_to(a.reshape(1, n), (P, n))

    def padded(a):
        return np.concatenate([a.reshape(-1, 1), np.zeros((P - a.size, 1), a.dtype)])

    cols = {
        "xis": as_columns(w["L0_attn_xis"], DC), "bq": as_columns(w["L0_xattn_bq"], DC),
        "bk": as_columns(w["L0_xattn_bk"], DC), "cn_b1": as_columns(w["L0_ffn_cn_b1"], 2),
        "cn_b2": as_columns(w["L0_ffn_cn_b2"], 1), "cn_b3": padded(w["L0_ffn_cn_b3"]),
        "cn_b4": as_columns(w["L0_ffn_cn_b4"], 1), "gc_b1": as_columns(w["L0_ffn_gc_b1"], 1),
        "gc_b2": padded(w["L0_ffn_gc_b2"]), "gc_b3": as_columns(w["L0_ffn_gc_b3"], 1),
        "range": as_columns(w["L0_ffn_adaptive_range"], 1),
        "sign": np.where(np.arange(P) < P // 2, 1.0, -1.0).astype(np.float32).reshape(P, 1),
        "conv_w": w["L1_attn_conv_w"].reshape(IC, P, TAPS).transpose(1, 0, 2).reshape(P, -1),
        "conv_b": as_columns(w["L1_attn_conv_b"], IC), "D": as_columns(w["L1_attn_D"], IC),
        "A_log": w["L1_attn_A_log"].reshape(IC, P, STATES).transpose(1, 0, 2).reshape(P, -1),
        "head_mask": (np.arange(P)[:, None] // DK == np.arange(HC)[None, :]).astype(np.float32),
    }
    rows = {"xis": w["L0_attn_xis"], "bv": w["L0_xattn_bv"], "bo": w["L0_xattn_bo"], "router_b": w["L1_ffn_router_b"],
            "rank": np.arange(EXPERTS, 0, -1).astype(np.float32)}
    head_rows = np.tile(np.repeat(np.eye(HEADS, dtype=mybir.dt.np(BF16)), KEYS, axis=1), (2, 1)).reshape(2 * HEADS, HEADS, KEYS)
    arrays = {
        "projT": rows_to_chunks(w["L0_attn_proj_matrix"].T), "rfwT": rows_to_chunks(w["L0_attn_input_weights"].T),
        "wq": rows_to_chunks(w["L0_xattn_Wq"]), "wk": rows_to_chunks(w["L0_xattn_Wk"]),
        "wv": rows_to_chunks(w["L0_xattn_Wv"]), "wo": rows_to_chunks(w["L0_xattn_Wo"]),
        "cn_w1": rows_to_chunks(w["L0_ffn_cn_w1"]), "cn_w2": rows_to_chunks(w["L0_ffn_cn_w2"]),
        "cn_w3": w["L0_ffn_cn_w3"], "cn_w4": np.broadcast_to(w["L0_ffn_cn_w4"], (64, P)),
        "gc_w1": rows_to_chunks(w["L0_ffn_gc_w1"]), "gc_w2": w["L0_ffn_gc_w2"],
        "gc_w3": np.broadcast_to(w["L0_ffn_gc_w3"], (64, P)),
        "winT": rows_to_chunks(w["L1_attn_W_in"].T), "woutT": rows_to_chunks(w["L1_attn_W_out"].T),
        "router_w": rows_to_chunks(w["L1_ffn_router_w"]),
        "expert_w": rows_to_chunks(w["L1_ffn_expert_w"].transpose(1, 0, 2).reshape(D, EXPERTS * D)),
        "expert_b": w["L1_ffn_expert_b"],
        "columns": np.concatenate([cols[n] for n in COLUMNS], axis=1),
        "rows": np.broadcast_to(np.concatenate([rows[n] for n in ROWS])[None, :], (P, N_ROWS)),
        "ident": np.eye(P, dtype=np.float32), "head_rows": head_rows,
        "x": x.reshape(G, NT, P, D).transpose(0, 2, 1, 3),
        "xT": x.reshape(G, T, DC, P).transpose(0, 3, 2, 1),
        "ctxT": c.reshape(G, NB * KEYS, DC, P).transpose(0, 3, 2, 1),
        "ctx": c.reshape(G, NB, KEYS, D).transpose(0, 2, 1, 3),
    }
    return {n: np.ascontiguousarray(a) for n, a in arrays.items()}


def kernel(**inputs):
    import concourse.bacc as bacc
    from concourse.bass_utils import run_bass_kernel_spmd

    arrays = host_arrays(**inputs)
    nc = bacc.Bacc("TRN2", target_bir_lowering=False, num_devices=1)
    aps = {n: nc.dram_tensor("in_" + n, a.shape, mybir.dt.from_np(a.dtype), kind="ExternalInput").ap() for n, a in arrays.items()}
    out = nc.dram_tensor("out", (G, P, NT, D), F32, kind="ExternalOutput").ap()
    program(nc, aps, out)
    r = run_bass_kernel_spmd(nc, [{"in_" + n: a for n, a in arrays.items()}], core_ids=[0])
    y = r.results[0]["out"]
    return np.asarray(y).reshape(G, P, NT, D).transpose(0, 2, 1, 3).reshape(B, S, D)
```

```python
from contextlib import ExitStack

import numpy as np

import concourse.bass as bass
from concourse import mybir

F32 = mybir.dt.float32
BF16 = mybir.dt.bfloat16
ALU = mybir.AluOpType
ACT = mybir.ActivationFunctionType
AX = mybir.AxisListType.X

P = 128
B, S, D = 32, 256, 256
KEYS = 120
HEADS, DK = 16, 16
NB = 2
G = B // NB
T = NB * S
NT = T // P
DC = D // P
HC = HEADS // DC
DV = DK + 1
INNER, STATES, TAPS = 512, 16, 4
IC = INNER // P
PAD = TAPS - 1
EXPERTS = 8
RFS = 256
EPS = 1e-5
RING = 8


def scan_plan():
    plan = []
    for c in range(IC + 1):
        if c < IC:
            plan.append(("scan", c, 0))
        if c:
            plan.append(("add", c - 1, STATES - 1))
        if c < IC:
            plan.append(("scan", c, 1))
        if c:
            plan.append(("mul", c - 1, 0))
        if c < IC:
            plan.append(("scan", c, 2))
        if c:
            plan.append(("out", c - 1, 0))
        if c < IC:
            plan.append(("add", c, 1))
            for n in range(3, STATES):
                plan += [("scan", c, n), ("add", c, n - 1)]
    return plan


PLAN = scan_plan()
AFTER = {step: k + 1 for k, step in enumerate(PLAN)}

COLUMNS = {}
for _name, _n in [("xis", DC), ("bq", DC), ("bk", DC), ("cn_b1", 2), ("cn_b2", 1), ("cn_b3", 1), ("cn_b4", 1),
                  ("gc_b1", 1), ("gc_b2", 1), ("gc_b3", 1), ("range", 1), ("sign", 1), ("conv_w", IC * TAPS),
                  ("conv_b", IC), ("D", IC), ("A_log", IC * STATES), ("head_mask", HC)]:
    COLUMNS[_name] = (sum(n for _, n in COLUMNS.values()), _n)
N_COLUMNS = sum(n for _, n in COLUMNS.values())
ROWS = {}
for _name, _n in [("xis", RFS), ("bv", D), ("bo", D), ("router_b", EXPERTS), ("rank", EXPERTS)]:
    ROWS[_name] = (sum(n for _, n in ROWS.values()), _n)
N_ROWS = sum(n for _, n in ROWS.values())

WEIGHTS = {
    "projT": (P, DC * RFS), "rfwT": (P, DC * D),
    "wq": (P, DC * D), "wk": (P, DC * D), "wv": (P, DC * D), "wo": (P, DC * D),
    "cn_w1": (P, DC * 256), "cn_w2": (P, DC * 128), "cn_w3": (P, 64), "cn_w4": (64, P),
    "gc_w1": (P, DC * 128), "gc_w2": (P, 64), "gc_w3": (64, P),
    "winT": (P, DC * 2 * INNER), "woutT": (P, IC * D),
    "router_w": (P, DC * EXPERTS), "expert_w": (P, DC * EXPERTS * D), "expert_b": (EXPERTS, D),
    "columns": (P, N_COLUMNS), "rows": (P, N_ROWS), "ident": (P, P),
}


class Signal:

    def __init__(self, sem, per, head=0):
        self.sem, self.per, self.head = sem, per, head

    def at(self, g, n):
        i, ahead = g if isinstance(g, tuple) else (0, g)
        return i * self.per + (ahead * self.per + n + self.head)

    def start_ahead(self, eng):
        eng.sem_inc(self.sem, self.head)


class Chain(Signal):

    def start(self, eng, g):
        self.eng, self.g, self.n = eng, g, 0

    def then(self, ins):
        self.n += 1
        return ins.then_inc(self.sem, 1)

    def settle(self, behind=0):
        self.eng.wait_ge(self.sem, self.at(self.g, self.n - behind))

    def link(self, ins):
        self.then(ins)
        self.settle()

    def end(self):
        assert self.n == self.per, (self.n, self.per)


def program(nc, ins, out):
    nc.disable_value_cache = True
    with ExitStack() as ctx:
        def sb(name, shape, dt=F32):
            return ctx.enter_context(nc.sbuf_tensor(name, shape, dt))

        def sem(name, per=1, head=0):
            return Signal(ctx.enter_context(nc.semaphore(name)), per, head)

        def chain(name, per):
            return Chain(ctx.enter_context(nc.semaphore(name)), per)

        bank = [ctx.enter_context(nc.psum_tensor(f"bank{i}", [P, 512], F32)) for i in range(8)]

        W = {name: sb("w_" + name, list(shape)) for name, shape in WEIGHTS.items()}

        def col(name, k=0, rows=P):
            at = COLUMNS[name][0] + k
            return W["columns"][0:rows, at:at + 1]

        def row(name):
            at, n = ROWS[name]
            return W["rows"][:, at:at + n]

        def chunks(name, k):
            return W[name][:, :].rearrange("p (k n) -> p k n", k=k)

        projT, rfwT = chunks("projT", DC), chunks("rfwT", DC)
        wq, wk, wv, wo = (chunks(n, DC) for n in ("wq", "wk", "wv", "wo"))
        cn_w1, cn_w2, gc_w1 = (chunks(n, DC) for n in ("cn_w1", "cn_w2", "gc_w1"))
        winT, woutT = chunks("winT", DC), chunks("woutT", IC)
        router_w, expert_w = chunks("router_w", DC), chunks("expert_w", DC)
        ident = W["ident"]

        rf_scaled = projT
        rf_norm = sb("rf_norm", [P, RFS])
        rf_bias = sb("rf_bias", [P, DC])
        rf_out = rfwT
        decay = sb("decay", [P, IC * STATES])
        half_b4 = sb("half_b4", [P, 1])
        half_gb3 = sb("half_gb3", [P, 1])
        gate_scale = sb("gate_scale", [P, 1])
        glob_scale = sb("glob_scale", [P, 1])
        base_sign = sb("base_sign", [P, 1])
        eps = sb("eps", [P, 1])
        head_rows = sb("head_rows16", [2 * HEADS, HEADS, KEYS], BF16)
        ident16 = sb("ident16", [P, P], BF16)

        x0 = sb("x0", [P, NT, D])
        x0T = sb("x0T", [P, DC, T])
        ctxT = sb("ctxT", [P, DC, NB * KEYS])
        sqsum = sb("sqsum", [P, T])
        feats = sb("feats", [P, DC, T])
        sq = feats
        rf_sq, rf_sqsum = feats[:, :, 0:D], sqsum[:, 0:D]
        kT = sb("kT", [P, DC, NB * KEYS])
        kmask = sb("kmask", [P, NB, DC, HC, KEYS])
        vals = sb("vals", [KEYS, NB, HEADS, DV])
        qT = sb("qT", [P, DC, T])
        smax = sb("smax", [P, NT, HEADS])
        smax_hi = sb("smax_hi", [P, NT, 2, HEADS], BF16)
        smax_rest = sb("smax_rest", [P, NT, HEADS])
        smaxT = sb("smaxT", [2 * HEADS, T], BF16)
        probs = sb("probs", [KEYS, 4, 2, S])
        wsum = sb("wsum", [P, NT, HEADS])
        ctxn = feats[:, :, :].rearrange("p c (t h d) -> p (c t) h d", t=2, h=HEADS)
        ctxnT = qT
        zsum = sb("zsum", [P, DC, NB])
        g1 = sb("g1", [P, NB])
        g2 = sb("g2", [64, NB])
        gt = sb("gt", [P, NB])
        base = sb("base", [P, NB])
        spare = kmask[:, :, :, :, :].rearrange("p b c h k -> p (b c h k)")

        def in_spare(k, n, rows=P):
            return spare[0:rows, k * NB * S:(k + n) * NB * S]

        h1 = in_spare(0, 2).rearrange("p (b r s) -> p b r s", b=NB, r=2)
        h2 = in_spare(2, 1).rearrange("p (b s) -> p b s", b=NB)
        h3 = in_spare(3, 1, 64).rearrange("p (b s) -> p b s", b=NB)
        gate = in_spare(4, 1).rearrange("p (b s) -> p b s", b=NB)
        couple = in_spare(5, 1).rearrange("p (b s) -> p b s", b=NB)
        turn = sq[:, :, :].rearrange("p c (b s) -> p c b s", b=NB)

        xpad = sb("xpad", [P, IC, NB, PAD + S])
        xc = sb("xc", [P, IC, T])
        res = sb("res", [P, IC, T])
        soft = sb("soft", [P, IC, T])
        conv = delta = soft
        xc2 = sb("xc2", [P, 2, T])
        a_ring = sb("a_ring", [P, RING, NB, S])
        state = sb("state", [P, 3, T])
        ysum = sb("ysum", [P, 2, T])
        yT = xpad[:, :, :, PAD:PAD + S]

        ctxTb = sb("ctxTb", [P, DC, NB * KEYS])
        ctxb = sb("ctxb", [KEYS, NB, D])
        ug = sb("ug", [KEYS, T])
        uu = sb("uu", [KEYS, T])
        logit = sb("logit", [P, NT, EXPERTS])
        lmax = sb("lmax", [P, NT])
        prob = sb("prob", [P, NT, EXPERTS])
        pmax = sb("pmax", [P, NT])
        psm = sb("psm", [P, NT])
        pinv = sb("pinv", [P, NT])
        pgate = sb("pgate", [P, NT])
        pick = sb("pick", [P, NT, EXPERTS])
        prank = sb("prank", [P, NT, EXPERTS])
        rmax = sb("rmax", [P, NT])
        weight = sb("weight", [P, NT, EXPERTS])
        weightT = ug[0:EXPERTS, :]

        class Norm:
            def __init__(self, name, x, xT, sum_=None):
                self.stats = sb(f"{name}_stats", [P, NT, 6])
                self.mv = sb(f"{name}_mv", [P, NT, 2])
                self.logv = sb(f"{name}_logv", [P, NT])
                self.rstd = sb(f"{name}_rstd", [P, NT])
                self.x = x
                self.sum = x if sum_ is None else sum_
                self.xT = xT
                self.sub_ready = sem(f"{name}_sub_ready", 2)
                self.sum_ready = sem(f"{name}_sum_ready", 2)
                self.var_ready = sem(f"{name}_var_ready", 1)
                self.log_ready = sem(f"{name}_log_ready", 1)
                self.rstd_ready = sem(f"{name}_rstd_ready", 1)
                self.x_ready = sem(f"{name}_x_ready", NT)
                if xT is not None:
                    self.turned = sem(f"{name}_turned", DC)
                    self.xT_ready = sem(f"{name}_xT_ready", DC)
                self.chain = chain(f"{name}_chain", NT)

        sum3 = in_spare(0, 2).rearrange("p (t d) -> p t d", t=NT)
        x12, x3, x45, x6 = (sb(n, [P, NT, D]) for n in ("x12", "x3", "x45", "x6"))
        x12T, x3T, x45T = (sb(n, [P, DC, T]) for n in ("x12T", "x3T", "x45T"))
        n1, n2, n3 = Norm("ln1", x12, x12T), Norm("ln2", x12, x12T), Norm("ln3", x3, x3T, sum3)
        n4, n5, n6 = Norm("ln4", x45, x45T), Norm("ln5", x45, x45T), Norm("ln6", x6, None)
        x1b, acc = x12, x6

        loaded_w = sem("loaded_w")
        loaded_x = sem("loaded_x", 3 * 16)
        loaded_ctx = sem("loaded_ctx", 2 * 16)
        stored = sem("stored", 16, 1)
        const_v = chain("const_v", 10 + RING)
        const_v2 = sem("const_v2")
        const_a = sem("const_a")
        const_p = sem("const_p")
        const_t = sem("const_t")

        held = sem("held")
        sq_chain = chain("sq_chain", 2)
        sqsum_ready = sem("sqsum_ready", 1)
        dots_ready = sem("dots_ready", DC, 1)
        feats_ready = sem("feats_ready", DC)

        kT_psum = sem("kT_psum", 1)
        v_psum = sem("v_psum", 1)
        q_psum = sem("q_psum", DC)
        kT_ready = sem("kT_ready", DC)
        qT_ready = sem("qT_ready", DC)
        vals_ready = sem("vals_ready", NB)
        kmask_ready = sem("kmask_ready", NB * DC)
        scores_ready = sem("scores_ready", NT * DC)
        smax_ready = sem("smax_ready", NT * DC)
        hi_chain = chain("hi_chain", 2)
        hi_ready = sem("hi_ready", 1)
        smaxT_psum = sem("smaxT_psum", 1)
        smaxT_ready = sem("smaxT_ready", 1)
        logits_ready = sem("logits_ready", NB * HEADS // 2)
        probs_ready = sem("probs_ready", NB * HEADS // 2)
        pv_ready = sem("pv_ready", NB * HEADS // 2)
        att_chain = chain("att_chain", NT)
        ctxn_ready = sem("ctxn_ready", NT)
        ctxn_turned = sem("ctxn_turned", DC)
        ctxnT_ready = sem("ctxnT_ready", DC)
        x1b_ready = sem("x1b_ready", 1)

        zsum_ready = sem("zsum_ready", DC)
        glob_psum = sem("glob_psum", 3)
        glob_ready = sem("glob_ready", 3)
        base_ready = sem("base_ready", 1)
        CYC = 3 * NB
        l1_psum = sem("l1_psum", CYC)
        l1_ready = sem("l1_ready", 2 * CYC)
        l2_psum = sem("l2_psum", CYC)
        l2_ready = sem("l2_ready", CYC)
        l3_psum = sem("l3_psum", CYC)
        l3_ready = sem("l3_ready", CYC)
        l4_psum = sem("l4_psum", CYC)
        gate_ready = sem("gate_ready", CYC)
        cyc_chain = chain("cyc_chain", 3 * CYC)
        z_ready = sem("z_ready", 2 * CYC, 1)

        in_psum = sem("in_psum", 2 * IC)
        in_read = sem("in_read", 2 * IC)
        conv_chain = chain("conv_chain", IC * (TAPS - 1))
        conv_ready = sem("conv_ready", IC)
        xc_ready = sem("xc_ready", IC)
        exp_ready = sem("exp_ready", 1)
        soft_ready = sem("soft_ready", 1)
        xc2_ready = sem("xc2_ready", IC)
        delta_ready = sem("delta_ready", IC)
        STEPS = IC * STATES
        decay_ready = sem("decay_ready", STEPS)
        scanned = chain("scanned", len(PLAN))

        u_psum = sem("u_psum", 1)
        ug_ready = sem("ug_ready", 1)
        uu_ready = sem("uu_ready", 1)
        router_psum = sem("router_psum", 1)
        logit_chain = chain("logit_chain", 2)
        logit_ready = sem("logit_ready", 1)
        prob_ready = sem("prob_ready", 1)
        pick_chain = chain("pick_chain", 8)
        weight_ready = sem("weight_ready", 1)
        weight_turned = sem("weight_turned", 1)
        weightT_ready = sem("weightT_ready", 1)
        bias_ready = sem("bias_ready", 2)
        MOE = NT * EXPERTS // 2
        expert_ready = sem("expert_ready", MOE)
        acc_start = sem("acc_start", 2)
        expert_added = sem("expert_added", 2 * MOE, 1)

        def norm_add(v, n, g, parts):
            for half, (sub, resid) in enumerate(parts):
                v.wait_ge(n.sub_ready.sem, n.sub_ready.at(g, half + 1))
                v.tensor_tensor(out=n.sum[:, 2 * half:2 * half + 2, :], in0=sub, in1=resid,
                                op=ALU.add).then_inc(n.sum_ready.sem, 1)

        def norm_stats(v, n, g):
            n.chain.start(v, g)
            for t in range(NT):
                v.wait_ge(n.sum_ready.sem, n.sum_ready.at(g, t // 2 + 1))
                n.chain.then(v.bn_stats(n.stats[:, t, :], n.sum[:, t, :]))
            n.chain.settle()
            v.sem_inc(held.sem, 1)
            for t in range(NT):
                last = v.bn_aggr(n.mv[:, t, :], n.stats[:, t, :])
            last.then_inc(n.var_ready.sem, 1)
            n.chain.end()

        def norm_rstd(a, n, g):
            a.wait_ge(n.var_ready.sem, n.var_ready.at(g, 1))
            a.activation(n.logv[:, :], n.mv[:, :, 1], ACT.Ln, bias=eps[:, :]).then_inc(n.log_ready.sem, 1)
            a.wait_ge(n.log_ready.sem, n.log_ready.at(g, 1))
            a.activation(n.rstd[:, :], n.logv[:, :], ACT.Exp, scale=-0.5).then_inc(n.rstd_ready.sem, 1)

        def norm_apply(v, n, g):
            v.wait_ge(n.rstd_ready.sem, n.rstd_ready.at(g, 1))
            for t in range(NT):
                v.tensor_scalar(n.x[:, t, :], n.sum[:, t, :], n.mv[:, t, 0:1], n.rstd[:, t:t + 1],
                                ALU.subtract, ALU.mult).then_inc(n.x_ready.sem, 1)

        def norm_turn(pe, n, g, banks):
            for c in range(DC):
                for t in range(NT):
                    pe.wait_ge(n.x_ready.sem, n.x_ready.at(g, t + 1))
                    last = pe.transpose(banks[c][:, t * P:(t + 1) * P], n.x[:, t, c * P:(c + 1) * P], ident[:, :])
                last.then_inc(n.turned.sem, 1)

        def norm_copy(a, n, g, banks):
            for c in range(DC):
                a.wait_ge(n.turned.sem, n.turned.at(g, c + 1))
                a.copy(n.xT[:, c, :], banks[c][:, :]).then_inc(n.xT_ready.sem, 1)

        def tiles(bank_, half=None):
            return bank_[:, :].rearrange("p (t d) -> p t d", t=2)

        OUT = [bank[2], bank[3]]
        TURN = [bank[4], bank[5]]
        MB = [bank[6], bank[7]]

        def added_after(s):
            return 4 * (s // 2) + 3 + s % 2

        block = ctx.enter_context(nc.Block())

        @block.sync
        def _(sp):
            for name in W:
                sp.dma_start(W[name][:, :], ins[name]).then_inc(loaded_w.sem, 16)
            sp.dma_start(head_rows[:, :, :], ins["head_rows"]).then_inc(loaded_w.sem, 16)

            def at(tensor, g):
                return tensor[g[0] + g[1]] if isinstance(g, tuple) else tensor[g]

            def load_front(g):
                sp.dma_start(x0T[:, :, :], at(ins["xT"], g)).then_inc(loaded_x.sem, 16)
                sp.dma_start(x0[:, :, :], at(ins["x"], g)).then_inc(loaded_x.sem, 16)
                sp.dma_start(ctxT[:, :, :], at(ins["ctxT"], g)).then_inc(loaded_x.sem, 16)

            def load_back(g):
                sp.dma_start(ctxTb[:, :, :], at(ins["ctxT"], g)).then_inc(loaded_ctx.sem, 16)
                sp.dma_start(ctxb[:, :, :], at(ins["ctx"], g)).then_inc(loaded_ctx.sem, 16)

            def front_free(g):
                sp.wait_ge(n1.sum_ready.sem, n1.sum_ready.at(g, 2))
                sp.sem_inc(held.sem, 1)
                sp.wait_ge(v_psum.sem, v_psum.at(g, 1))
                sp.sem_inc(held.sem, 1)
                sp.wait_ge(kT_psum.sem, kT_psum.at(g, 1))
                sp.sem_inc(held.sem, 1)

            def back_free(g):
                sp.wait_ge(n5.sub_ready.sem, n5.sub_ready.at(g, 2))
                sp.sem_inc(held.sem, 1)

            def store(g):
                sp.wait_ge(n6.x_ready.sem, n6.x_ready.at(g, NT))
                sp.sem_inc(held.sem, 1)
                sp.dma_start(at(out, g), n6.x[:, :, :]).then_inc(stored.sem, 16)

            stored.start_ahead(sp)
            load_front(0)
            load_back(0)
            front_free(0)
            load_front(1)
            with sp.Fori(0, G - 2) as i:
                front_free((i, 1))
                load_front((i, 2))
                back_free((i, 0))
                load_back((i, 1))
                store((i, 0))
            back_free(G - 2)
            load_back(G - 1)
            store(G - 2)
            store(G - 1)
            sp.wait_ge(stored.sem, stored.at(G, 0))

        @block.tensor
        def _(pe):
            def mm(o, l, r, start, stop):
                return pe.matmul(o, l, r, start=start, stop=stop)

            def setup():
                pe.wait_ge(loaded_w.sem, 16 * (len(W) + 1))
                pe.wait_ge(const_v.sem, const_v.per)
                pe.wait_ge(const_p.sem, 3)
                for r in range(DC):
                    for c in range(DC):
                        mm(bank[r][:, 0:D], rf_scaled[:, c, r * P:(r + 1) * P], rfwT[:, c, :], c == 0, False)
                    mm(bank[r][:, 0:D], rf_norm[:, r * P:(r + 1) * P], rf_sqsum[:, :], False, True)\
                        .then_inc(const_t.sem, 1)

            def rfs(g):
                pe.wait_ge(loaded_x.sem, loaded_x.at(g, 48))
                pe.wait_ge(sqsum_ready.sem, sqsum_ready.at(g, 1))
                for r in range(DC):
                    for c in range(DC):
                        mm(bank[r][:, :], rf_scaled[:, c, r * P:(r + 1) * P], x0T[:, c, :], c == 0, False)
                    mm(bank[r][:, :], rf_norm[:, r * P:(r + 1) * P], sqsum[:, :], False, True)\
                        .then_inc(dots_ready.sem, 1)

            def project(g, n, ready, lhsT, rhs, k, banks, wait_each=None):
                if wait_each is None:
                    pe.wait_ge(ready.sem, ready.at(g, ready.per))
                for t in range(NT):
                    for c in range(k):
                        last = mm(banks[t // 2][:, t % 2 * D:t % 2 * D + D], lhsT[:, c, t * P:(t + 1) * P],
                                  rhs[:, c, :], c == 0, c == k - 1)
                    if t % 2:
                        last.then_inc(n.sub_ready.sem, 1)

            def key_values(g):
                pe.wait_ge(feats_ready.sem, feats_ready.at(g, DC))
                for e in range(DC):
                    for c in range(DC):
                        last = mm(bank[0][:, e * 240:(e + 1) * 240], wk[:, c, e * P:(e + 1) * P], ctxT[:, c, :],
                                  c == 0, c == DC - 1)
                last.then_inc(kT_psum.sem, 1)
                for b in range(NB):
                    for c in range(DC):
                        last = mm(bank[1][0:KEYS, b * D:(b + 1) * D], ctxT[:, c, b * KEYS:(b + 1) * KEYS],
                                  wv[:, c, :], c == 0, c == DC - 1)
                last.then_inc(v_psum.sem, 1)

            def queries(g):
                pe.wait_ge(n1.xT_ready.sem, n1.xT_ready.at(g, DC))
                pe.wait_ge(n1.sum_ready.sem, n1.sum_ready.at(g, 2))
                for e in range(DC):
                    for c in range(DC):
                        last = mm(bank[2 + e][:, :], wq[:, c, e * P:(e + 1) * P], n1.xT[:, c, :], c == 0, c == DC - 1)
                    last.then_inc(q_psum.sem, 1)

            def scores(g, s0, s1):
                pe.wait_ge(vals_ready.sem, vals_ready.at(g, NB))
                for s in range(s0, s1):
                    t, e = divmod(s, DC)
                    pair = s % 2
                    pe.wait_ge(qT_ready.sem, qT_ready.at(g, DC))
                    pe.wait_ge(kmask_ready.sem, kmask_ready.at(g, (t // 2 + 1) * DC))
                    if s >= 2:
                        pe.wait_ge(smax_ready.sem, smax_ready.at(g, s - 1))
                    for half in range(2):
                        last = mm(bank[2 * pair + half][:, 0:480], qT[:, e, t * P:(t + 1) * P],
                                  kmask[:, t // 2, e, 4 * half:4 * half + 4, :], True, True)
                    last.then_inc(scores_ready.sem, 1)

            def turn_maxima(g):
                pe.wait_ge(hi_ready.sem, hi_ready.at(g, 1))
                pe.wait_ge(n1.xT_ready.sem, n1.xT_ready.at(g, DC))
                smaxT_bank = bank[4][0:2 * HEADS, 0:T // 2].bitcast(BF16)
                for t in range(NT):
                    last = pe.transpose(smaxT_bank[:, t * P:(t + 1) * P],
                                        smax_hi[:, t, :, :].rearrange("p a h -> p (a h)"), ident16[:, :])
                last.then_inc(smaxT_psum.sem, 1)

            def weigh(g, s):
                b, pair = divmod(s, HEADS // 2)
                if s == 0:
                    pe.wait_ge(smaxT_ready.sem, smaxT_ready.at(g, 1))
                if s >= 4:
                    pe.wait_ge(probs_ready.sem, probs_ready.at(g, s - 3))
                for k in range(2):
                    h = 2 * pair + k
                    dst = bank[s % 4][0:KEYS, k * S:(k + 1) * S]
                    mm(dst, kmask[:, b, h // HC, h % HC, :], qT[:, h // HC, b * S:(b + 1) * S], True, False)
                    last = mm(dst, head_rows[:, h, :], smaxT[:, b * S:(b + 1) * S], False, True)
                last.then_inc(logits_ready.sem, 1)

            def mix(g, s):
                b, pair = divmod(s, HEADS // 2)
                pe.wait_ge(probs_ready.sem, probs_ready.at(g, s + 1))
                if pair == 0 and b:
                    pe.wait_ge(ctxn_ready.sem, ctxn_ready.at(g, 2 * b))
                for q in range(2):
                    for k in range(2):
                        h = 2 * pair + k
                        last = mm(bank[4 + q][:, h * DV:(h + 1) * DV], probs[:, s % 4, k, q * P:(q + 1) * P],
                                  vals[:, b, h, :], True, True)
                last.then_inc(pv_ready.sem, 1)

            def attend(g, s0, s1):
                for s in range(s0, s1):
                    if s < NB * HEADS // 2:
                        weigh(g, s)
                    if s >= 2:
                        mix(g, s - 2)

            def output(g):
                pe.wait_ge(probs_ready.sem, probs_ready.at(g, NB * HEADS // 2))
                for c in range(DC):
                    for t in range(NT):
                        pe.wait_ge(ctxn_ready.sem, ctxn_ready.at(g, t + 1))
                        last = pe.transpose(bank[c][:, t * P:(t + 1) * P],
                                            ctxn[:, t, c * HC:(c + 1) * HC, :].rearrange("p h d -> p (h d)"),
                                            ident[:, :])
                    last.then_inc(ctxn_turned.sem, 1)
                project(g, n2, ctxnT_ready, ctxnT, wo, DC, OUT)

            def glob(g):
                z = bank[0]
                pe.wait_ge(zsum_ready.sem, zsum_ready.at(g, DC))
                for c in range(DC):
                    last = mm(z[:, 0:NB], gc_w1[:, c, :], zsum[:, c, :], c == 0, c == DC - 1)
                last.then_inc(glob_psum.sem, 1)
                pe.wait_ge(glob_ready.sem, glob_ready.at(g, 1))
                mm(z[0:64, NB:2 * NB], W["gc_w2"][:, :], g1[:, :], True, True).then_inc(glob_psum.sem, 1)
                pe.wait_ge(glob_ready.sem, glob_ready.at(g, 2))
                mm(z[:, 2 * NB:3 * NB], W["gc_w3"][:, :], g2[:, :], True, True).then_inc(glob_psum.sem, 1)

            def layer(g, n, s):
                b = s % NB
                if n == 1:
                    if s >= NB:
                        pe.wait_ge(z_ready.sem, z_ready.at(g, 2 * (s - NB) + 2))
                    elif s == 0:
                        pe.wait_ge(glob_ready.sem, glob_ready.at(g, 3))
                        pe.wait_ge(n2.xT_ready.sem, n2.xT_ready.at(g, DC))
                    for r in range(2):
                        for c in range(DC):
                            last = mm(bank[b][:, r * S:(r + 1) * S], cn_w1[:, c, r * P:(r + 1) * P],
                                      n2.xT[:, c, b * S:(b + 1) * S], c == 0, c == DC - 1)
                    last.then_inc(l1_psum.sem, 1)
                elif n == 2:
                    pe.wait_ge(l1_ready.sem, l1_ready.at(g, 2 * s + 2))
                    if s < NB:
                        pe.wait_ge(n2.sum_ready.sem, n2.sum_ready.at(g, 2))
                    for c in range(2):
                        last = mm(bank[2 + b][:, 0:S], cn_w2[:, c, :], h1[:, b, c, :], c == 0, c == 1)
                    last.then_inc(l2_psum.sem, 1)
                elif n == 3:
                    pe.wait_ge(l2_ready.sem, l2_ready.at(g, s + 1))
                    mm(bank[2 + b][0:64, S:2 * S], W["cn_w3"][:, :], h2[:, b, :], True, True)\
                        .then_inc(l3_psum.sem, 1)
                else:
                    pe.wait_ge(l3_ready.sem, l3_ready.at(g, s + 1))
                    mm(bank[4 + b][:, 0:S], W["cn_w4"][:, :], h3[:, b, :], True, True).then_inc(l4_psum.sem, 1)

            def rotate_back(g):
                for t in range(NT):
                    pe.wait_ge(z_ready.sem, z_ready.at(g, 2 * (CYC - NB) + 2 * (t // 2) + 2))
                    for c in range(DC):
                        last = pe.transpose(OUT[t // 2][:, t % 2 * D + c * P:t % 2 * D + (c + 1) * P],
                                            n2.xT[:, c, t * P:(t + 1) * P], ident[:, :])
                    if t % 2:
                        last.then_inc(n3.sub_ready.sem, 1)

            def mamba_in(g, b):
                pe.wait_ge(n3.xT_ready.sem, n3.xT_ready.at(g, DC))
                if b is not None:
                    pe.wait_ge(uu_ready.sem, uu_ready.at(b, 1))
                for j in range(2 * IC):
                    if j >= 2:
                        pe.wait_ge(in_read.sem, in_read.at(g, j - 1))
                    for c in range(DC):
                        last = mm(MB[j % 2][:, :], winT[:, c, j * P:(j + 1) * P], n3.xT[:, c, :], c == 0, c == DC - 1)
                    last.then_inc(in_psum.sem, 1)

            def mamba_out(g):
                for t in range(NT):
                    for c in range(IC):
                        if t == 0:
                            pe.wait_ge(scanned.sem, scanned.at(g, AFTER["out", c, 0]))
                        last = mm(MB[t // 2][:, t % 2 * D:t % 2 * D + D], yT[:, c, t // 2, t % 2 * P:t % 2 * P + P],
                                  woutT[:, c, :], c == 0, c == IC - 1)
                    if t % 2:
                        last.then_inc(n4.sub_ready.sem, 1)

            def gated_in(g):
                pe.wait_ge(n4.xT_ready.sem, n4.xT_ready.at(g, DC))
                pe.wait_ge(loaded_ctx.sem, loaded_ctx.at(g, 32))
                for b in range(NB):
                    for c in range(DC):
                        last = mm(MB[0][0:KEYS, b * S:(b + 1) * S], ctxTb[:, c, b * KEYS:(b + 1) * KEYS],
                                  n4.xT[:, c, b * S:(b + 1) * S], c == 0, c == DC - 1)
                last.then_inc(u_psum.sem, 1)

            def gated_out(g, m):
                if m is not None:
                    pe.wait_ge(in_read.sem, in_read.at(m, 2 * IC))
                pe.wait_ge(uu_ready.sem, uu_ready.at(g, 1))
                for t in range(NT):
                    last = mm(MB[t // 2][:, t % 2 * D:t % 2 * D + D], uu[:, t * P:(t + 1) * P],
                              ctxb[:, t // 2, :], True, True)
                    if t % 2:
                        last.then_inc(n5.sub_ready.sem, 1)

            def router(g):
                pe.wait_ge(n5.xT_ready.sem, n5.xT_ready.at(g, DC))
                for t in range(NT):
                    for c in range(DC):
                        last = mm(MB[0][:, t * EXPERTS:(t + 1) * EXPERTS], n5.xT[:, c, t * P:(t + 1) * P],
                                  router_w[:, c, :], c == 0, c == DC - 1)
                last.then_inc(router_psum.sem, 1)

            def expert_bias(g):
                pe.wait_ge(weight_ready.sem, weight_ready.at(g, 1))
                for t in range(NT):
                    last = pe.transpose(MB[1][0:EXPERTS, t * P:(t + 1) * P], weight[:, t, :], ident[:, :])
                last.then_inc(weight_turned.sem, 1)
                pe.wait_ge(weightT_ready.sem, weightT_ready.at(g, 1))
                for t in range(NT):
                    last = mm(MB[t // 2][:, t % 2 * D:t % 2 * D + D], weightT[:, t * P:(t + 1) * P],
                              W["expert_b"][:, :], True, True)
                    if t % 2:
                        last.then_inc(bias_ready.sem, 1)

            def experts(g, s0, s1):
                for s in range(s0, s1):
                    pair, t = s // NT, s % NT
                    if s >= 2:
                        pe.wait_ge(expert_added.sem, expert_added.at(g, added_after(s - 2)))
                    else:
                        pe.wait_ge(acc_start.sem, acc_start.at(g, 2))
                    for c in range(DC):
                        last = mm(MB[s % 2][:, :], n5.xT[:, c, t * P:(t + 1) * P],
                                  expert_w[:, c, pair * 2 * D:(pair + 1) * 2 * D], c == 0, c == DC - 1)
                    last.then_inc(expert_ready.sem, 1)

            def turn(f, m, b):
                if b is not None:
                    gated_in(b)
                if m is not None:
                    mamba_in(m, b)
                if b is not None:
                    gated_out(b, m)
                if f is not None:
                    rfs(f)
                    project(f, n1, feats_ready, feats, rf_out, DC, OUT)
                    key_values(f)
                if b is not None:
                    norm_turn(pe, n5, b, MB)
                    router(b)
                if f is not None:
                    norm_turn(pe, n1, f, TURN)
                    queries(f)
                if b is not None:
                    expert_bias(b)
                for k in range(4):
                    if f is not None:
                        scores(f, 2 * k, 2 * k + 2)
                    if b is not None:
                        experts(b, k, k + 1)
                if f is not None:
                    turn_maxima(f)
                if f is not None:
                    attend(f, 0, NB * HEADS // 2 + 2)
                    output(f)
                if b is not None:
                    experts(b, 4, 8)
                if f is not None:
                    norm_turn(pe, n2, f, TURN)
                if b is not None:
                    experts(b, 8, 10)
                if f is not None:
                    glob(f)
                for s in range(CYC):
                    if f is not None:
                        layer(f, 1, s)
                        if s:
                            layer(f, 4, s - 1)
                    if b is not None:
                        experts(b, 10 + s, 11 + s)
                    if f is not None:
                        layer(f, 2, s)
                        layer(f, 3, s)
                if f is not None:
                    layer(f, 4, CYC - 1)
                    rotate_back(f)
                if m is not None:
                    if b is not None:
                        pe.wait_ge(expert_added.sem, expert_added.at(b, 2 * MOE))
                    mamba_out(m)
                if f is not None:
                    norm_turn(pe, n3, f, TURN)
                if m is not None:
                    norm_turn(pe, n4, m, [bank[0], bank[1]])

            setup()
            dots_ready.start_ahead(pe)
            pe.wait_ge(const_a.sem, 4)
            turn(0, None, None)
            turn(1, 0, None)
            with pe.Fori(0, G - 2) as i:
                turn((i, 2), (i, 1), (i, 0))
            turn(None, G - 1, G - 2)
            turn(None, None, G - 1)

        @block.vector
        def _(v):
            def setup():
                const_v.start(v, 0)
                for k in range(RING):
                    const_v.then(v.memset(a_ring[:, k, :, 0:1], 0.0))
                const_v.then(v.memset(xpad[:, :, :, 0:PAD], 0.0))
                const_v.then(v.memset(vals[:, :, :, DK:DV], 1.0))
                const_v.then(v.memset(eps[:, :], EPS))
                v.wait_ge(loaded_w.sem, 16 * (len(W) + 1))
                for c in range(DC):
                    const_v.then(v.tensor_tensor(out=rf_scaled[:, c, :], in0=rf_scaled[:, c, :], in1=row("xis"),
                                                 op=ALU.mult))
                const_v.link(v.tensor_tensor(out=rf_norm[:, :], in0=row("xis"), in1=row("xis"), op=ALU.mult))
                const_v.then(v.tensor_scalar(rf_norm[:, :], rf_norm[:, :], -0.5, None, ALU.mult))
                at = COLUMNS["xis"][0]
                const_v.then(v.tensor_scalar(rf_bias[:, :], W["columns"][:, at:at + DC], -0.5 * float(np.log(RFS)),
                                             None, ALU.add))
                const_v.then(v.tensor_copy(ident16[:, :], ident[:, :]))
                const_v.then(v.tensor_scalar(half_b4[:, :], col("cn_b4"), 0.5, None, ALU.mult))
                const_v.end()
                v.tensor_scalar(half_gb3[:, :], col("gc_b3"), 0.5, None, ALU.mult).then_inc(const_v2.sem, 1)
                v.tensor_scalar(gate_scale[:, :], col("range"), 0.3, col("sign"), ALU.mult, ALU.mult)\
                    .then_inc(const_v2.sem, 1)
                v.tensor_scalar(glob_scale[:, :], col("range"), 0.7, col("sign"), ALU.mult, ALU.mult)\
                    .then_inc(const_v2.sem, 1)
                v.tensor_scalar(base_sign[:, :], col("sign"), 0.1, None, ALU.mult).then_inc(const_v2.sem, 1)
                v.wait_ge(const_a.sem, 1)
                v.tensor_scalar(decay[:, :], decay[:, :], -1.0, None, ALU.mult).then_inc(const_v2.sem, 1)
                v.wait_ge(const_v2.sem, 5)

            def ln1_sum(g):
                v.wait_ge(loaded_x.sem, loaded_x.at(g, 48))
                norm_add(v, n1, g, [(tiles(OUT[h]), x0[:, 2 * h:2 * h + 2, :]) for h in range(2)])
                norm_stats(v, n1, g)

            def values(g):
                v.wait_ge(v_psum.sem, v_psum.at(g, 1))
                for b in range(NB):
                    v.tensor_tensor(out=vals[:, b, :, 0:DK],
                                    in0=bank[1][0:KEYS, b * D:(b + 1) * D].rearrange("p (h d) -> p h d", h=HEADS),
                                    in1=row("bv")[0:KEYS, :].rearrange("p (h d) -> p h d", h=HEADS),
                                    op=ALU.add).then_inc(vals_ready.sem, 1)

            def maxima(g, s0, s1):
                for s in range(s0, s1):
                    t, e = divmod(s, DC)
                    v.wait_ge(scores_ready.sem, scores_ready.at(g, s + 1))
                    for half in range(2):
                        h0 = e * HC + 4 * half
                        last = v.tensor_reduce(smax[:, t, h0:h0 + 4],
                                               bank[2 * (s % 2) + half][:, 0:480].rearrange("p (h k) -> p h k", h=4),
                                               AX, ALU.max)
                    last.then_inc(smax_ready.sem, 1)

            def negate_maxima(g):
                v.wait_ge(smax_ready.sem, smax_ready.at(g, NT * DC))
                hi_chain.start(v, g)
                hi_chain.link(v.tensor_scalar(smax_hi[:, :, 0, :], smax[:, :, :], -1.0, None, ALU.mult))
                hi_chain.link(v.scalar_tensor_tensor(out=smax_rest[:, :, :], in0=smax[:, :, :], scalar=-1.0,
                                                     in1=smax_hi[:, :, 0, :], op0=ALU.mult, op1=ALU.subtract))
                hi_chain.end()
                v.tensor_copy(smax_hi[:, :, 1, :], smax_rest[:, :, :]).then_inc(hi_ready.sem, 1)

            def copy_maxima(g):
                v.wait_ge(smaxT_psum.sem, smaxT_psum.at(g, 1))
                v.tensor_copy(smaxT[:, :], bank[4][0:2 * HEADS, 0:T // 2].bitcast(BF16)).then_inc(smaxT_ready.sem, 1)

            def normalize_context(g, b):
                v.wait_ge(pv_ready.sem, pv_ready.at(g, (b + 1) * HEADS // 2))
                for q in range(2):
                    t = 2 * b + q
                    o = bank[4 + q][:, 0:HEADS * DV].rearrange("p (h d) -> p h d", h=HEADS)
                    att_chain.then(v.reciprocal(wsum[:, t, :], o[:, :, DK]))
                for q in range(2):
                    t = 2 * b + q
                    o = bank[4 + q][:, 0:HEADS * DV].rearrange("p (h d) -> p h d", h=HEADS)
                    v.wait_ge(att_chain.sem, att_chain.at(g, t + 1))
                    v.tensor_tensor(out=ctxn[:, t, :, :], in0=o[:, :, 0:DK],
                                    in1=wsum[:, t, :].unsqueeze(2).to_broadcast([P, HEADS, DK]),
                                    op=ALU.mult).then_inc(ctxn_ready.sem, 1)

            def ln2_sum(g):
                v.wait_ge(x1b_ready.sem, x1b_ready.at(g, 1))
                norm_add(v, n2, g, [(tiles(OUT[h]), x1b[:, 2 * h:2 * h + 2, :]) for h in range(2)])
                norm_stats(v, n2, g)

            def sequence_sums(g):
                for c in range(DC):
                    v.wait_ge(n2.xT_ready.sem, n2.xT_ready.at(g, c + 1))
                    v.tensor_reduce(zsum[:, c, :], n2.xT[:, c, :].rearrange("p (b s) -> p b s", b=NB), AX, ALU.add)\
                        .then_inc(zsum_ready.sem, 1)

            def global_base(g):
                v.wait_ge(glob_ready.sem, glob_ready.at(g, 3))
                v.tensor_scalar(base[:, :], gt[:, :], glob_scale[:, :], base_sign[:, :], ALU.mult, ALU.add)\
                    .then_inc(base_ready.sem, 1)
                cyc_chain.start(v, g)

            def rotate(g, s):
                b = s % NB
                z0 = n2.xT[:, 0, b * S:(b + 1) * S]
                z1 = n2.xT[:, 1, b * S:(b + 1) * S]
                if s == 0:
                    v.wait_ge(base_ready.sem, base_ready.at(g, 1))
                v.wait_ge(gate_ready.sem, gate_ready.at(g, s + 1))
                cyc_chain.link(v.tensor_scalar(couple[:, b, :], gate[:, b, :], gate_scale[:, :], base[:, b:b + 1],
                                               ALU.mult, ALU.add))
                cyc_chain.then(v.tensor_tensor(out=turn[:, 0, b, :], in0=couple[:, b, :], in1=z1, op=ALU.mult))
                cyc_chain.link(v.tensor_tensor(out=turn[:, 1, b, :], in0=couple[:, b, :], in1=z0, op=ALU.mult))
                v.tensor_tensor(out=z0, in0=z0, in1=turn[:, 0, b, :], op=ALU.add).then_inc(z_ready.sem, 1)
                v.tensor_tensor(out=z1, in0=z1, in1=turn[:, 1, b, :], op=ALU.subtract).then_inc(z_ready.sem, 1)
                if s == CYC - 1:
                    cyc_chain.end()

            def ln3_sum(g):
                norm_add(v, n3, g, [(tiles(OUT[h]), n2.x[:, 2 * h:2 * h + 2, :]) for h in range(2)])
                norm_stats(v, n3, g)

            def convolve(g):
                conv_chain.start(v, g)
                for c0 in range(0, IC, 2):
                    v.wait_ge(in_read.sem, in_read.at(g, c0 + 2))
                    for k in range(TAPS):
                        for c in range(c0, c0 + 2):
                            o = conv[:, c, :].rearrange("p (b s) -> p b s", b=NB)
                            x = xpad[:, c, :, k:k + S]
                            w = col("conv_w", c * TAPS + k)
                            if k:
                                conv_chain.settle(1)
                            if k == 0:
                                step = v.tensor_scalar(o, x, w, None, ALU.mult)
                            else:
                                step = v.scalar_tensor_tensor(out=o, in0=x, scalar=w, in1=o, op0=ALU.mult,
                                                              op1=ALU.add)
                            if k < TAPS - 1:
                                conv_chain.then(step)
                            else:
                                step.then_inc(conv_ready.sem, 1)
                                if c == c0:
                                    conv_chain.settle()
                conv_chain.end()

            def step(g, what, c, n):
                k = c * STATES + n
                total, one = ysum[:, c % 2, :], state[:, n % 3, :]
                if what == "scan":
                    if n == 0:
                        v.wait_ge(xc2_ready.sem, xc2_ready.at(g, c + 1))
                    v.wait_ge(decay_ready.sem, decay_ready.at(g, k + 1))
                    scanned.then(v.tensor_tensor_scan(one if n else total,
                                                      a_ring[:, k % RING, :, :].rearrange("p b s -> p (b s)"),
                                                      xc2[:, c % 2, :], 0.0, ALU.mult, ALU.add))
                    return
                scanned.settle(0 if scanned.n >= len(PLAN) - 3 else 1)
                if what == "add":
                    scanned.then(v.tensor_tensor(out=total, in0=total, in1=one, op=ALU.add))
                elif what == "mul":
                    scanned.then(v.tensor_tensor(out=total, in0=total, in1=res[:, c, :], op=ALU.mult))
                elif what == "out":
                    scanned.then(v.scalar_tensor_tensor(
                        out=yT[:, c, :, :], in0=total.rearrange("p (b s) -> p b s", b=NB), scalar=col("D", c),
                        in1=xc[:, c, :].rearrange("p (b s) -> p b s", b=NB), op0=ALU.add, op1=ALU.mult))

            def states(g, upto):
                if g is None:
                    return
                if scanned.n is None:
                    scanned.start(v, g)
                while scanned.n < upto:
                    step(g, *PLAN[scanned.n])
                if upto == len(PLAN):
                    scanned.end()
                    scanned.n = None

            def ln4_sum(g):
                norm_add(v, n4, g, [(tiles(MB[h]), n3.x[:, 2 * h:2 * h + 2, :]) for h in range(2)])
                norm_stats(v, n4, g)

            def gated(g):
                v.wait_ge(ug_ready.sem, ug_ready.at(g, 1))
                v.tensor_tensor(out=uu[:, :], in0=MB[0][0:KEYS, :], in1=ug[:, :], op=ALU.mult)\
                    .then_inc(uu_ready.sem, 1)

            def ln5_sum(g):
                norm_add(v, n5, g, [(tiles(MB[h]), n4.x[:, 2 * h:2 * h + 2, :]) for h in range(2)])
                norm_stats(v, n5, g)

            def over_experts(a):
                return a.unsqueeze(2).to_broadcast([P, NT, EXPERTS])

            def over_tiles(a):
                return a.unsqueeze(1).to_broadcast([P, NT, EXPERTS])

            def route(g):
                v.wait_ge(router_psum.sem, router_psum.at(g, 1))
                logit_chain.start(v, g)
                logit_chain.link(v.tensor_tensor(
                    out=logit[:, :, :], in0=MB[0][:, 0:NT * EXPERTS].rearrange("p (t e) -> p t e", t=NT),
                    in1=over_tiles(row("router_b")), op=ALU.add))
                logit_chain.link(v.tensor_reduce(lmax[:, :], logit[:, :, :], AX, ALU.max))
                logit_chain.end()
                v.tensor_tensor(out=logit[:, :, :], in0=logit[:, :, :], in1=over_experts(lmax[:, :]),
                                op=ALU.subtract).then_inc(logit_ready.sem, 1)

            def pick_expert(g):
                v.wait_ge(prob_ready.sem, prob_ready.at(g, 1))
                pick_chain.start(v, g)
                pick_chain.then(v.tensor_reduce(pmax[:, :], prob[:, :, :], AX, ALU.max))
                pick_chain.link(v.tensor_reduce(psm[:, :], prob[:, :, :], AX, ALU.add))
                pick_chain.then(v.reciprocal(pinv[:, :], psm[:, :]))
                pick_chain.link(v.tensor_tensor(out=pick[:, :, :], in0=prob[:, :, :], in1=over_experts(pmax[:, :]),
                                                op=ALU.is_equal))
                pick_chain.then(v.tensor_tensor(out=pgate[:, :], in0=pmax[:, :], in1=pinv[:, :], op=ALU.mult))
                pick_chain.link(v.tensor_tensor(out=prank[:, :, :], in0=pick[:, :, :], in1=over_tiles(row("rank")),
                                                op=ALU.mult))
                pick_chain.link(v.tensor_reduce(rmax[:, :], prank[:, :, :], AX, ALU.max))
                pick_chain.link(v.tensor_tensor(out=pick[:, :, :], in0=prank[:, :, :], in1=over_experts(rmax[:, :]),
                                                op=ALU.is_equal))
                pick_chain.end()
                v.tensor_tensor(out=weight[:, :, :], in0=pick[:, :, :], in1=over_experts(pgate[:, :]),
                                op=ALU.mult).then_inc(weight_ready.sem, 1)
                v.wait_ge(weight_ready.sem, weight_ready.at(g, 1))

            def start_sum(g):
                v.wait_ge(stored.sem, stored.at(g, 0))
                for h in range(2):
                    v.wait_ge(bias_ready.sem, bias_ready.at(g, h + 1))
                    v.tensor_tensor(out=acc[:, 2 * h:2 * h + 2, :], in0=tiles(MB[h]), in1=n5.x[:, 2 * h:2 * h + 2, :],
                                    op=ALU.add).then_inc(acc_start.sem, 1)
                v.wait_ge(acc_start.sem, acc_start.at(g, 2))

            def combine(g, s0, s1):
                for s2 in range(s0 // 2, s1 // 2):
                    pair, t0 = s2 // 2, s2 % 2 * 2
                    for e in range(2):
                        for t in (t0, t0 + 1):
                            s = pair * NT + t
                            done = 4 * s2 + 2 * e + (t - t0)
                            if e == 0:
                                v.wait_ge(expert_ready.sem, expert_ready.at(g, s + 1))
                            if e:
                                v.wait_ge(expert_added.sem, expert_added.at(g, done - 1))
                            elif pair:
                                v.wait_ge(expert_added.sem, expert_added.at(g, done - 5))
                            x = 2 * pair + e
                            v.scalar_tensor_tensor(out=acc[:, t, :], in0=MB[s % 2][:, e * D:(e + 1) * D],
                                                   scalar=weight[:, t, x:x + 1], in1=acc[:, t, :], op0=ALU.mult,
                                                   op1=ALU.add).then_inc(expert_added.sem, 1)

            def ln6_stats(g):
                n = n6
                n.chain.start(v, g)
                v.wait_ge(expert_added.sem, expert_added.at(g, 2 * MOE))
                for t in range(NT):
                    n.chain.then(v.bn_stats(n.stats[:, t, :], acc[:, t, :]))
                n.chain.settle()
                v.sem_inc(held.sem, 1)
                for t in range(NT):
                    last = v.bn_aggr(n.mv[:, t, :], n.stats[:, t, :])
                last.then_inc(n.var_ready.sem, 1)
                n.chain.end()

            def ln6_apply(g):
                n = n6
                v.wait_ge(n.rstd_ready.sem, n.rstd_ready.at(g, 1))
                for t in range(NT):
                    v.tensor_scalar(n.x[:, t, :], acc[:, t, :], n.mv[:, t, 0:1], n.rstd[:, t:t + 1],
                                    ALU.subtract, ALU.mult).then_inc(n.x_ready.sem, 1)

            def turn_(f, m, b):
                share = len(PLAN) // 4
                if b is not None:
                    gated(b)
                if m is not None:
                    convolve(m)
                if b is not None:
                    ln5_sum(b)
                if f is not None:
                    ln1_sum(f)
                if b is not None:
                    norm_apply(v, n5, b)
                if f is not None:
                    values(f)
                    norm_apply(v, n1, f)
                if b is not None:
                    route(b)
                states(m, 4)
                if b is not None:
                    pick_expert(b)
                states(m, 6)
                if b is not None:
                    start_sum(b)
                states(m, 8)
                for k in range(4):
                    if f is not None:
                        maxima(f, 2 * k, 2 * k + 2)
                    if b is not None and k % 2:
                        combine(b, 2 * (k // 2), 2 * (k // 2) + 2)
                if f is not None:
                    negate_maxima(f)
                states(m, 12)
                if f is not None:
                    copy_maxima(f)
                for k in range(6):
                    if f is not None and k == 3:
                        att_chain.start(v, f)
                        normalize_context(f, 0)
                    states(m, 12 + 12 * (k + 1))
                if f is not None:
                    normalize_context(f, 1)
                    att_chain.end()
                states(m, 88)
                if f is not None:
                    ln2_sum(f)
                if b is not None:
                    combine(b, 4, 6)
                states(m, 92)
                if f is not None:
                    norm_apply(v, n2, f)
                if b is not None:
                    combine(b, 6, 8)
                states(m, 96)
                if f is not None:
                    sequence_sums(f)
                if b is not None:
                    combine(b, 8, 10)
                states(m, 100)
                if f is not None:
                    global_base(f)
                for s in range(CYC):
                    if f is not None:
                        rotate(f, s)
                    if b is not None and s % 2 == 0:
                        combine(b, 10 + s, 12 + s)
                    states(m, (103, 108, 112, 118, 122, 125)[s])
                states(m, len(PLAN))
                if f is not None:
                    ln3_sum(f)
                if m is not None:
                    ln4_sum(m)
                if f is not None:
                    norm_apply(v, n3, f)
                if m is not None:
                    norm_apply(v, n4, m)
                if b is not None:
                    ln6_stats(b)
                    ln6_apply(b)

            scanned.n = None
            setup()
            expert_added.start_ahead(v)
            z_ready.start_ahead(v)
            turn_(0, None, None)
            turn_(1, 0, None)
            with v.Fori(0, G - 2) as i:
                turn_((i, 2), (i, 1), (i, 0))
            turn_(None, G - 1, G - 2)
            turn_(None, None, G - 1)

        @block.scalar
        def _(a):
            def nat():
                a.preload_act_table_set("natural_log_exp_and_others")

            def setup():
                nat()
                a.wait_ge(loaded_w.sem, 16 * (len(W) + 1))
                at, n = COLUMNS["A_log"]
                a.activation(decay[:, :], W["columns"][:, at:at + n], ACT.Exp).then_inc(const_a.sem, 1)
                a.wait_ge(const_v.sem, const_v.per)
                a.wait_ge(const_v2.sem, 5)
                for r in range(DC):
                    a.wait_ge(const_t.sem, DC)
                    a.activation(rf_out[:, r, :], bank[r][:, 0:D], ACT.Exp, bias=rf_bias[:, r:r + 1])\
                        .then_inc(const_a.sem, 1)
                a.activation(g1[:, :], eps[:, :].to_broadcast([P, NB]), ACT.Copy).then_inc(const_a.sem, 1)

            def feat(g):
                for r in range(DC):
                    a.wait_ge(dots_ready.sem, dots_ready.at(g, r + 1))
                    a.activation(feats[:, r, :], bank[r][:, :], ACT.Exp, bias=rf_bias[:, r:r + 1])\
                        .then_inc(feats_ready.sem, 1)

            def keys(g):
                a.wait_ge(kT_psum.sem, kT_psum.at(g, 1))
                for e in range(DC):
                    a.activation(kT[:, e, :], bank[0][:, e * 240:(e + 1) * 240], ACT.Identity, bias=col("bk", e))\
                        .then_inc(kT_ready.sem, 1)

            def queries(g):
                for e in range(DC):
                    a.wait_ge(q_psum.sem, q_psum.at(g, e + 1))
                    a.activation(qT[:, e, :], bank[2 + e][:, :], ACT.Identity, bias=col("bq", e))\
                        .then_inc(qT_ready.sem, 1)

            def softmax(g, s0, s1):
                for s in range(s0, s1):
                    a.wait_ge(logits_ready.sem, logits_ready.at(g, s + 1))
                    if s >= 4:
                        a.wait_ge(pv_ready.sem, pv_ready.at(g, s - 3))
                    a.activation(probs[:, s % 4, :, :].rearrange("p k s -> p (k s)"), bank[s % 4][0:KEYS, :],
                                 ACT.Exp, scale=1.0 / np.sqrt(DK)).then_inc(probs_ready.sem, 1)

            def copy_context(g):
                for c in range(DC):
                    a.wait_ge(ctxn_turned.sem, ctxn_turned.at(g, c + 1))
                    a.copy(ctxnT[:, c, :], bank[c][:, :]).then_inc(ctxnT_ready.sem, 1)

            def global_network(g):
                z = bank[0]
                a.wait_ge(glob_psum.sem, glob_psum.at(g, 1))
                a.activation(g1[:, :], z[:, 0:NB], ACT.Gelu, bias=col("gc_b1"), scale=1.0 / S)\
                    .then_inc(glob_ready.sem, 1)
                a.wait_ge(glob_psum.sem, glob_psum.at(g, 2))
                a.activation(g2[:, :], z[0:64, NB:2 * NB], ACT.Gelu, bias=col("gc_b2", 0, 64))\
                    .then_inc(glob_ready.sem, 1)
                a.wait_ge(glob_psum.sem, glob_psum.at(g, 3))
                a.activation(gt[:, :], z[:, 2 * NB:3 * NB], ACT.Tanh, bias=half_gb3[:, :], scale=0.5)\
                    .then_inc(glob_ready.sem, 1)

            def network(g, n, s):
                b = s % NB
                if n == 1:
                    a.wait_ge(l1_psum.sem, l1_psum.at(g, s + 1))
                    for r in range(2):
                        a.activation(h1[:, b, r, :], bank[b][:, r * S:(r + 1) * S], ACT.Gelu,
                                     bias=col("cn_b1", r)).then_inc(l1_ready.sem, 1)
                elif n == 2:
                    a.wait_ge(l2_psum.sem, l2_psum.at(g, s + 1))
                    a.activation(h2[:, b, :], bank[2 + b][:, 0:S], ACT.Gelu, bias=col("cn_b2"))\
                        .then_inc(l2_ready.sem, 1)
                elif n == 3:
                    a.wait_ge(l3_psum.sem, l3_psum.at(g, s + 1))
                    a.activation(h3[:, b, :], bank[2 + b][0:64, S:2 * S], ACT.Gelu, bias=col("cn_b3", 0, 64))\
                        .then_inc(l3_ready.sem, 1)
                else:
                    a.wait_ge(l4_psum.sem, l4_psum.at(g, s + 1))
                    if s >= NB:
                        a.wait_ge(z_ready.sem, z_ready.at(g, 2 * (s - NB) + 2))
                    a.activation(gate[:, b, :], bank[4 + b][:, 0:S], ACT.Tanh, bias=half_b4[:, :], scale=0.5)\
                        .then_inc(gate_ready.sem, 1)

            def mamba_in(g):
                for j in range(2 * IC):
                    if j == IC:
                        a.preload_act_table_set("silu_and_others")
                    a.wait_ge(in_psum.sem, in_psum.at(g, j + 1))
                    src = MB[j % 2][:, :]
                    if j < IC:
                        a.copy(xpad[:, j, :, PAD:PAD + S], src.rearrange("p (b s) -> p b s", b=NB))\
                            .then_inc(in_read.sem, 1)
                    else:
                        a.activation(res[:, j - IC, :], src, ACT.Silu).then_inc(in_read.sem, 1)
                for c in range(IC):
                    a.wait_ge(conv_ready.sem, conv_ready.at(g, c + 1))
                    a.activation(xc[:, c, :], conv[:, c, :], ACT.Silu, bias=col("conv_b", c)).then_inc(xc_ready.sem, 1)

            def softplus(g):
                a.wait_ge(xc_ready.sem, xc_ready.at(g, IC))
                a.activation(soft[:, :, :], xc[:, :, :], ACT.Exp, scale=-1.0).then_inc(exp_ready.sem, 1)
                a.wait_ge(exp_ready.sem, exp_ready.at(g, 1))
                a.activation(soft[:, :, :], soft[:, :, :], ACT.Ln, bias=1.0).then_inc(soft_ready.sem, 1)

            decays_done = [0]

            def decays(g, upto):
                if g is None:
                    return
                for k in range(decays_done[0], upto):
                    c = k // STATES
                    if k % STATES == 0:
                        a.wait_ge(delta_ready.sem, delta_ready.at(g, c + 1))
                    if k >= RING:
                        a.wait_ge(scanned.sem, scanned.at(g, AFTER["scan", (k - RING) // STATES,
                                                                   (k - RING) % STATES]))
                    a.activation(a_ring[:, k % RING, :, 1:S],
                                 delta[:, c, :].rearrange("p (b s) -> p b s", b=NB)[:, :, 1:S],
                                 ACT.Exp, scale=decay[:, k:k + 1]).then_inc(decay_ready.sem, 1)
                    if k % STATES == 0:
                        a.activation(xc2[:, c % 2, :], xc[:, c, :], ACT.Square).then_inc(xc2_ready.sem, 1)
                decays_done[0] = upto % STEPS

            def gated(g):
                a.preload_act_table_set("gelu_apprx_tanh_and_others")
                a.wait_ge(u_psum.sem, u_psum.at(g, 1))
                a.activation(ug[:, :], MB[0][0:KEYS, :], ACT.Gelu_apprx_tanh).then_inc(ug_ready.sem, 1)

            def route(g):
                a.wait_ge(logit_ready.sem, logit_ready.at(g, 1))
                a.activation(prob[:, :, :], logit[:, :, :], ACT.Exp).then_inc(prob_ready.sem, 1)

            def copy_weights(g):
                a.wait_ge(weight_turned.sem, weight_turned.at(g, 1))
                a.copy(weightT[:, :], MB[1][0:EXPERTS, :]).then_inc(weightT_ready.sem, 1)

            def gelu():
                a.preload_act_table_set("gelu_and_others")

            def turn_(f, m, b):
                if b is not None:
                    gated(b)
                if m is not None:
                    mamba_in(m)
                nat()
                if f is not None:
                    feat(f)
                if b is not None:
                    norm_rstd(a, n5, b)
                if m is not None:
                    softplus(m)
                if f is not None:
                    keys(f)
                    norm_rstd(a, n1, f)
                if b is not None:
                    norm_copy(a, n5, b, MB)
                if f is not None:
                    norm_copy(a, n1, f, TURN)
                    queries(f)
                decays(m, 4)
                if b is not None:
                    route(b)
                decays(m, 6)
                if b is not None:
                    copy_weights(b)
                decays(m, 8)
                for k in range(8):
                    decays(m, 8 + 9 * (k + 1) // 2)
                    if f is not None:
                        softmax(f, 2 * k, 2 * k + 2)
                decays(m, 48)
                if f is not None:
                    copy_context(f)
                    norm_rstd(a, n2, f)
                if f is not None:
                    norm_copy(a, n2, f, TURN)
                decays(m, 56)
                if f is not None:
                    gelu()
                    global_network(f)
                    for s in range(CYC):
                        network(f, 1, s)
                        if s:
                            network(f, 4, s - 1)
                        network(f, 2, s)
                        network(f, 3, s)
                        if s == 3 and m is not None:
                            nat()
                            decays(m, STEPS)
                            gelu()
                    network(f, 4, CYC - 1)
                    nat()
                elif m is not None:
                    decays(m, STEPS)
                if f is not None:
                    norm_rstd(a, n3, f)
                if m is not None:
                    norm_rstd(a, n4, m)
                if f is not None:
                    norm_copy(a, n3, f, TURN)
                if m is not None:
                    norm_copy(a, n4, m, [bank[0], bank[1]])
                if b is not None:
                    norm_rstd(a, n6, b)

            setup()
            turn_(0, None, None)
            turn_(1, 0, None)
            with a.Fori(0, G - 2) as i:
                turn_((i, 2), (i, 1), (i, 0))
            turn_(None, G - 1, G - 2)
            turn_(None, None, G - 1)

        @block.gpsimd
        def _(p):
            def setup():
                p.wait_ge(loaded_w.sem, 16 * (len(W) + 1))
                for c in range(DC):
                    p.tensor_tensor(out=rf_sq[:, c, :], in0=rfwT[:, c, :], in1=rfwT[:, c, :], op=ALU.mult)\
                        .then_inc(const_p.sem, 1)
                p.wait_ge(const_p.sem, 2)
                p.tensor_tensor(out=rf_sqsum[:, :], in0=rf_sq[:, 0, :], in1=rf_sq[:, 1, :], op=ALU.add)\
                    .then_inc(const_p.sem, 1)
                p.wait_ge(const_p.sem, 3)
                p.wait_ge(const_t.sem, DC)

            def norms(g):
                p.wait_ge(loaded_x.sem, loaded_x.at(g, 48))
                p.wait_ge(dots_ready.sem, dots_ready.at(g, 0))
                p.wait_ge(z_ready.sem, z_ready.at(g, 0))
                sq_chain.start(p, g)
                for c in range(DC):
                    sq_chain.then(p.tensor_tensor(out=sq[:, c, :], in0=x0T[:, c, :], in1=x0T[:, c, :], op=ALU.mult))
                sq_chain.settle()
                sq_chain.end()
                p.tensor_tensor(out=sqsum[:, :], in0=sq[:, 0, :], in1=sq[:, 1, :], op=ALU.add)\
                    .then_inc(sqsum_ready.sem, 1)

            def mask_keys(g):
                at, n = COLUMNS["head_mask"]
                mask = W["columns"][:, at:at + n].unsqueeze(2).to_broadcast([P, HC, KEYS])
                p.wait_ge(kT_ready.sem, kT_ready.at(g, DC))
                for b in range(NB):
                    for e in range(DC):
                        k = kT[:, e, b * KEYS:(b + 1) * KEYS].unsqueeze(1).to_broadcast([P, HC, KEYS])
                        p.tensor_tensor(out=kmask[:, b, e, :, :], in0=k, in1=mask, op=ALU.mult)\
                            .then_inc(kmask_ready.sem, 1)

            def add_bias(g):
                p.wait_ge(n1.turned.sem, n1.turned.at(g, DC))
                p.tensor_tensor(out=x1b[:, :, :], in0=n1.x[:, :, :], in1=row("bo").unsqueeze(1).to_broadcast([P, NT, D]),
                                op=ALU.add).then_inc(x1b_ready.sem, 1)

            def deltas(g):
                p.wait_ge(soft_ready.sem, soft_ready.at(g, 1))
                for c in range(IC):
                    p.tensor_tensor(out=delta[:, c, :], in0=xc[:, c, :], in1=soft[:, c, :], op=ALU.add)\
                        .then_inc(delta_ready.sem, 1)

            def turn_(f, m):
                if f is not None:
                    norms(f)
                if m is not None:
                    deltas(m)
                if f is not None:
                    mask_keys(f)
                    add_bias(f)

            setup()
            turn_(0, None)
            turn_(1, 0)
            with p.Fori(0, G - 2) as i:
                turn_((i, 2), (i, 1))
            turn_(None, G - 1)


def host_arrays(x, ctx_1024, **w):
    x, c = np.asarray(x), np.asarray(ctx_1024)
    w = {k: np.asarray(a) for k, a in w.items()}

    def rows_to_chunks(a):
        k = a.shape[0] // P
        return a.reshape(k, P, -1).transpose(1, 0, 2).reshape(P, -1)

    def as_columns(a, n):
        return a.reshape(n, -1).T if a.size > n else np.broadcast_to(a.reshape(1, n), (P, n))

    def padded(a):
        return np.concatenate([a.reshape(-1, 1), np.zeros((P - a.size, 1), a.dtype)])

    cols = {
        "xis": as_columns(w["L0_attn_xis"], DC), "bq": as_columns(w["L0_xattn_bq"], DC),
        "bk": as_columns(w["L0_xattn_bk"], DC), "cn_b1": as_columns(w["L0_ffn_cn_b1"], 2),
        "cn_b2": as_columns(w["L0_ffn_cn_b2"], 1), "cn_b3": padded(w["L0_ffn_cn_b3"]),
        "cn_b4": as_columns(w["L0_ffn_cn_b4"], 1), "gc_b1": as_columns(w["L0_ffn_gc_b1"], 1),
        "gc_b2": padded(w["L0_ffn_gc_b2"]), "gc_b3": as_columns(w["L0_ffn_gc_b3"], 1),
        "range": as_columns(w["L0_ffn_adaptive_range"], 1),
        "sign": np.where(np.arange(P) < P // 2, 1.0, -1.0).astype(np.float32).reshape(P, 1),
        "conv_w": w["L1_attn_conv_w"].reshape(IC, P, TAPS).transpose(1, 0, 2).reshape(P, -1),
        "conv_b": as_columns(w["L1_attn_conv_b"], IC), "D": as_columns(w["L1_attn_D"], IC),
        "A_log": w["L1_attn_A_log"].reshape(IC, P, STATES).transpose(1, 0, 2).reshape(P, -1),
        "head_mask": (np.arange(P)[:, None] // DK == np.arange(HC)[None, :]).astype(np.float32),
    }
    rows = {"xis": w["L0_attn_xis"], "bv": w["L0_xattn_bv"], "bo": w["L0_xattn_bo"], "router_b": w["L1_ffn_router_b"],
            "rank": np.arange(EXPERTS, 0, -1).astype(np.float32)}
    head_rows = np.tile(np.repeat(np.eye(HEADS, dtype=mybir.dt.np(BF16)), KEYS, axis=1), (2, 1)).reshape(2 * HEADS, HEADS, KEYS)
    arrays = {
        "projT": rows_to_chunks(w["L0_attn_proj_matrix"].T), "rfwT": rows_to_chunks(w["L0_attn_input_weights"].T),
        "wq": rows_to_chunks(w["L0_xattn_Wq"]), "wk": rows_to_chunks(w["L0_xattn_Wk"]),
        "wv": rows_to_chunks(w["L0_xattn_Wv"]), "wo": rows_to_chunks(w["L0_xattn_Wo"]),
        "cn_w1": rows_to_chunks(w["L0_ffn_cn_w1"]), "cn_w2": rows_to_chunks(w["L0_ffn_cn_w2"]),
        "cn_w3": w["L0_ffn_cn_w3"], "cn_w4": np.broadcast_to(w["L0_ffn_cn_w4"], (64, P)),
        "gc_w1": rows_to_chunks(w["L0_ffn_gc_w1"]), "gc_w2": w["L0_ffn_gc_w2"],
        "gc_w3": np.broadcast_to(w["L0_ffn_gc_w3"], (64, P)),
        "winT": rows_to_chunks(w["L1_attn_W_in"].T), "woutT": rows_to_chunks(w["L1_attn_W_out"].T),
        "router_w": rows_to_chunks(w["L1_ffn_router_w"]),
        "expert_w": rows_to_chunks(w["L1_ffn_expert_w"].transpose(1, 0, 2).reshape(D, EXPERTS * D)),
        "expert_b": w["L1_ffn_expert_b"],
        "columns": np.concatenate([cols[n] for n in COLUMNS], axis=1),
        "rows": np.broadcast_to(np.concatenate([rows[n] for n in ROWS])[None, :], (P, N_ROWS)),
        "ident": np.eye(P, dtype=np.float32), "head_rows": head_rows,
        "x": x.reshape(G, NT, P, D).transpose(0, 2, 1, 3),
        "xT": x.reshape(G, T, DC, P).transpose(0, 3, 2, 1),
        "ctxT": c.reshape(G, NB * KEYS, DC, P).transpose(0, 3, 2, 1),
        "ctx": c.reshape(G, NB, KEYS, D).transpose(0, 2, 1, 3),
    }
    return {n: np.ascontiguousarray(a) for n, a in arrays.items()}


def kernel(**inputs):
    import concourse.bacc as bacc
    from concourse.bass_utils import run_bass_kernel_spmd

    arrays = host_arrays(**inputs)
    nc = bacc.Bacc("TRN2", target_bir_lowering=False, num_devices=1)
    aps = {n: nc.dram_tensor("in_" + n, a.shape, mybir.dt.from_np(a.dtype), kind="ExternalInput").ap() for n, a in arrays.items()}
    out = nc.dram_tensor("out", (G, P, NT, D), F32, kind="ExternalOutput").ap()
    program(nc, aps, out)
    r = run_bass_kernel_spmd(nc, [{"in_" + n: a for n, a in arrays.items()}], core_ids=[0])
    y = r.results[0]["out"]
    return np.asarray(y).reshape(G, P, NT, D).transpose(0, 2, 1, 3).reshape(B, S, D)
```

```python
from contextlib import ExitStack

import numpy as np

import concourse.bass as bass
from concourse import mybir

F32 = mybir.dt.float32
BF16 = mybir.dt.bfloat16
ALU = mybir.AluOpType
ACT = mybir.ActivationFunctionType
AX = mybir.AxisListType.X

P = 128
B, S, D = 32, 256, 256
KEYS = 120
HEADS, DK = 16, 16
NB = 2
G = B // NB
T = NB * S
NT = T // P
DC = D // P
HC = HEADS // DC
DV = DK + 1
INNER, STATES, TAPS = 512, 16, 4
IC = INNER // P
PAD = TAPS - 1
EXPERTS = 8
RFS = 256
EPS = 1e-5
RING = 8


def scan_plan():
    plan = []
    for c in range(IC + 1):
        scans = [("scan", c, n) for n in (0, 4, 2, 1)] if c < IC else [None] * 4
        gates = [("add", c - 1, STATES - 2), ("merge", c - 1, 0), ("mul", c - 1, 0), ("out", c - 1, 0)] if c else [None] * 4
        for steps in zip(scans, gates):
            plan += [step for step in steps if step]
        if c < IC:
            plan.append(("scan", c, 3))
            for n in range(5, STATES, 2):
                plan += [("add", c, n - 3), ("scan", c, n)]
                if n + 1 < STATES:
                    plan.append(("scan", c, n + 1))
    return plan


PLAN = scan_plan()
AFTER = {step: k + 1 for k, step in enumerate(PLAN)}



def decays_of(steps):
    return max(c * STATES + n + 1 for what, c, n in PLAN[:steps] if what == "scan")


COLUMNS = {}
for _name, _n in [("xis", DC), ("bq", DC), ("bk", DC), ("cn_b1", 2), ("cn_b2", 1), ("cn_b3", 1), ("cn_b4", 1),
                  ("gc_b1", 1), ("gc_b2", 1), ("gc_b3", 1), ("range", 1), ("sign", 1), ("conv_w", IC * TAPS),
                  ("conv_b", IC), ("D", IC), ("A_log", IC * STATES), ("head_mask", HC)]:
    COLUMNS[_name] = (sum(n for _, n in COLUMNS.values()), _n)
N_COLUMNS = sum(n for _, n in COLUMNS.values())
ROWS = {}
for _name, _n in [("xis", RFS), ("bv", D), ("bo", D), ("router_b", EXPERTS), ("rank", EXPERTS)]:
    ROWS[_name] = (sum(n for _, n in ROWS.values()), _n)
N_ROWS = sum(n for _, n in ROWS.values())

WEIGHTS = {
    "projT": (P, DC * RFS), "rfwT": (P, DC * D),
    "wq": (P, DC * D), "wk": (P, DC * D), "wv": (P, DC * D), "wo": (P, DC * D),
    "cn_w1": (P, DC * 256), "cn_w2": (P, DC * 128), "cn_w3": (P, 64), "cn_w4": (64, P),
    "gc_w1": (P, DC * 128), "gc_w2": (P, 64), "gc_w3": (64, P),
    "winT": (P, DC * 2 * INNER), "woutT": (P, IC * D),
    "router_w": (P, DC * EXPERTS), "expert_w": (P, DC * EXPERTS * D), "expert_b": (EXPERTS, D),
    "columns": (P, N_COLUMNS), "rows": (P, N_ROWS), "ident": (P, P),
}


class Signal:

    def __init__(self, sem, per, head=0):
        self.sem, self.per, self.head = sem, per, head

    def at(self, g, n):
        i, ahead = g if isinstance(g, tuple) else (0, g)
        return i * self.per + (ahead * self.per + n + self.head)

    def start_ahead(self, eng):
        eng.sem_inc(self.sem, self.head)


class Chain(Signal):

    def start(self, eng, g):
        self.eng, self.g, self.n = eng, g, 0

    def then(self, ins):
        self.n += 1
        return ins.then_inc(self.sem, 1)

    def settle(self, behind=0):
        self.eng.wait_ge(self.sem, self.at(self.g, self.n - behind))

    def link(self, ins):
        self.then(ins)
        self.settle()

    def end(self):
        assert self.n == self.per, (self.n, self.per)


def program(nc, ins, out):
    nc.disable_value_cache = True
    with ExitStack() as ctx:
        def sb(name, shape, dt=F32):
            return ctx.enter_context(nc.sbuf_tensor(name, shape, dt))

        def sem(name, per=1, head=0):
            return Signal(ctx.enter_context(nc.semaphore(name)), per, head)

        def chain(name, per):
            return Chain(ctx.enter_context(nc.semaphore(name)), per)

        bank = [ctx.enter_context(nc.psum_tensor(f"bank{i}", [P, 512], F32)) for i in range(8)]

        W = {name: sb("w_" + name, list(shape)) for name, shape in WEIGHTS.items()}

        def col(name, k=0, rows=P):
            at = COLUMNS[name][0] + k
            return W["columns"][0:rows, at:at + 1]

        def row(name):
            at, n = ROWS[name]
            return W["rows"][:, at:at + n]

        def chunks(name, k):
            return W[name][:, :].rearrange("p (k n) -> p k n", k=k)

        projT, rfwT = chunks("projT", DC), chunks("rfwT", DC)
        wq, wk, wv, wo = (chunks(n, DC) for n in ("wq", "wk", "wv", "wo"))
        cn_w1, cn_w2, gc_w1 = (chunks(n, DC) for n in ("cn_w1", "cn_w2", "gc_w1"))
        winT, woutT = chunks("winT", DC), chunks("woutT", IC)
        router_w, expert_w = chunks("router_w", DC), chunks("expert_w", DC)
        ident = W["ident"]

        rf_scaled = projT
        rf_norm = sb("rf_norm", [P, RFS])
        rf_bias = sb("rf_bias", [P, DC])
        rf_out = rfwT
        decay = sb("decay", [P, IC * STATES])
        half_b4 = sb("half_b4", [P, 1])
        half_gb3 = sb("half_gb3", [P, 1])
        gate_scale = sb("gate_scale", [P, 1])
        glob_scale = sb("glob_scale", [P, 1])
        base_sign = sb("base_sign", [P, 1])
        eps = sb("eps", [P, 1])
        head_rows = sb("head_rows16", [2 * HEADS, HEADS, KEYS], BF16)
        ident16 = sb("ident16", [P, P], BF16)

        x0 = sb("x0", [P, NT, D])
        x0T = sb("x0T", [P, DC, T])
        ctxT = sb("ctxT", [P, DC, NB * KEYS])
        sqsum = sb("sqsum", [P, T])
        feats = sb("feats", [P, DC, T])
        sq = feats
        rf_sq, rf_sqsum = feats[:, :, 0:D], sqsum[:, 0:D]
        kT = sb("kT", [P, DC, NB * KEYS])
        kmask = sb("kmask", [P, NB, DC, HC, KEYS])
        vals = sb("vals", [KEYS, NB, HEADS, DV])
        qT = sb("qT", [P, DC, T])
        smax = sb("smax", [P, NT, HEADS])
        smax_hi = sb("smax_hi", [P, NT, 2, HEADS], BF16)
        smax_rest = sb("smax_rest", [P, NT, HEADS])
        smaxT = sb("smaxT", [2 * HEADS, T], BF16)
        probs = sb("probs", [KEYS, 4, 2, S])
        wsum = sb("wsum", [P, NT, HEADS])
        ctxn = feats[:, :, :].rearrange("p c (t h d) -> p (c t) h d", t=2, h=HEADS)
        ctxnT = qT
        zsum = sb("zsum", [P, DC, NB])
        g1 = sb("g1", [P, NB])
        g2 = sb("g2", [64, NB])
        gt = sb("gt", [P, NB])
        base = sb("base", [P, NB])
        spare = kmask[:, :, :, :, :].rearrange("p b c h k -> p (b c h k)")

        def in_spare(k, n, rows=P):
            return spare[0:rows, k * NB * S:(k + n) * NB * S]

        h1 = in_spare(0, 2).rearrange("p (b r s) -> p b r s", b=NB, r=2)
        h2 = in_spare(2, 1).rearrange("p (b s) -> p b s", b=NB)
        h3 = in_spare(3, 1, 64).rearrange("p (b s) -> p b s", b=NB)
        gate = in_spare(4, 1).rearrange("p (b s) -> p b s", b=NB)
        couple = in_spare(5, 1).rearrange("p (b s) -> p b s", b=NB)
        turn = qT[:, :, :].rearrange("p c (b s) -> p c b s", b=NB)

        xpad = sb("xpad", [P, IC, NB, PAD + S])
        xc = sb("xc", [P, IC, T])
        res = sb("res", [P, IC, T])
        soft = sb("soft", [P, IC, T])
        conv = delta = soft
        xc2 = sb("xc2", [P, 2, T])
        a_ring = sb("a_ring", [P, RING, NB, S])
        even, odd = sb("even", [P, 2, T]), sb("odd", [P, 2, T])
        ysum = sb("ysum", [P, 2, T])
        odd_sum = sb("odd_sum", [P, T])
        yT = xpad[:, :, :, PAD:PAD + S]

        ctxTb = sb("ctxTb", [P, DC, NB * KEYS])
        ctxb = sb("ctxb", [KEYS, NB, D])
        ug = sb("ug", [KEYS, T])
        uu = ug
        logit = sb("logit", [P, NT, EXPERTS])
        lmax = sb("lmax", [P, NT])
        prob = sb("prob", [P, NT, EXPERTS])
        pmax = sb("pmax", [P, NT])
        psm = sb("psm", [P, NT])
        pinv = sb("pinv", [P, NT])
        pgate = sb("pgate", [P, NT])
        pick = sb("pick", [P, NT, EXPERTS])
        prank = sb("prank", [P, NT, EXPERTS])
        rmax = sb("rmax", [P, NT])
        weight = sb("weight", [P, NT, EXPERTS])
        weightT = ug[0:EXPERTS, :]

        class Norm:
            def __init__(self, name, x, xT, sum_=None):
                self.stats = sb(f"{name}_stats", [P, NT, 6])
                self.mv = sb(f"{name}_mv", [P, NT, 2])
                self.logv = sb(f"{name}_logv", [P, NT])
                self.rstd = sb(f"{name}_rstd", [P, NT])
                self.x = x
                self.sum = x if sum_ is None else sum_
                self.xT = xT
                self.sub_ready = sem(f"{name}_sub_ready", 2)
                self.sum_ready = sem(f"{name}_sum_ready", 2)
                self.var_ready = sem(f"{name}_var_ready", 1)
                self.log_ready = sem(f"{name}_log_ready", 1)
                self.rstd_ready = sem(f"{name}_rstd_ready", 1)
                self.x_ready = sem(f"{name}_x_ready", NT)
                if xT is not None:
                    self.turned = sem(f"{name}_turned", DC)
                    self.xT_ready = sem(f"{name}_xT_ready", DC)
                self.chain = chain(f"{name}_chain", NT)

        sum3 = in_spare(0, 2).rearrange("p (t d) -> p t d", t=NT)
        x12, x3, x45, x6 = (sb(n, [P, NT, D]) for n in ("x12", "x3", "x45", "x6"))
        x12T, x3T, x45T = (sb(n, [P, DC, T]) for n in ("x12T", "x3T", "x45T"))
        n1, n2, n3 = Norm("ln1", x12, x12T), Norm("ln2", x12, x12T), Norm("ln3", x3, x3T, sum3)
        n4, n5, n6 = Norm("ln4", x45, x45T), Norm("ln5", x45, x45T), Norm("ln6", x6, None)
        x1b, acc = x12, x6

        loaded_w = sem("loaded_w")
        loaded_x = sem("loaded_x", 3 * 16)
        loaded_ctx = sem("loaded_ctx", 2 * 16)
        stored = sem("stored", 16, 1)
        const_v = chain("const_v", 10 + RING)
        const_v2 = sem("const_v2")
        const_a = sem("const_a")
        const_p = sem("const_p")
        const_t = sem("const_t")

        held = sem("held")
        sq_chain = chain("sq_chain", 2)
        sqsum_ready = sem("sqsum_ready", 1)
        dots_ready = sem("dots_ready", DC, 1)
        feats_ready = sem("feats_ready", DC)

        kT_psum = sem("kT_psum", 1)
        v_psum = sem("v_psum", 1)
        q_psum = sem("q_psum", DC)
        kT_ready = sem("kT_ready", DC)
        qT_ready = sem("qT_ready", DC)
        vals_ready = sem("vals_ready", NB)
        kmask_ready = sem("kmask_ready", NB * DC)
        scores_ready = sem("scores_ready", NT * DC)
        smax_ready = sem("smax_ready", NT * DC)
        hi_chain = chain("hi_chain", 2)
        hi_ready = sem("hi_ready", 1)
        smaxT_psum = sem("smaxT_psum", 1)
        smaxT_ready = sem("smaxT_ready", 1)
        logits_ready = sem("logits_ready", NB * HEADS // 2)
        probs_ready = sem("probs_ready", NB * HEADS // 2)
        pv_ready = sem("pv_ready", NB * HEADS // 2)
        att_chain = chain("att_chain", NT)
        ctxn_ready = sem("ctxn_ready", NT)
        ctxn_turned = sem("ctxn_turned", DC)
        ctxnT_ready = sem("ctxnT_ready", DC)
        x1b_ready = sem("x1b_ready", 1)

        zsum_ready = sem("zsum_ready", DC)
        glob_psum = sem("glob_psum", 3)
        glob_ready = sem("glob_ready", 3)
        base_ready = sem("base_ready", 1)
        CYC = 3 * NB
        l1_psum = sem("l1_psum", CYC)
        l1_ready = sem("l1_ready", 2 * CYC)
        l2_psum = sem("l2_psum", CYC)
        l2_ready = sem("l2_ready", CYC)
        l3_psum = sem("l3_psum", CYC)
        l3_ready = sem("l3_ready", CYC)
        l4_psum = sem("l4_psum", CYC)
        gate_ready = sem("gate_ready", CYC)
        cyc_chain = chain("cyc_chain", 3 * CYC)
        z_ready = sem("z_ready", 2 * CYC)

        in_psum = sem("in_psum", 2 * IC)
        in_read = sem("in_read", 2 * IC)
        conv_chain = chain("conv_chain", IC * (TAPS - 1))
        conv_ready = sem("conv_ready", IC)
        xc_ready = sem("xc_ready", IC)
        exp_ready = sem("exp_ready", 1)
        soft_ready = sem("soft_ready", 1)
        xc2_ready = sem("xc2_ready", IC)
        delta_ready = sem("delta_ready", IC)
        STEPS = IC * STATES
        decay_ready = sem("decay_ready", STEPS)
        scanned = chain("scanned", len(PLAN))
        ODD_ADDS = STATES // 2 - 1
        odd_added = sem("odd_added", IC * ODD_ADDS)

        u_psum = sem("u_psum", 1)
        ug_ready = sem("ug_ready", 1)
        uu_ready = sem("uu_ready", 1)
        router_psum = sem("router_psum", 1)
        logit_chain = chain("logit_chain", 2)
        logit_ready = sem("logit_ready", 1)
        prob_ready = sem("prob_ready", 1)
        pick_chain = chain("pick_chain", 8)
        weight_ready = sem("weight_ready", 1)
        weight_turned = sem("weight_turned", 1)
        weightT_ready = sem("weightT_ready", 1)
        bias_ready = sem("bias_ready", 2)
        MOE = NT * EXPERTS // 2
        expert_ready = sem("expert_ready", MOE)
        acc_start = sem("acc_start", 2)
        expert_added = sem("expert_added", 2 * MOE, 1)

        def norm_add(v, n, g, parts):
            for half, (sub, resid) in enumerate(parts):
                v.wait_ge(n.sub_ready.sem, n.sub_ready.at(g, half + 1))
                v.tensor_tensor(out=n.sum[:, 2 * half:2 * half + 2, :], in0=sub, in1=resid,
                                op=ALU.add).then_inc(n.sum_ready.sem, 1)

        def norm_stats(v, n, g):
            n.chain.start(v, g)
            for t in range(NT):
                v.wait_ge(n.sum_ready.sem, n.sum_ready.at(g, t // 2 + 1))
                n.chain.then(v.bn_stats(n.stats[:, t, :], n.sum[:, t, :]))
            n.chain.settle()
            v.sem_inc(held.sem, 1)
            for t in range(NT):
                last = v.bn_aggr(n.mv[:, t, :], n.stats[:, t, :])
            last.then_inc(n.var_ready.sem, 1)
            n.chain.end()

        def norm_rstd(a, n, g):
            a.wait_ge(n.var_ready.sem, n.var_ready.at(g, 1))
            a.activation(n.logv[:, :], n.mv[:, :, 1], ACT.Ln, bias=eps[:, :]).then_inc(n.log_ready.sem, 1)
            a.wait_ge(n.log_ready.sem, n.log_ready.at(g, 1))
            a.activation(n.rstd[:, :], n.logv[:, :], ACT.Exp, scale=-0.5).then_inc(n.rstd_ready.sem, 1)

        def norm_apply(v, n, g):
            v.wait_ge(n.rstd_ready.sem, n.rstd_ready.at(g, 1))
            for t in range(NT):
                v.tensor_scalar(n.x[:, t, :], n.sum[:, t, :], n.mv[:, t, 0:1], n.rstd[:, t:t + 1],
                                ALU.subtract, ALU.mult).then_inc(n.x_ready.sem, 1)

        def norm_turn(pe, n, g, banks):
            for c in range(DC):
                for t in range(NT):
                    pe.wait_ge(n.x_ready.sem, n.x_ready.at(g, t + 1))
                    last = pe.transpose(banks[c][:, t * P:(t + 1) * P], n.x[:, t, c * P:(c + 1) * P], ident[:, :])
                last.then_inc(n.turned.sem, 1)

        def norm_copy(a, n, g, banks):
            for c in range(DC):
                a.wait_ge(n.turned.sem, n.turned.at(g, c + 1))
                a.copy(n.xT[:, c, :], banks[c][:, :]).then_inc(n.xT_ready.sem, 1)

        def tiles(bank_, half=None):
            return bank_[:, :].rearrange("p (t d) -> p t d", t=2)

        OUT = [bank[2], bank[3]]
        TURN = [bank[4], bank[5]]
        MB = [bank[6], bank[7]]

        def added_after(s):
            return 4 * (s // 2) + 3 + s % 2

        block = ctx.enter_context(nc.Block())

        @block.sync
        def _(sp):
            for name in W:
                sp.dma_start(W[name][:, :], ins[name]).then_inc(loaded_w.sem, 16)
            sp.dma_start(head_rows[:, :, :], ins["head_rows"]).then_inc(loaded_w.sem, 16)

            def at(tensor, g):
                return tensor[g[0] + g[1]] if isinstance(g, tuple) else tensor[g]

            def load_front(g):
                sp.dma_start(x0T[:, :, :], at(ins["xT"], g)).then_inc(loaded_x.sem, 16)
                sp.dma_start(x0[:, :, :], at(ins["x"], g)).then_inc(loaded_x.sem, 16)
                sp.dma_start(ctxT[:, :, :], at(ins["ctxT"], g)).then_inc(loaded_x.sem, 16)

            def load_back(g):
                sp.dma_start(ctxTb[:, :, :], at(ins["ctxT"], g)).then_inc(loaded_ctx.sem, 16)
                sp.dma_start(ctxb[:, :, :], at(ins["ctx"], g)).then_inc(loaded_ctx.sem, 16)

            def front_free(g):
                sp.wait_ge(n1.sum_ready.sem, n1.sum_ready.at(g, 2))
                sp.sem_inc(held.sem, 1)
                sp.wait_ge(v_psum.sem, v_psum.at(g, 1))
                sp.sem_inc(held.sem, 1)
                sp.wait_ge(kT_psum.sem, kT_psum.at(g, 1))
                sp.sem_inc(held.sem, 1)

            def back_free(g):
                sp.wait_ge(n5.sub_ready.sem, n5.sub_ready.at(g, 2))
                sp.sem_inc(held.sem, 1)

            def store(g):
                sp.wait_ge(n6.x_ready.sem, n6.x_ready.at(g, NT))
                sp.sem_inc(held.sem, 1)
                sp.dma_start(at(out, g), n6.x[:, :, :]).then_inc(stored.sem, 16)

            stored.start_ahead(sp)
            load_front(0)
            load_back(0)
            for g in range(2):
                front_free(g)
                load_front(g + 1)
            with sp.Fori(0, G - 3) as i:
                front_free((i, 2))
                load_front((i, 3))
                back_free((i, 0))
                load_back((i, 1))
                store((i, 0))
            back_free(G - 3)
            load_back(G - 2)
            store(G - 3)
            back_free(G - 2)
            load_back(G - 1)
            store(G - 2)
            store(G - 1)
            sp.wait_ge(stored.sem, stored.at(G, 0))

        @block.tensor
        def _(pe):
            def mm(o, l, r, start, stop):
                return pe.matmul(o, l, r, start=start, stop=stop)

            def setup():
                pe.wait_ge(loaded_w.sem, 16 * (len(W) + 1))
                pe.wait_ge(const_v.sem, const_v.per)
                pe.wait_ge(const_p.sem, 3)
                for r in range(DC):
                    for c in range(DC):
                        mm(bank[r][:, 0:D], rf_scaled[:, c, r * P:(r + 1) * P], rfwT[:, c, :], c == 0, False)
                    mm(bank[r][:, 0:D], rf_norm[:, r * P:(r + 1) * P], rf_sqsum[:, :], False, True)\
                        .then_inc(const_t.sem, 1)

            def rfs(g, r):
                if r == 0:
                    pe.wait_ge(loaded_x.sem, loaded_x.at(g, 48))
                    if g != 0:
                        pe.wait_ge(l1_ready.sem, l1_ready.at(g, 0))
                for c in range(DC):
                    mm(bank[r][:, :], rf_scaled[:, c, r * P:(r + 1) * P], x0T[:, c, :], c == 0, False)
                pe.wait_ge(sqsum_ready.sem, sqsum_ready.at(g, 1))
                mm(bank[r][:, :], rf_norm[:, r * P:(r + 1) * P], sqsum[:, :], False, True)\
                    .then_inc(dots_ready.sem, 1)

            def project(g, n, ready, lhsT, rhs, k, banks, wait_each=None):
                if wait_each is None:
                    pe.wait_ge(ready.sem, ready.at(g, ready.per))
                for t in range(NT):
                    for c in range(k):
                        last = mm(banks[t // 2][:, t % 2 * D:t % 2 * D + D], lhsT[:, c, t * P:(t + 1) * P],
                                  rhs[:, c, :], c == 0, c == k - 1)
                    if t % 2:
                        last.then_inc(n.sub_ready.sem, 1)

            def key_values(g):
                pe.wait_ge(feats_ready.sem, feats_ready.at(g, DC))
                for e in range(DC):
                    for c in range(DC):
                        last = mm(bank[0][:, e * 240:(e + 1) * 240], wk[:, c, e * P:(e + 1) * P], ctxT[:, c, :],
                                  c == 0, c == DC - 1)
                last.then_inc(kT_psum.sem, 1)
                for b in range(NB):
                    for c in range(DC):
                        last = mm(bank[1][0:KEYS, b * D:(b + 1) * D], ctxT[:, c, b * KEYS:(b + 1) * KEYS],
                                  wv[:, c, :], c == 0, c == DC - 1)
                last.then_inc(v_psum.sem, 1)

            def queries(g):
                pe.wait_ge(n1.xT_ready.sem, n1.xT_ready.at(g, DC))
                pe.wait_ge(n1.sum_ready.sem, n1.sum_ready.at(g, 2))
                for e in range(DC):
                    for c in range(DC):
                        last = mm(bank[2 + e][:, :], wq[:, c, e * P:(e + 1) * P], n1.xT[:, c, :], c == 0, c == DC - 1)
                    last.then_inc(q_psum.sem, 1)

            def scores(g, s0, s1):
                pe.wait_ge(vals_ready.sem, vals_ready.at(g, NB))
                for s in range(s0, s1):
                    t, e = divmod(s, DC)
                    pair = s % 2
                    pe.wait_ge(qT_ready.sem, qT_ready.at(g, DC))
                    pe.wait_ge(kmask_ready.sem, kmask_ready.at(g, (t // 2 + 1) * DC))
                    if s >= 2:
                        pe.wait_ge(smax_ready.sem, smax_ready.at(g, s - 1))
                    for half in range(2):
                        last = mm(bank[2 * pair + half][:, 0:480], qT[:, e, t * P:(t + 1) * P],
                                  kmask[:, t // 2, e, 4 * half:4 * half + 4, :], True, True)
                    last.then_inc(scores_ready.sem, 1)

            def turn_maxima(g):
                pe.wait_ge(hi_ready.sem, hi_ready.at(g, 1))
                pe.wait_ge(n1.xT_ready.sem, n1.xT_ready.at(g, DC))
                smaxT_bank = bank[4][0:2 * HEADS, 0:T // 2].bitcast(BF16)
                for t in range(NT):
                    last = pe.transpose(smaxT_bank[:, t * P:(t + 1) * P],
                                        smax_hi[:, t, :, :].rearrange("p a h -> p (a h)"), ident16[:, :])
                last.then_inc(smaxT_psum.sem, 1)

            def weigh(g, s):
                b, pair = divmod(s, HEADS // 2)
                if s == 0:
                    pe.wait_ge(smaxT_ready.sem, smaxT_ready.at(g, 1))
                if s >= 4:
                    pe.wait_ge(probs_ready.sem, probs_ready.at(g, s - 3))
                for k in range(2):
                    h = 2 * pair + k
                    dst = bank[s % 4][0:KEYS, k * S:(k + 1) * S]
                    mm(dst, kmask[:, b, h // HC, h % HC, :], qT[:, h // HC, b * S:(b + 1) * S], True, False)
                    last = mm(dst, head_rows[:, h, :], smaxT[:, b * S:(b + 1) * S], False, True)
                last.then_inc(logits_ready.sem, 1)

            def mix(g, s):
                b, pair = divmod(s, HEADS // 2)
                pe.wait_ge(probs_ready.sem, probs_ready.at(g, s + 1))
                if pair == 0 and b:
                    pe.wait_ge(ctxn_ready.sem, ctxn_ready.at(g, 2 * b))
                for q in range(2):
                    for k in range(2):
                        h = 2 * pair + k
                        last = mm(bank[4 + q][:, h * DV:(h + 1) * DV], probs[:, s % 4, k, q * P:(q + 1) * P],
                                  vals[:, b, h, :], True, True)
                last.then_inc(pv_ready.sem, 1)

            def attend(g, s0, s1):
                for s in range(s0, s1):
                    if s < NB * HEADS // 2:
                        weigh(g, s)
                    if s >= 2:
                        mix(g, s - 2)

            def turn_context(g):
                pe.wait_ge(probs_ready.sem, probs_ready.at(g, NB * HEADS // 2))
                for c in range(DC):
                    for t in range(NT):
                        pe.wait_ge(ctxn_ready.sem, ctxn_ready.at(g, t + 1))
                        last = pe.transpose(bank[c][:, t * P:(t + 1) * P],
                                            ctxn[:, t, c * HC:(c + 1) * HC, :].rearrange("p h d -> p (h d)"),
                                            ident[:, :])
                    last.then_inc(ctxn_turned.sem, 1)

            def glob(g, n):
                z = bank[5][:, S:2 * S]
                if n == 1:
                    pe.wait_ge(zsum_ready.sem, zsum_ready.at(g, DC))
                    for c in range(DC):
                        last = mm(z[:, 0:NB], gc_w1[:, c, :], zsum[:, c, :], c == 0, c == DC - 1)
                    last.then_inc(glob_psum.sem, 1)
                elif n == 2:
                    pe.wait_ge(glob_ready.sem, glob_ready.at(g, 1))
                    mm(z[0:64, NB:2 * NB], W["gc_w2"][:, :], g1[:, :], True, True).then_inc(glob_psum.sem, 1)
                else:
                    pe.wait_ge(glob_ready.sem, glob_ready.at(g, 2))
                    mm(z[:, 2 * NB:3 * NB], W["gc_w3"][:, :], g2[:, :], True, True).then_inc(glob_psum.sem, 1)

            def layer(g, n, s):
                b = s % NB
                if n == 1:
                    if s >= NB:
                        pe.wait_ge(z_ready.sem, z_ready.at(g, 2 * (s - NB) + 2))
                    elif s == 0:
                        pe.wait_ge(n2.xT_ready.sem, n2.xT_ready.at(g, DC))
                    for r in range(2):
                        for c in range(DC):
                            last = mm(bank[b][:, r * S:(r + 1) * S], cn_w1[:, c, r * P:(r + 1) * P],
                                      n2.xT[:, c, b * S:(b + 1) * S], c == 0, c == DC - 1)
                    last.then_inc(l1_psum.sem, 1)
                elif n == 2:
                    pe.wait_ge(l1_ready.sem, l1_ready.at(g, 2 * s + 2))
                    if s < NB:
                        pe.wait_ge(n2.sum_ready.sem, n2.sum_ready.at(g, 2))
                    for c in range(2):
                        last = mm(bank[2 + b][:, 0:S], cn_w2[:, c, :], h1[:, b, c, :], c == 0, c == 1)
                    last.then_inc(l2_psum.sem, 1)
                elif n == 3:
                    pe.wait_ge(l2_ready.sem, l2_ready.at(g, s + 1))
                    mm(bank[2 + b][0:64, S:2 * S], W["cn_w3"][:, :], h2[:, b, :], True, True)\
                        .then_inc(l3_psum.sem, 1)
                else:
                    pe.wait_ge(l3_ready.sem, l3_ready.at(g, s + 1))
                    mm(bank[4 + b][:, 0:S], W["cn_w4"][:, :], h3[:, b, :], True, True).then_inc(l4_psum.sem, 1)

            def rotate_back(g, b):
                for t in (2 * b, 2 * b + 1):
                    pe.wait_ge(z_ready.sem, z_ready.at(g, 2 * (CYC - NB) + 2 * (t // 2) + 2))
                    for c in range(DC):
                        last = pe.transpose(OUT[t // 2][:, t % 2 * D + c * P:t % 2 * D + (c + 1) * P],
                                            n2.xT[:, c, t * P:(t + 1) * P], ident[:, :])
                    if t % 2:
                        last.then_inc(n3.sub_ready.sem, 1)

            def mamba_in(g, b, j0, j1):
                if j0 == 0:
                    pe.wait_ge(n3.xT_ready.sem, n3.xT_ready.at(g, DC))
                for j in range(j0, j1):
                    if j == 1 and b is not None:
                        pe.wait_ge(uu_ready.sem, uu_ready.at(b, 1))
                    if j >= 2:
                        pe.wait_ge(in_read.sem, in_read.at(g, j - 1))
                    for c in range(DC):
                        last = mm(MB[(j + 1) % 2][:, :], winT[:, c, j * P:(j + 1) * P], n3.xT[:, c, :], c == 0, c == DC - 1)
                    last.then_inc(in_psum.sem, 1)

            def mamba_out(g, b, k0, k1):
                for k in range(k0, k1):
                    t, c = divmod(k, IC)
                    if k == 0 and b is not None:
                        pe.wait_ge(expert_added.sem, expert_added.at(b, 2 * MOE))
                    if t == 0:
                        pe.wait_ge(scanned.sem, scanned.at(g, AFTER["out", c, 0]))
                    last = mm(MB[t // 2][:, t % 2 * D:t % 2 * D + D], yT[:, c, t // 2, t % 2 * P:t % 2 * P + P],
                              woutT[:, c, :], c == 0, c == IC - 1)
                    if t % 2 and c == IC - 1:
                        last.then_inc(n4.sub_ready.sem, 1)

            def gated_in(g):
                pe.wait_ge(n4.xT_ready.sem, n4.xT_ready.at(g, DC))
                pe.wait_ge(loaded_ctx.sem, loaded_ctx.at(g, 32))
                for b in range(NB):
                    for c in range(DC):
                        last = mm(MB[0][0:KEYS, b * S:(b + 1) * S], ctxTb[:, c, b * KEYS:(b + 1) * KEYS],
                                  n4.xT[:, c, b * S:(b + 1) * S], c == 0, c == DC - 1)
                last.then_inc(u_psum.sem, 1)

            def gated_out(g, m):
                if m is not None:
                    pe.wait_ge(in_read.sem, in_read.at(m, 2 * IC))
                pe.wait_ge(uu_ready.sem, uu_ready.at(g, 1))
                for t in range(NT):
                    last = mm(MB[t // 2][:, t % 2 * D:t % 2 * D + D], uu[:, t * P:(t + 1) * P],
                              ctxb[:, t // 2, :], True, True)
                    if t % 2:
                        last.then_inc(n5.sub_ready.sem, 1)

            def router(g):
                pe.wait_ge(n5.xT_ready.sem, n5.xT_ready.at(g, DC))
                for t in range(NT):
                    for c in range(DC):
                        last = mm(MB[0][:, t * EXPERTS:(t + 1) * EXPERTS], n5.xT[:, c, t * P:(t + 1) * P],
                                  router_w[:, c, :], c == 0, c == DC - 1)
                last.then_inc(router_psum.sem, 1)

            def turn_weights(g):
                pe.wait_ge(weight_ready.sem, weight_ready.at(g, 1))
                for t in range(NT):
                    last = pe.transpose(MB[1][0:EXPERTS, t * P:(t + 1) * P], weight[:, t, :], ident[:, :])
                last.then_inc(weight_turned.sem, 1)

            def expert_bias(g):
                pe.wait_ge(weightT_ready.sem, weightT_ready.at(g, 1))
                for t in range(NT):
                    last = mm(MB[t // 2][:, t % 2 * D:t % 2 * D + D], weightT[:, t * P:(t + 1) * P],
                              W["expert_b"][:, :], True, True)
                    if t % 2:
                        last.then_inc(bias_ready.sem, 1)

            def experts(g, s0, s1):
                for s in range(s0, s1):
                    pair, t = s // NT, s % NT
                    if s >= 2:
                        pe.wait_ge(expert_added.sem, expert_added.at(g, added_after(s - 2)))
                    else:
                        pe.wait_ge(acc_start.sem, acc_start.at(g, 2))
                    for c in range(DC):
                        last = mm(MB[s % 2][:, :], n5.xT[:, c, t * P:(t + 1) * P],
                                  expert_w[:, c, pair * 2 * D:(pair + 1) * 2 * D], c == 0, c == DC - 1)
                    last.then_inc(expert_ready.sem, 1)

            def turn(f, m, b):
                if f is not None:
                    rfs(f, 0)
                if m is not None:
                    rotate_back(m, 1)
                if f is not None:
                    rfs(f, 1)
                if b is not None:
                    norm_turn(pe, n4, b, MB)
                if f is not None:
                    if m is not None:
                        pe.wait_ge(n3.sum_ready.sem, n3.sum_ready.at(m, 2))
                    project(f, n1, feats_ready, feats, rf_out, DC, OUT)
                if b is not None:
                    gated_in(b)
                if m is not None:
                    norm_turn(pe, n3, m, TURN)
                if f is not None:
                    key_values(f)
                if m is not None:
                    mamba_in(m, b, 0, IC)
                if f is not None:
                    norm_turn(pe, n1, f, TURN)
                if m is not None:
                    mamba_in(m, b, IC, 2 * IC)
                if f is not None:
                    queries(f)
                if b is not None:
                    gated_out(b, m)
                if f is not None:
                    scores(f, 0, 2)
                if b is not None:
                    norm_turn(pe, n5, b, MB)
                if f is not None:
                    scores(f, 2, 3)
                if b is not None:
                    router(b)
                if f is not None:
                    scores(f, 3, 4)
                if b is not None:
                    turn_weights(b)
                if f is not None:
                    scores(f, 4, 5)
                if b is not None:
                    expert_bias(b)
                if f is not None:
                    scores(f, 5, 8)
                if b is not None:
                    experts(b, 0, 1)
                if f is not None:
                    turn_maxima(f)
                if b is not None:
                    experts(b, 1, 2)
                for k in range(NB * HEADS // 2 + 2):
                    if f is not None:
                        attend(f, k, k + 1)
                    if b is not None and k % 2 and k < 17:
                        experts(b, 2 + k // 2, 3 + k // 2)
                if b is not None:
                    experts(b, 10, 11)
                if f is not None:
                    turn_context(f)
                if b is not None:
                    experts(b, 11, 12)
                if f is not None:
                    project(f, n2, ctxnT_ready, ctxnT, wo, DC, OUT)
                if b is not None:
                    experts(b, 12, 14)
                if f is not None:
                    norm_turn(pe, n2, f, TURN)
                if b is not None:
                    experts(b, 14, 16)
                if f is not None:
                    layer(f, 1, 0)
                    glob(f, 1)
                    layer(f, 1, 1)
                    glob(f, 2)
                for s in range(CYC):
                    if f is not None:
                        if s >= NB:
                            layer(f, 1, s)
                        if s == 0:
                            glob(f, 3)
                        else:
                            layer(f, 4, s - 1)
                    out = 4 * (s - 1) if m is not None and 1 <= s < 5 else None
                    if out is not None:
                        mamba_out(m, b, out, out + 2)
                    if f is not None:
                        layer(f, 2, s)
                    if out is not None:
                        mamba_out(m, b, out + 2, out + 4)
                    if f is not None:
                        layer(f, 3, s)
                if f is not None:
                    layer(f, 4, CYC - 1)
                    rotate_back(f, 0)

            setup()
            dots_ready.start_ahead(pe)
            pe.wait_ge(const_a.sem, 4)
            turn(0, None, None)
            turn(1, 0, None)
            with pe.Fori(0, G - 2) as i:
                turn((i, 2), (i, 1), (i, 0))
            turn(None, G - 1, G - 2)
            turn(None, None, G - 1)

        @block.vector
        def _(v):
            def setup():
                const_v.start(v, 0)
                for k in range(RING):
                    const_v.then(v.memset(a_ring[:, k, :, 0:1], 0.0))
                const_v.then(v.memset(xpad[:, :, :, 0:PAD], 0.0))
                const_v.then(v.memset(vals[:, :, :, DK:DV], 1.0))
                const_v.then(v.memset(eps[:, :], EPS))
                v.wait_ge(loaded_w.sem, 16 * (len(W) + 1))
                for c in range(DC):
                    const_v.then(v.tensor_tensor(out=rf_scaled[:, c, :], in0=rf_scaled[:, c, :], in1=row("xis"),
                                                 op=ALU.mult))
                const_v.link(v.tensor_tensor(out=rf_norm[:, :], in0=row("xis"), in1=row("xis"), op=ALU.mult))
                const_v.then(v.tensor_scalar(rf_norm[:, :], rf_norm[:, :], -0.5, None, ALU.mult))
                at = COLUMNS["xis"][0]
                const_v.then(v.tensor_scalar(rf_bias[:, :], W["columns"][:, at:at + DC], -0.5 * float(np.log(RFS)),
                                             None, ALU.add))
                const_v.then(v.tensor_copy(ident16[:, :], ident[:, :]))
                const_v.then(v.tensor_scalar(half_b4[:, :], col("cn_b4"), 0.5, None, ALU.mult))
                const_v.end()
                v.tensor_scalar(half_gb3[:, :], col("gc_b3"), 0.5, None, ALU.mult).then_inc(const_v2.sem, 1)
                v.tensor_scalar(gate_scale[:, :], col("range"), 0.3, col("sign"), ALU.mult, ALU.mult)\
                    .then_inc(const_v2.sem, 1)
                v.tensor_scalar(glob_scale[:, :], col("range"), 0.7, col("sign"), ALU.mult, ALU.mult)\
                    .then_inc(const_v2.sem, 1)
                v.tensor_scalar(base_sign[:, :], col("sign"), 0.1, None, ALU.mult).then_inc(const_v2.sem, 1)
                v.wait_ge(const_a.sem, 1)
                v.tensor_scalar(decay[:, :], decay[:, :], -1.0, None, ALU.mult).then_inc(const_v2.sem, 1)
                v.wait_ge(const_v2.sem, 5)

            def ln1_sum(g):
                v.wait_ge(loaded_x.sem, loaded_x.at(g, 48))
                norm_add(v, n1, g, [(tiles(OUT[h]), x0[:, 2 * h:2 * h + 2, :]) for h in range(2)])
                norm_stats(v, n1, g)

            def values(g):
                v.wait_ge(v_psum.sem, v_psum.at(g, 1))
                for b in range(NB):
                    v.tensor_tensor(out=vals[:, b, :, 0:DK],
                                    in0=bank[1][0:KEYS, b * D:(b + 1) * D].rearrange("p (h d) -> p h d", h=HEADS),
                                    in1=row("bv")[0:KEYS, :].rearrange("p (h d) -> p h d", h=HEADS),
                                    op=ALU.add).then_inc(vals_ready.sem, 1)

            def maxima(g, s0, s1):
                for s in range(s0, s1):
                    t, e = divmod(s, DC)
                    v.wait_ge(scores_ready.sem, scores_ready.at(g, s + 1))
                    for half in range(2):
                        h0 = e * HC + 4 * half
                        last = v.tensor_reduce(smax[:, t, h0:h0 + 4],
                                               bank[2 * (s % 2) + half][:, 0:480].rearrange("p (h k) -> p h k", h=4),
                                               AX, ALU.max)
                    last.then_inc(smax_ready.sem, 1)

            def negate_maxima(g):
                v.wait_ge(smax_ready.sem, smax_ready.at(g, NT * DC))
                hi_chain.start(v, g)
                hi_chain.link(v.tensor_scalar(smax_hi[:, :, 0, :], smax[:, :, :], -1.0, None, ALU.mult))
                hi_chain.link(v.scalar_tensor_tensor(out=smax_rest[:, :, :], in0=smax[:, :, :], scalar=-1.0,
                                                     in1=smax_hi[:, :, 0, :], op0=ALU.mult, op1=ALU.subtract))
                hi_chain.end()
                v.tensor_copy(smax_hi[:, :, 1, :], smax_rest[:, :, :]).then_inc(hi_ready.sem, 1)

            def copy_maxima(g):
                v.wait_ge(smaxT_psum.sem, smaxT_psum.at(g, 1))
                v.tensor_copy(smaxT[:, :], bank[4][0:2 * HEADS, 0:T // 2].bitcast(BF16)).then_inc(smaxT_ready.sem, 1)

            def normalize_context(g, b):
                v.wait_ge(pv_ready.sem, pv_ready.at(g, (b + 1) * HEADS // 2))
                for q in range(2):
                    t = 2 * b + q
                    o = bank[4 + q][:, 0:HEADS * DV].rearrange("p (h d) -> p h d", h=HEADS)
                    att_chain.then(v.reciprocal(wsum[:, t, :], o[:, :, DK]))
                for q in range(2):
                    t = 2 * b + q
                    o = bank[4 + q][:, 0:HEADS * DV].rearrange("p (h d) -> p h d", h=HEADS)
                    v.wait_ge(att_chain.sem, att_chain.at(g, t + 1))
                    v.tensor_tensor(out=ctxn[:, t, :, :], in0=o[:, :, 0:DK],
                                    in1=wsum[:, t, :].unsqueeze(2).to_broadcast([P, HEADS, DK]),
                                    op=ALU.mult).then_inc(ctxn_ready.sem, 1)

            def ln2_sum(g):
                v.wait_ge(x1b_ready.sem, x1b_ready.at(g, 1))
                norm_add(v, n2, g, [(tiles(OUT[h]), x1b[:, 2 * h:2 * h + 2, :]) for h in range(2)])
                norm_stats(v, n2, g)

            def sequence_sums(g):
                for c in range(DC):
                    v.wait_ge(n2.xT_ready.sem, n2.xT_ready.at(g, c + 1))
                    v.tensor_reduce(zsum[:, c, :], n2.xT[:, c, :].rearrange("p (b s) -> p b s", b=NB), AX, ALU.add)\
                        .then_inc(zsum_ready.sem, 1)

            def global_base(g):
                v.wait_ge(glob_ready.sem, glob_ready.at(g, 3))
                v.tensor_scalar(base[:, :], gt[:, :], glob_scale[:, :], base_sign[:, :], ALU.mult, ALU.add)\
                    .then_inc(base_ready.sem, 1)
                cyc_chain.start(v, g)

            def rotate(g, s):
                b = s % NB
                z0 = n2.xT[:, 0, b * S:(b + 1) * S]
                z1 = n2.xT[:, 1, b * S:(b + 1) * S]
                if s == 0:
                    v.wait_ge(base_ready.sem, base_ready.at(g, 1))
                v.wait_ge(gate_ready.sem, gate_ready.at(g, s + 1))
                cyc_chain.link(v.tensor_scalar(couple[:, b, :], gate[:, b, :], gate_scale[:, :], base[:, b:b + 1],
                                               ALU.mult, ALU.add))
                cyc_chain.then(v.tensor_tensor(out=turn[:, 0, b, :], in0=couple[:, b, :], in1=z1, op=ALU.mult))
                cyc_chain.link(v.tensor_tensor(out=turn[:, 1, b, :], in0=couple[:, b, :], in1=z0, op=ALU.mult))
                v.tensor_tensor(out=z0, in0=z0, in1=turn[:, 0, b, :], op=ALU.add).then_inc(z_ready.sem, 1)
                v.tensor_tensor(out=z1, in0=z1, in1=turn[:, 1, b, :], op=ALU.subtract).then_inc(z_ready.sem, 1)
                if s == CYC - 1:
                    cyc_chain.end()

            def ln3_sum(g):
                norm_add(v, n3, g, [(tiles(OUT[h]), n2.x[:, 2 * h:2 * h + 2, :]) for h in range(2)])
                norm_stats(v, n3, g)

            def convolve(g):
                conv_chain.start(v, g)
                for c0 in range(0, IC, 2):
                    v.wait_ge(in_read.sem, in_read.at(g, c0 + 2))
                    for k in range(TAPS):
                        for c in range(c0, c0 + 2):
                            o = conv[:, c, :].rearrange("p (b s) -> p b s", b=NB)
                            x = xpad[:, c, :, k:k + S]
                            w = col("conv_w", c * TAPS + k)
                            if k:
                                conv_chain.settle(1)
                            if k == 0:
                                step = v.tensor_scalar(o, x, w, None, ALU.mult)
                            else:
                                step = v.scalar_tensor_tensor(out=o, in0=x, scalar=w, in1=o, op0=ALU.mult,
                                                              op1=ALU.add)
                            if k < TAPS - 1:
                                conv_chain.then(step)
                            else:
                                step.then_inc(conv_ready.sem, 1)
                                if c == c0:
                                    conv_chain.settle()
                conv_chain.end()

            def step(g, what, c, n):
                k = c * STATES + n
                total = ysum[:, c % 2, :]
                if scanned.n > 1:
                    scanned.settle(0 if scanned.n >= len(PLAN) - 3 else 1)
                if what == "scan":
                    if n == 0:
                        v.wait_ge(xc2_ready.sem, xc2_ready.at(g, c + 1))
                    if n == 0:
                        state = total
                    elif n == 1:
                        state = odd_sum[:, :]
                    else:
                        state = (odd if n % 2 else even)[:, n // 2 % 2, :]
                        if n % 2 and n >= 7:
                            v.wait_ge(odd_added.sem, odd_added.at(g, c * ODD_ADDS + (n - 5) // 2))
                    v.wait_ge(decay_ready.sem, decay_ready.at(g, k + 1))
                    scanned.then(v.tensor_tensor_scan(state,
                                                      a_ring[:, k % RING, :, :].rearrange("p b s -> p (b s)"),
                                                      xc2[:, c % 2, :], 0.0, ALU.mult, ALU.add))
                elif what == "add":
                    scanned.then(v.tensor_tensor(out=total, in0=total, in1=even[:, n // 2 % 2, :], op=ALU.add))
                elif what == "merge":
                    v.wait_ge(odd_added.sem, odd_added.at(g, (c + 1) * ODD_ADDS))
                    scanned.then(v.tensor_tensor(out=total, in0=total, in1=odd_sum[:, :], op=ALU.add))
                elif what == "mul":
                    scanned.then(v.tensor_tensor(out=total, in0=total, in1=res[:, c, :], op=ALU.mult))
                elif what == "out":
                    scanned.then(v.scalar_tensor_tensor(
                        out=yT[:, c, :, :], in0=total.rearrange("p (b s) -> p b s", b=NB), scalar=col("D", c),
                        in1=xc[:, c, :].rearrange("p (b s) -> p b s", b=NB), op0=ALU.add, op1=ALU.mult))

            def states(g, upto):
                if g is None:
                    return
                if scanned.n is None:
                    scanned.start(v, g)
                while scanned.n < upto:
                    step(g, *PLAN[scanned.n])
                if upto == len(PLAN):
                    scanned.end()
                    scanned.n = None

            def ln4_sum(g):
                norm_add(v, n4, g, [(tiles(MB[h]), n3.x[:, 2 * h:2 * h + 2, :]) for h in range(2)])
                norm_stats(v, n4, g)

            def gated(g):
                v.wait_ge(ug_ready.sem, ug_ready.at(g, 1))
                v.tensor_tensor(out=uu[:, :], in0=MB[0][0:KEYS, :], in1=ug[:, :], op=ALU.mult)\
                    .then_inc(uu_ready.sem, 1)

            def ln5_sum(g):
                norm_add(v, n5, g, [(tiles(MB[h]), n4.x[:, 2 * h:2 * h + 2, :]) for h in range(2)])
                norm_stats(v, n5, g)

            def over_experts(a):
                return a.unsqueeze(2).to_broadcast([P, NT, EXPERTS])

            def over_tiles(a):
                return a.unsqueeze(1).to_broadcast([P, NT, EXPERTS])

            def route(g):
                v.wait_ge(router_psum.sem, router_psum.at(g, 1))
                logit_chain.start(v, g)
                logit_chain.link(v.tensor_tensor(
                    out=logit[:, :, :], in0=MB[0][:, 0:NT * EXPERTS].rearrange("p (t e) -> p t e", t=NT),
                    in1=over_tiles(row("router_b")), op=ALU.add))
                logit_chain.link(v.tensor_reduce(lmax[:, :], logit[:, :, :], AX, ALU.max))
                logit_chain.end()
                v.tensor_tensor(out=logit[:, :, :], in0=logit[:, :, :], in1=over_experts(lmax[:, :]),
                                op=ALU.subtract).then_inc(logit_ready.sem, 1)

            def pick_expert(g):
                v.wait_ge(prob_ready.sem, prob_ready.at(g, 1))
                pick_chain.start(v, g)
                pick_chain.then(v.tensor_reduce(pmax[:, :], prob[:, :, :], AX, ALU.max))
                pick_chain.link(v.tensor_reduce(psm[:, :], prob[:, :, :], AX, ALU.add))
                pick_chain.then(v.reciprocal(pinv[:, :], psm[:, :]))
                pick_chain.link(v.tensor_tensor(out=pick[:, :, :], in0=prob[:, :, :], in1=over_experts(pmax[:, :]),
                                                op=ALU.is_equal))
                pick_chain.then(v.tensor_tensor(out=pgate[:, :], in0=pmax[:, :], in1=pinv[:, :], op=ALU.mult))
                pick_chain.link(v.tensor_tensor(out=prank[:, :, :], in0=pick[:, :, :], in1=over_tiles(row("rank")),
                                                op=ALU.mult))
                pick_chain.link(v.tensor_reduce(rmax[:, :], prank[:, :, :], AX, ALU.max))
                pick_chain.link(v.tensor_tensor(out=pick[:, :, :], in0=prank[:, :, :], in1=over_experts(rmax[:, :]),
                                                op=ALU.is_equal))
                pick_chain.end()
                v.tensor_tensor(out=weight[:, :, :], in0=pick[:, :, :], in1=over_experts(pgate[:, :]),
                                op=ALU.mult).then_inc(weight_ready.sem, 1)
                v.wait_ge(weight_ready.sem, weight_ready.at(g, 1))

            def start_sum(g):
                v.wait_ge(stored.sem, stored.at(g, 0))
                for h in range(2):
                    v.wait_ge(bias_ready.sem, bias_ready.at(g, h + 1))
                    v.tensor_tensor(out=acc[:, 2 * h:2 * h + 2, :], in0=tiles(MB[h]), in1=n5.x[:, 2 * h:2 * h + 2, :],
                                    op=ALU.add).then_inc(acc_start.sem, 1)
                v.wait_ge(acc_start.sem, acc_start.at(g, 2))

            def combine(g, s0, s1):
                for s2 in range(s0 // 2, s1 // 2):
                    pair, t0 = s2 // 2, s2 % 2 * 2
                    for e in range(2):
                        for t in (t0, t0 + 1):
                            s = pair * NT + t
                            done = 4 * s2 + 2 * e + (t - t0)
                            if e == 0:
                                v.wait_ge(expert_ready.sem, expert_ready.at(g, s + 1))
                            if e:
                                v.wait_ge(expert_added.sem, expert_added.at(g, done - 1))
                            elif pair:
                                v.wait_ge(expert_added.sem, expert_added.at(g, done - 5))
                            x = 2 * pair + e
                            v.scalar_tensor_tensor(out=acc[:, t, :], in0=MB[s % 2][:, e * D:(e + 1) * D],
                                                   scalar=weight[:, t, x:x + 1], in1=acc[:, t, :], op0=ALU.mult,
                                                   op1=ALU.add).then_inc(expert_added.sem, 1)

            def ln6_stats(g):
                n = n6
                n.chain.start(v, g)
                v.wait_ge(expert_added.sem, expert_added.at(g, 2 * MOE))
                for t in range(NT):
                    n.chain.then(v.bn_stats(n.stats[:, t, :], acc[:, t, :]))
                n.chain.settle()
                v.sem_inc(held.sem, 1)
                for t in range(NT):
                    last = v.bn_aggr(n.mv[:, t, :], n.stats[:, t, :])
                last.then_inc(n.var_ready.sem, 1)
                n.chain.end()

            def ln6_apply(g):
                n = n6
                v.wait_ge(n.rstd_ready.sem, n.rstd_ready.at(g, 1))
                for t in range(NT):
                    v.tensor_scalar(n.x[:, t, :], acc[:, t, :], n.mv[:, t, 0:1], n.rstd[:, t:t + 1],
                                    ALU.subtract, ALU.mult).then_inc(n.x_ready.sem, 1)

            def turn_(f, m, b):
                if f is not None:
                    ln1_sum(f)
                    norm_apply(v, n1, f)
                if b is not None:
                    gated(b)
                if f is not None:
                    values(f)
                if m is not None:
                    convolve(m)
                if b is not None:
                    ln5_sum(b)
                if f is not None:
                    maxima(f, 0, 2)
                if b is not None:
                    norm_apply(v, n5, b)
                states(m, 1)
                if f is not None:
                    maxima(f, 2, 3)
                if b is not None:
                    route(b)
                states(m, 3)
                if b is not None:
                    pick_expert(b)
                if f is not None:
                    maxima(f, 3, 4)
                states(m, 8)
                if f is not None:
                    maxima(f, 4, 5)
                states(m, 10)
                if b is not None:
                    start_sum(b)
                if f is not None:
                    maxima(f, 5, 6)
                states(m, 14)
                if f is not None:
                    maxima(f, 6, 8)
                    negate_maxima(f)
                states(m, 18)
                if f is not None:
                    copy_maxima(f)
                if b is not None:
                    combine(b, 0, 2)
                for k in range(16):
                    if f is not None and k == 9:
                        att_chain.start(v, f)
                        normalize_context(f, 0)
                    if b is not None and k % 4 == 3:
                        combine(b, 2 + k // 4 * 2, 4 + k // 4 * 2)
                    states(m, 18 + 7 * (k + 1) // 2)
                if f is not None:
                    normalize_context(f, 1)
                    att_chain.end()
                states(m, 76)
                if b is not None:
                    combine(b, 10, 12)
                states(m, 80)
                if f is not None:
                    ln2_sum(f)
                states(m, 81)
                if f is not None:
                    norm_apply(v, n2, f)
                if b is not None:
                    combine(b, 12, 14)
                states(m, 84)
                if f is not None:
                    sequence_sums(f)
                states(m, AFTER["scan", IC - 1, STATES - 1 - RING] + 4)
                if b is not None:
                    combine(b, 14, 16)
                states(m, len(PLAN))
                if f is not None:
                    global_base(f)
                for s in range(CYC):
                    if f is not None:
                        rotate(f, s)
                    if b is not None and s == 3:
                        ln6_stats(b)
                    if m is not None and s == CYC - 2:
                        ln4_sum(m)
                if m is not None:
                    norm_apply(v, n4, m)
                if f is not None:
                    ln3_sum(f)
                if f is not None:
                    norm_apply(v, n3, f)
                if b is not None:
                    ln6_apply(b)

            scanned.n = None
            setup()
            expert_added.start_ahead(v)
            turn_(0, None, None)
            turn_(1, 0, None)
            with v.Fori(0, G - 2) as i:
                turn_((i, 2), (i, 1), (i, 0))
            turn_(None, G - 1, G - 2)
            turn_(None, None, G - 1)

        @block.scalar
        def _(a):
            def nat():
                a.preload_act_table_set("natural_log_exp_and_others")

            def setup():
                nat()
                a.wait_ge(loaded_w.sem, 16 * (len(W) + 1))
                at, n = COLUMNS["A_log"]
                a.activation(decay[:, :], W["columns"][:, at:at + n], ACT.Exp).then_inc(const_a.sem, 1)
                a.wait_ge(const_v.sem, const_v.per)
                a.wait_ge(const_v2.sem, 5)
                for r in range(DC):
                    a.wait_ge(const_t.sem, DC)
                    a.activation(rf_out[:, r, :], bank[r][:, 0:D], ACT.Exp, bias=rf_bias[:, r:r + 1])\
                        .then_inc(const_a.sem, 1)
                a.activation(g1[:, :], eps[:, :].to_broadcast([P, NB]), ACT.Copy).then_inc(const_a.sem, 1)

            def feat(g, r):
                a.wait_ge(dots_ready.sem, dots_ready.at(g, r + 1))
                a.activation(feats[:, r, :], bank[r][:, :], ACT.Exp, bias=rf_bias[:, r:r + 1])\
                    .then_inc(feats_ready.sem, 1)

            def keys(g):
                a.wait_ge(kT_psum.sem, kT_psum.at(g, 1))
                for e in range(DC):
                    a.activation(kT[:, e, :], bank[0][:, e * 240:(e + 1) * 240], ACT.Identity, bias=col("bk", e))\
                        .then_inc(kT_ready.sem, 1)

            def queries(g):
                for e in range(DC):
                    a.wait_ge(q_psum.sem, q_psum.at(g, e + 1))
                    a.activation(qT[:, e, :], bank[2 + e][:, :], ACT.Identity, bias=col("bq", e))\
                        .then_inc(qT_ready.sem, 1)

            def softmax(g, s0, s1):
                for s in range(s0, s1):
                    a.wait_ge(logits_ready.sem, logits_ready.at(g, s + 1))
                    if s >= 4:
                        a.wait_ge(pv_ready.sem, pv_ready.at(g, s - 3))
                    a.activation(probs[:, s % 4, :, :].rearrange("p k s -> p (k s)"), bank[s % 4][0:KEYS, :],
                                 ACT.Exp, scale=1.0 / np.sqrt(DK)).then_inc(probs_ready.sem, 1)

            def copy_context(g):
                for c in range(DC):
                    a.wait_ge(ctxn_turned.sem, ctxn_turned.at(g, c + 1))
                    a.copy(ctxnT[:, c, :], bank[c][:, :]).then_inc(ctxnT_ready.sem, 1)

            def global_network(g, n):
                z = bank[5][:, S:2 * S]
                a.wait_ge(glob_psum.sem, glob_psum.at(g, n))
                if n == 1:
                    a.activation(g1[:, :], z[:, 0:NB], ACT.Gelu, bias=col("gc_b1"), scale=1.0 / S)\
                        .then_inc(glob_ready.sem, 1)
                elif n == 2:
                    a.activation(g2[:, :], z[0:64, NB:2 * NB], ACT.Gelu, bias=col("gc_b2", 0, 64))\
                        .then_inc(glob_ready.sem, 1)
                else:
                    a.activation(gt[:, :], z[:, 2 * NB:3 * NB], ACT.Tanh, bias=half_gb3[:, :], scale=0.5)\
                        .then_inc(glob_ready.sem, 1)

            def network(g, n, s):
                b = s % NB
                if n == 1:
                    a.wait_ge(l1_psum.sem, l1_psum.at(g, s + 1))
                    for r in range(2):
                        a.activation(h1[:, b, r, :], bank[b][:, r * S:(r + 1) * S], ACT.Gelu,
                                     bias=col("cn_b1", r)).then_inc(l1_ready.sem, 1)
                elif n == 2:
                    a.wait_ge(l2_psum.sem, l2_psum.at(g, s + 1))
                    a.activation(h2[:, b, :], bank[2 + b][:, 0:S], ACT.Gelu, bias=col("cn_b2"))\
                        .then_inc(l2_ready.sem, 1)
                elif n == 3:
                    a.wait_ge(l3_psum.sem, l3_psum.at(g, s + 1))
                    a.activation(h3[:, b, :], bank[2 + b][0:64, S:2 * S], ACT.Gelu, bias=col("cn_b3", 0, 64))\
                        .then_inc(l3_ready.sem, 1)
                else:
                    a.wait_ge(l4_psum.sem, l4_psum.at(g, s + 1))
                    if s >= NB:
                        a.wait_ge(z_ready.sem, z_ready.at(g, 2 * (s - NB) + 2))
                    a.activation(gate[:, b, :], bank[4 + b][:, 0:S], ACT.Tanh, bias=half_b4[:, :], scale=0.5)\
                        .then_inc(gate_ready.sem, 1)

            def mamba_in(g, j0, j1):
                for j in range(j0, j1):
                    if j == IC:
                        a.preload_act_table_set("silu_and_others")
                    a.wait_ge(in_psum.sem, in_psum.at(g, j + 1))
                    src = MB[(j + 1) % 2][:, :]
                    if j < IC:
                        a.copy(xpad[:, j, :, PAD:PAD + S], src.rearrange("p (b s) -> p b s", b=NB))\
                            .then_inc(in_read.sem, 1)
                    else:
                        a.activation(res[:, j - IC, :], src, ACT.Silu).then_inc(in_read.sem, 1)

            def silu_conv(g):
                for c in range(IC):
                    a.wait_ge(conv_ready.sem, conv_ready.at(g, c + 1))
                    a.activation(xc[:, c, :], conv[:, c, :], ACT.Silu, bias=col("conv_b", c)).then_inc(xc_ready.sem, 1)

            def softplus(g):
                a.wait_ge(xc_ready.sem, xc_ready.at(g, IC))
                a.activation(soft[:, :, :], xc[:, :, :], ACT.Exp, scale=-1.0).then_inc(exp_ready.sem, 1)
                a.wait_ge(exp_ready.sem, exp_ready.at(g, 1))
                a.activation(soft[:, :, :], soft[:, :, :], ACT.Ln, bias=1.0).then_inc(soft_ready.sem, 1)

            decays_done = [0]

            def decays(g, upto):
                if g is None:
                    return
                for k in range(decays_done[0], upto):
                    c = k // STATES
                    if k % STATES == 0:
                        a.wait_ge(delta_ready.sem, delta_ready.at(g, c + 1))
                    if k >= RING:
                        a.wait_ge(scanned.sem, scanned.at(g, AFTER["scan", (k - RING) // STATES,
                                                                   (k - RING) % STATES]))
                    a.activation(a_ring[:, k % RING, :, 1:S],
                                 delta[:, c, :].rearrange("p (b s) -> p b s", b=NB)[:, :, 1:S],
                                 ACT.Exp, scale=decay[:, k:k + 1]).then_inc(decay_ready.sem, 1)
                    if k % STATES == 0:
                        a.activation(xc2[:, c % 2, :], xc[:, c, :], ACT.Square).then_inc(xc2_ready.sem, 1)
                decays_done[0] = upto % STEPS

            def gated(g):
                a.preload_act_table_set("gelu_apprx_tanh_and_others")
                a.wait_ge(u_psum.sem, u_psum.at(g, 1))
                a.activation(ug[:, :], MB[0][0:KEYS, :], ACT.Gelu_apprx_tanh).then_inc(ug_ready.sem, 1)

            def route(g):
                a.wait_ge(logit_ready.sem, logit_ready.at(g, 1))
                a.activation(prob[:, :, :], logit[:, :, :], ACT.Exp).then_inc(prob_ready.sem, 1)

            def copy_weights(g):
                a.wait_ge(weight_turned.sem, weight_turned.at(g, 1))
                a.copy(weightT[:, :], MB[1][0:EXPERTS, :]).then_inc(weightT_ready.sem, 1)

            def gelu():
                a.preload_act_table_set("gelu_and_others")

            def turn_(f, m, b):
                if f is not None:
                    feat(f, 0)
                if m is not None:
                    norm_rstd(a, n3, m)
                if f is not None:
                    feat(f, 1)
                if b is not None:
                    norm_copy(a, n4, b, MB)
                if f is not None:
                    norm_rstd(a, n1, f)
                if b is not None:
                    gated(b)
                if m is not None:
                    norm_copy(a, n3, m, TURN)
                if f is not None:
                    keys(f)
                if m is not None:
                    mamba_in(m, 0, IC)
                if f is not None:
                    norm_copy(a, n1, f, TURN)
                if m is not None:
                    mamba_in(m, IC, 2 * IC)
                    silu_conv(m)
                nat()
                if f is not None:
                    queries(f)
                if m is not None:
                    softplus(m)
                if b is not None:
                    norm_rstd(a, n5, b)
                    norm_copy(a, n5, b, MB)
                decays(m, 6)
                if b is not None:
                    route(b)
                decays(m, 8)
                if b is not None:
                    copy_weights(b)
                for k in range(8):
                    decays(m, 17 + 13 * k // 3)
                    if f is not None:
                        softmax(f, 2 * k, 2 * k + 2)
                decays(m, decays_of(76) + 1)
                if f is not None:
                    copy_context(f)
                decays(m, decays_of(80) + 1)
                if f is not None:
                    norm_rstd(a, n2, f)
                decays(m, decays_of(86))
                if f is not None:
                    norm_copy(a, n2, f, TURN)
                decays(m, STEPS)
                if f is not None:
                    gelu()
                    network(f, 1, 0)
                    global_network(f, 1)
                    network(f, 1, 1)
                    global_network(f, 2)
                    for s in range(CYC):
                        if s >= NB:
                            network(f, 1, s)
                        if s == 0:
                            global_network(f, 3)
                        else:
                            network(f, 4, s - 1)
                        network(f, 2, s)
                        network(f, 3, s)
                    network(f, 4, CYC - 1)
                    nat()
                if m is not None:
                    norm_rstd(a, n4, m)
                if b is not None:
                    norm_rstd(a, n6, b)

            setup()
            turn_(0, None, None)
            turn_(1, 0, None)
            with a.Fori(0, G - 2) as i:
                turn_((i, 2), (i, 1), (i, 0))
            turn_(None, G - 1, G - 2)
            turn_(None, None, G - 1)

        @block.gpsimd
        def _(p):
            def setup():
                p.wait_ge(loaded_w.sem, 16 * (len(W) + 1))
                for c in range(DC):
                    p.tensor_tensor(out=rf_sq[:, c, :], in0=rfwT[:, c, :], in1=rfwT[:, c, :], op=ALU.mult)\
                        .then_inc(const_p.sem, 1)
                p.wait_ge(const_p.sem, 2)
                p.tensor_tensor(out=rf_sqsum[:, :], in0=rf_sq[:, 0, :], in1=rf_sq[:, 1, :], op=ALU.add)\
                    .then_inc(const_p.sem, 1)
                p.wait_ge(const_p.sem, 3)
                p.wait_ge(const_t.sem, DC)

            def norms(g):
                p.wait_ge(loaded_x.sem, loaded_x.at(g, 48))
                p.wait_ge(dots_ready.sem, dots_ready.at(g, 0))
                if g != 0:
                    p.wait_ge(ctxn_turned.sem, ctxn_turned.at(g, 0))
                sq_chain.start(p, g)
                for c in range(DC):
                    sq_chain.then(p.tensor_tensor(out=sq[:, c, :], in0=x0T[:, c, :], in1=x0T[:, c, :], op=ALU.mult))
                sq_chain.settle()
                sq_chain.end()
                p.tensor_tensor(out=sqsum[:, :], in0=sq[:, 0, :], in1=sq[:, 1, :], op=ALU.add)\
                    .then_inc(sqsum_ready.sem, 1)

            def mask_keys(g):
                at, n = COLUMNS["head_mask"]
                mask = W["columns"][:, at:at + n].unsqueeze(2).to_broadcast([P, HC, KEYS])
                p.wait_ge(kT_ready.sem, kT_ready.at(g, DC))
                for b in range(NB):
                    for e in range(DC):
                        k = kT[:, e, b * KEYS:(b + 1) * KEYS].unsqueeze(1).to_broadcast([P, HC, KEYS])
                        p.tensor_tensor(out=kmask[:, b, e, :, :], in0=k, in1=mask, op=ALU.mult)\
                            .then_inc(kmask_ready.sem, 1)

            def add_bias(g):
                p.wait_ge(n1.turned.sem, n1.turned.at(g, DC))
                p.tensor_tensor(out=x1b[:, :, :], in0=n1.x[:, :, :], in1=row("bo").unsqueeze(1).to_broadcast([P, NT, D]),
                                op=ALU.add).then_inc(x1b_ready.sem, 1)

            def deltas(g):
                p.wait_ge(soft_ready.sem, soft_ready.at(g, 1))
                for c in range(IC):
                    p.tensor_tensor(out=delta[:, c, :], in0=xc[:, c, :], in1=soft[:, c, :], op=ALU.add)\
                        .then_inc(delta_ready.sem, 1)

            def add_odd(g):
                for c in range(IC):
                    for n in range(3, STATES, 2):
                        k = c * ODD_ADDS + (n - 3) // 2
                        p.wait_ge(scanned.sem, scanned.at(g, AFTER["scan", c, n]))
                        if k:
                            p.wait_ge(odd_added.sem, odd_added.at(g, k))
                        p.tensor_tensor(out=odd_sum[:, :], in0=odd_sum[:, :], in1=odd[:, n // 2 % 2, :], op=ALU.add)\
                            .then_inc(odd_added.sem, 1)

            def turn_(f, m):
                if f is not None:
                    norms(f)
                    mask_keys(f)
                    add_bias(f)
                if m is not None:
                    deltas(m)
                    add_odd(m)

            setup()
            turn_(0, None)
            turn_(1, 0)
            with p.Fori(0, G - 2) as i:
                turn_((i, 2), (i, 1))
            turn_(None, G - 1)


def host_arrays(x, ctx_1024, **w):
    x, c = np.asarray(x), np.asarray(ctx_1024)
    w = {k: np.asarray(a) for k, a in w.items()}

    def rows_to_chunks(a):
        k = a.shape[0] // P
        return a.reshape(k, P, -1).transpose(1, 0, 2).reshape(P, -1)

    def as_columns(a, n):
        return a.reshape(n, -1).T if a.size > n else np.broadcast_to(a.reshape(1, n), (P, n))

    def padded(a):
        return np.concatenate([a.reshape(-1, 1), np.zeros((P - a.size, 1), a.dtype)])

    cols = {
        "xis": as_columns(w["L0_attn_xis"], DC), "bq": as_columns(w["L0_xattn_bq"], DC),
        "bk": as_columns(w["L0_xattn_bk"], DC), "cn_b1": as_columns(w["L0_ffn_cn_b1"], 2),
        "cn_b2": as_columns(w["L0_ffn_cn_b2"], 1), "cn_b3": padded(w["L0_ffn_cn_b3"]),
        "cn_b4": as_columns(w["L0_ffn_cn_b4"], 1), "gc_b1": as_columns(w["L0_ffn_gc_b1"], 1),
        "gc_b2": padded(w["L0_ffn_gc_b2"]), "gc_b3": as_columns(w["L0_ffn_gc_b3"], 1),
        "range": as_columns(w["L0_ffn_adaptive_range"], 1),
        "sign": np.where(np.arange(P) < P // 2, 1.0, -1.0).astype(np.float32).reshape(P, 1),
        "conv_w": w["L1_attn_conv_w"].reshape(IC, P, TAPS).transpose(1, 0, 2).reshape(P, -1),
        "conv_b": as_columns(w["L1_attn_conv_b"], IC), "D": as_columns(w["L1_attn_D"], IC),
        "A_log": w["L1_attn_A_log"].reshape(IC, P, STATES).transpose(1, 0, 2).reshape(P, -1),
        "head_mask": (np.arange(P)[:, None] // DK == np.arange(HC)[None, :]).astype(np.float32),
    }
    rows = {"xis": w["L0_attn_xis"], "bv": w["L0_xattn_bv"], "bo": w["L0_xattn_bo"], "router_b": w["L1_ffn_router_b"],
            "rank": np.arange(EXPERTS, 0, -1).astype(np.float32)}
    head_rows = np.tile(np.repeat(np.eye(HEADS, dtype=mybir.dt.np(BF16)), KEYS, axis=1), (2, 1)).reshape(2 * HEADS, HEADS, KEYS)
    arrays = {
        "projT": rows_to_chunks(w["L0_attn_proj_matrix"].T), "rfwT": rows_to_chunks(w["L0_attn_input_weights"].T),
        "wq": rows_to_chunks(w["L0_xattn_Wq"]), "wk": rows_to_chunks(w["L0_xattn_Wk"]),
        "wv": rows_to_chunks(w["L0_xattn_Wv"]), "wo": rows_to_chunks(w["L0_xattn_Wo"]),
        "cn_w1": rows_to_chunks(w["L0_ffn_cn_w1"]), "cn_w2": rows_to_chunks(w["L0_ffn_cn_w2"]),
        "cn_w3": w["L0_ffn_cn_w3"], "cn_w4": np.broadcast_to(w["L0_ffn_cn_w4"], (64, P)),
        "gc_w1": rows_to_chunks(w["L0_ffn_gc_w1"]), "gc_w2": w["L0_ffn_gc_w2"],
        "gc_w3": np.broadcast_to(w["L0_ffn_gc_w3"], (64, P)),
        "winT": rows_to_chunks(w["L1_attn_W_in"].T), "woutT": rows_to_chunks(w["L1_attn_W_out"].T),
        "router_w": rows_to_chunks(w["L1_ffn_router_w"]),
        "expert_w": rows_to_chunks(w["L1_ffn_expert_w"].transpose(1, 0, 2).reshape(D, EXPERTS * D)),
        "expert_b": w["L1_ffn_expert_b"],
        "columns": np.concatenate([cols[n] for n in COLUMNS], axis=1),
        "rows": np.broadcast_to(np.concatenate([rows[n] for n in ROWS])[None, :], (P, N_ROWS)),
        "ident": np.eye(P, dtype=np.float32), "head_rows": head_rows,
        "x": x.reshape(G, NT, P, D).transpose(0, 2, 1, 3),
        "xT": x.reshape(G, T, DC, P).transpose(0, 3, 2, 1),
        "ctxT": c.reshape(G, NB * KEYS, DC, P).transpose(0, 3, 2, 1),
        "ctx": c.reshape(G, NB, KEYS, D).transpose(0, 2, 1, 3),
    }
    return {n: np.ascontiguousarray(a) for n, a in arrays.items()}


def kernel(**inputs):
    import concourse.bacc as bacc
    from concourse.bass_utils import run_bass_kernel_spmd

    arrays = host_arrays(**inputs)
    nc = bacc.Bacc("TRN2", target_bir_lowering=False, num_devices=1)
    aps = {n: nc.dram_tensor("in_" + n, a.shape, mybir.dt.from_np(a.dtype), kind="ExternalInput").ap() for n, a in arrays.items()}
    out = nc.dram_tensor("out", (G, P, NT, D), F32, kind="ExternalOutput").ap()
    program(nc, aps, out)
    r = run_bass_kernel_spmd(nc, [{"in_" + n: a for n, a in arrays.items()}], core_ids=[0])
    y = r.results[0]["out"]
    return np.asarray(y).reshape(G, P, NT, D).transpose(0, 2, 1, 3).reshape(B, S, D)
```
